# Optimizing a Trainium2 kernel written in Bass

```python
import numpy as np
import jax
import jax.numpy as jnp

def _softmax(x, axis=-1):
    return jax.nn.softmax(x, axis=axis)

def _gelu(x):
    return jax.nn.gelu(x, approximate=True)

def _silu(x):
    return jax.nn.silu(x)

def _sigmoid(x):
    return jax.nn.sigmoid(x)

def _layernorm(x, axis=-1, eps=1e-05):
    m = jnp.mean(x, axis=axis, keepdims=True)
    v = jnp.var(x, axis=axis, keepdims=True)
    return (x - m) / jnp.sqrt(v + eps)

def _scatter_add(tgt, idx, src, axis=0):
    return tgt.at[idx].add(src)

def _segment_sum(src, seg, n):
    return jax.ops.segment_sum(src, seg, n)
kernel_name = 'mk_metaformer_d2_conv_nhwc512_r4_e36d92'

def setup_inputs(seed: int=0):
    np.random.seed(seed)
    _w = jnp.asarray

    def _rec_inputs():
        import jax
        import jax.numpy as jnp
        _gk = jax.random.key(seed)
        x = -0.000125 + 0.9999 * jax.random.normal(jax.random.fold_in(_gk, 1), (8, 32, 64, 128), jnp.float32)
        return x
    x = _rec_inputs()

    def _L0_conv_setup():
        import jax, jax.numpy as jnp
        import numpy as np
        B, CIN, COUT = (8, 32, 32)
        NLAT, NLON = (64, 128)
        M1, M2 = (32, 32)
        LMAX, MMAX = (NLAT, NLON // 2 + 1)
        SCALE = 1.0 / (CIN * COUT)
        TWO_PI = 2.0 * np.pi

        def _legendre(nlat, lmax, mmax):
            theta = np.pi * (np.arange(nlat) + 0.5) / nlat
            ct, st = (np.cos(theta), np.sin(theta))
            P = np.zeros((lmax, mmax, nlat), dtype=np.float64)
            P[0, 0] = 1.0 / np.sqrt(2.0)
            for m in range(min(lmax, mmax)):
                if m > 0:
                    P[m, m] = np.sqrt((2.0 * m + 1.0) / (2.0 * m)) * st * P[m - 1, m - 1]
                if m + 1 < lmax:
                    P[m + 1, m] = np.sqrt(2.0 * m + 3.0) * ct * P[m, m]
                for l in range(m + 2, lmax):
                    a = np.sqrt((4.0 * l * l - 1.0) / (l * l - m * m))
                    b = np.sqrt((2.0 * l + 1.0) * (l - 1 - m) * (l - 1 + m) / ((2.0 * l - 3.0) * (l * l - m * m)))
                    P[l, m] = a * ct * P[l - 1, m] - b * P[l - 2, m]
            w = st * np.pi / nlat
            return (P.astype(np.float32), w.astype(np.float32))
        _P, _W = _legendre(NLAT, LMAX, MMAX)
        P_ANA = jnp.asarray(_P * _W[None, None, :])
        P_SYN = jnp.asarray(_P)

        def _sht(x):
            xf = jnp.fft.rfft(x, axis=-1) * (np.sqrt(TWO_PI) / NLON)
            return jnp.einsum('lmj,bcjm->bclm', P_ANA, xf)

        def _isht(c):
            g = jnp.einsum('lmj,bclm->bcjm', P_SYN, c) * (1.0 / np.sqrt(TWO_PI))
            return jnp.fft.irfft(g, n=NLON, axis=-1) * NLON
        key = jax.random.key(seed)
        ks = jax.random.split(key, 5)
        x = jax.random.normal(ks[0], (B, CIN, NLAT, NLON), dtype=jnp.float32)
        shp = (CIN, COUT, M1, M2)
        w1r = SCALE * jax.random.uniform(ks[1], shp, dtype=jnp.float32)
        w1i = SCALE * jax.random.uniform(ks[2], shp, dtype=jnp.float32)
        w2r = SCALE * jax.random.uniform(ks[3], shp, dtype=jnp.float32)
        w2i = SCALE * jax.random.uniform(ks[4], shp, dtype=jnp.float32)
        return {'x': x, 'w1r': w1r, 'w1i': w1i, 'w2r': w2r, 'w2i': w2i}
    _L0_conv_all = _L0_conv_setup()
    _L0_conv_in = {k: v for k, v in _L0_conv_all.items() if k in ('w1r', 'w1i', 'w2r', 'w2i')}
    del _L0_conv_all

    def _L0_ffn_setup():
        import jax, jax.numpy as jnp
        import numpy as np
        MARK_AX = 0
        OPCODE_BASE = 16
        OP_SHL = OPCODE_BASE + 23
        OP_SHR = OPCODE_BASE + 24
        ALU_LO = 16
        ALU_HI = 20
        AX_CARRY_LO = 24
        OUTPUT_LO = 32
        OUTPUT_HI = 36
        B, SEQ, D = (8, 8192, 128)
        key = jax.random.key(seed)
        ks = jax.random.split(key, 6)
        x = jax.random.uniform(ks[0], (B, SEQ, D), dtype=jnp.float32) * 0.4
        mark = (jax.random.uniform(ks[1], (B, SEQ)) < 0.75).astype(jnp.float32)
        op_sel = jax.random.randint(ks[2], (B, SEQ), 0, 3)
        lo = jax.random.randint(ks[3], (B, SEQ), 0, 16)
        hi = jax.random.randint(ks[4], (B, SEQ), 0, 16)
        sa = jax.random.randint(ks[5], (B, SEQ), 0, 16)
        oh = lambda idx: jax.nn.one_hot(idx, 16, dtype=jnp.float32)
        x = x.at[..., MARK_AX].set(mark)
        x = x.at[..., OP_SHL].set((op_sel == 1).astype(jnp.float32))
        x = x.at[..., OP_SHR].set((op_sel == 2).astype(jnp.float32))
        x = x.at[..., ALU_LO:ALU_LO + 16].set(oh(lo))
        x = x.at[..., ALU_HI:ALU_HI + 16].set(oh(hi))
        x = x.at[..., AX_CARRY_LO:AX_CARRY_LO + 16].set(oh(sa))
        return {'x_bd': x}
    _L0_ffn_all = _L0_ffn_setup()
    _L0_ffn_in = {k: v for k, v in _L0_ffn_all.items() if k in ()}
    del _L0_ffn_all

    def _L1_conv_setup():
        import jax, jax.numpy as jnp
        import numpy as np
        TAU = 2.0
        BN_EPS = 1e-05
        ALPHA = 2.0
        NUM_HEADS = 8
        SCALE = 0.125

        def _h(v):
            return (v >= 0.0).astype(v.dtype)
        heaviside = jax.custom_vjp(_h)

        def _h_fwd(v):
            return (_h(v), v)

        def _h_bwd(v, g):
            sg = ALPHA / 2.0 / (1.0 + (jnp.pi / 2.0 * ALPHA * v) ** 2)
            return (g * sg,)
        heaviside.defvjp(_h_fwd, _h_bwd)

        def lif(x, v_th):

            def step(v, xt):
                v = v + (xt - v) / TAU
                s = heaviside(v - v_th)
                v = v * (1.0 - s)
                return (v, s)
            _, s = jax.lax.scan(step, jnp.zeros_like(x[0]), x)
            return s

        def bn(y, g, b, m, var):
            return (y - m) * (g * jax.lax.rsqrt(var + BN_EPS)) + b
        key = jax.random.key(seed)
        ks = jax.random.split(key, 3)
        T, B, N, C = (4, 32, 64, 128)
        x = jax.random.normal(ks[0], (T, B, N, C), dtype=jnp.float32)
        lin_w = jax.random.normal(ks[1], (4, C, C), dtype=jnp.float32) * 0.05
        lin_b = jnp.zeros((4, C), dtype=jnp.float32)
        bn_g = jnp.ones((4, C), dtype=jnp.float32)
        bn_b = jnp.zeros((4, C), dtype=jnp.float32)
        bn_m = jax.random.normal(ks[2], (4, C), dtype=jnp.float32) * 0.1
        bn_v = jnp.ones((4, C), dtype=jnp.float32)
        return {'x': x, 'lin_w': lin_w, 'lin_b': lin_b, 'bn_g': bn_g, 'bn_b': bn_b, 'bn_m': bn_m, 'bn_v': bn_v}
    _L1_conv_all = _L1_conv_setup()
    _L1_conv_in = {k: v for k, v in _L1_conv_all.items() if k in ('lin_w', 'lin_b', 'bn_g', 'bn_b', 'bn_m', 'bn_v')}
    del _L1_conv_all

    def _L1_ffn_setup():
        import jax, jax.numpy as jnp
        import numpy as np
        B, S, D, DFF, E, K = (4, 512, 128, 256, 8, 2)
        key = jax.random.key(seed)
        ks = jax.random.split(key, 5)
        x = jax.random.normal(ks[0], (B, S, D), dtype=jnp.float32)
        Wg = jax.random.normal(ks[1], (D, E), dtype=jnp.float32) * 0.02
        bg = jnp.zeros((E,), dtype=jnp.float32)
        W1 = jax.random.normal(ks[2], (E, D, 2 * DFF), dtype=jnp.float32) * 0.02
        b1 = jnp.zeros((E, 2 * DFF), dtype=jnp.float32)
        W2 = jax.random.normal(ks[3], (E, DFF, D), dtype=jnp.float32) * 0.02
        b2 = jnp.zeros((E, D), dtype=jnp.float32)
        return {'x': x, 'Wg': Wg, 'bg': bg, 'W1': W1, 'b1': b1, 'W2': W2, 'b2': b2}
    _L1_ffn_all = _L1_ffn_setup()
    _L1_ffn_in = {k: v for k, v in _L1_ffn_all.items() if k in ('Wg', 'bg', 'W1', 'b1', 'W2', 'b2')}
    del _L1_ffn_all
    return {'x': x, 'L0_conv_w1r': _L0_conv_in['w1r'], 'L0_conv_w1i': _L0_conv_in['w1i'], 'L0_conv_w2r': _L0_conv_in['w2r'], 'L0_conv_w2i': _L0_conv_in['w2i'], 'L1_conv_lin_w': _L1_conv_in['lin_w'], 'L1_conv_lin_b': _L1_conv_in['lin_b'], 'L1_conv_bn_g': _L1_conv_in['bn_g'], 'L1_conv_bn_b': _L1_conv_in['bn_b'], 'L1_conv_bn_m': _L1_conv_in['bn_m'], 'L1_conv_bn_v': _L1_conv_in['bn_v'], 'L1_ffn_Wg': _L1_ffn_in['Wg'], 'L1_ffn_bg': _L1_ffn_in['bg'], 'L1_ffn_W1': _L1_ffn_in['W1'], 'L1_ffn_b1': _L1_ffn_in['b1'], 'L1_ffn_W2': _L1_ffn_in['W2'], 'L1_ffn_b2': _L1_ffn_in['b2']}

def reference(x, L0_conv_w1r, L0_conv_w1i, L0_conv_w2r, L0_conv_w2i, L1_conv_lin_w, L1_conv_lin_b, L1_conv_bn_g, L1_conv_bn_b, L1_conv_bn_m, L1_conv_bn_v, L1_ffn_Wg, L1_ffn_bg, L1_ffn_W1, L1_ffn_b1, L1_ffn_W2, L1_ffn_b2):
    import jax
    import jax.numpy as jnp

    def _L0_conv_ref(x, w1r, w1i, w2r, w2i):
        import jax, jax.numpy as jnp
        import numpy as np
        B, CIN, COUT = (8, 32, 32)
        NLAT, NLON = (64, 128)
        M1, M2 = (32, 32)
        LMAX, MMAX = (NLAT, NLON // 2 + 1)
        SCALE = 1.0 / (CIN * COUT)
        TWO_PI = 2.0 * np.pi

        def _legendre(nlat, lmax, mmax):
            theta = np.pi * (np.arange(nlat) + 0.5) / nlat
            ct, st = (np.cos(theta), np.sin(theta))
            P = np.zeros((lmax, mmax, nlat), dtype=np.float64)
            P[0, 0] = 1.0 / np.sqrt(2.0)
            for m in range(min(lmax, mmax)):
                if m > 0:
                    P[m, m] = np.sqrt((2.0 * m + 1.0) / (2.0 * m)) * st * P[m - 1, m - 1]
                if m + 1 < lmax:
                    P[m + 1, m] = np.sqrt(2.0 * m + 3.0) * ct * P[m, m]
                for l in range(m + 2, lmax):
                    a = np.sqrt((4.0 * l * l - 1.0) / (l * l - m * m))
                    b = np.sqrt((2.0 * l + 1.0) * (l - 1 - m) * (l - 1 + m) / ((2.0 * l - 3.0) * (l * l - m * m)))
                    P[l, m] = a * ct * P[l - 1, m] - b * P[l - 2, m]
            w = st * np.pi / nlat
            return (P.astype(np.float32), w.astype(np.float32))
        _P, _W = _legendre(NLAT, LMAX, MMAX)
        P_ANA = jnp.asarray(_P * _W[None, None, :])
        P_SYN = jnp.asarray(_P)

        def _sht(x):
            xf = jnp.fft.rfft(x, axis=-1) * (np.sqrt(TWO_PI) / NLON)
            return jnp.einsum('lmj,bcjm->bclm', P_ANA, xf)

        def _isht(c):
            g = jnp.einsum('lmj,bclm->bcjm', P_SYN, c) * (1.0 / np.sqrt(TWO_PI))
            return jnp.fft.irfft(g, n=NLON, axis=-1) * NLON
        w1 = jax.lax.complex(w1r, w1i)
        w2 = jax.lax.complex(w2r, w2i)
        x_ft = _sht(x)
        top = jnp.einsum('bixy,ioxy->boxy', x_ft[:, :, :M1, :M2], w1)
        bot = jnp.einsum('bixy,ioxy->boxy', x_ft[:, :, -M1:, :M2], w2)
        out_ft = jnp.zeros((B, COUT, LMAX, MMAX), dtype=jnp.complex64)
        out_ft = out_ft.at[:, :, :M1, :M2].set(top)
        out_ft = out_ft.at[:, :, LMAX - M1:, :M2].set(bot)
        return _isht(out_ft)

    def _L0_ffn_ref(x_bd):
        import jax, jax.numpy as jnp
        import numpy as np
        MARK_AX = 0
        OPCODE_BASE = 16
        OP_SHL = OPCODE_BASE + 23
        OP_SHR = OPCODE_BASE + 24
        ALU_LO = 16
        ALU_HI = 20
        AX_CARRY_LO = 24
        OUTPUT_LO = 32
        OUTPUT_HI = 36
        B, SEQ, D = (8, 8192, 128)
        hot = x_bd > 0.5
        first16 = lambda off: jnp.argmax(hot[..., off:off + 16], axis=-1).astype(jnp.int32)
        lo = first16(ALU_LO)
        hi = first16(ALU_HI)
        sa = first16(AX_CARRY_LO)
        val = lo + 16 * hi
        shl = jnp.left_shift(val, sa) & 255
        shr = jnp.right_shift(val, sa)
        mark = hot[..., MARK_AX]
        is_shl = hot[..., OP_SHL]
        is_shr = jnp.logical_and(hot[..., OP_SHR], jnp.logical_not(is_shl))
        act_shl = jnp.logical_and(mark, is_shl)
        act_shr = jnp.logical_and(mark, is_shr)
        active = jnp.logical_or(act_shl, act_shr)
        res = jnp.where(act_shl, shl, jnp.where(act_shr, shr, 0))
        res = jnp.clip(res, 0, 255)
        rlo = res & 15
        rhi = res >> 4
        amp = 2.0 * active.astype(x_bd.dtype)
        add_lo = amp[..., None] * jax.nn.one_hot(rlo, 16, dtype=x_bd.dtype)
        add_hi = amp[..., None] * jax.nn.one_hot(rhi, 16, dtype=x_bd.dtype)
        out = x_bd.at[..., OUTPUT_LO:OUTPUT_LO + 16].add(add_lo)
        out = out.at[..., OUTPUT_HI:OUTPUT_HI + 16].add(add_hi)
        return out

    def _L1_conv_ref(x, lin_w, lin_b, bn_g, bn_b, bn_m, bn_v):
        import jax, jax.numpy as jnp
        import numpy as np
        TAU = 2.0
        BN_EPS = 1e-05
        ALPHA = 2.0
        NUM_HEADS = 8
        SCALE = 0.125

        def _h(v):
            return (v >= 0.0).astype(v.dtype)
        heaviside = jax.custom_vjp(_h)

        def _h_fwd(v):
            return (_h(v), v)

        def _h_bwd(v, g):
            sg = ALPHA / 2.0 / (1.0 + (jnp.pi / 2.0 * ALPHA * v) ** 2)
            return (g * sg,)
        heaviside.defvjp(_h_fwd, _h_bwd)

        def lif(x, v_th):

            def step(v, xt):
                v = v + (xt - v) / TAU
                s = heaviside(v - v_th)
                v = v * (1.0 - s)
                return (v, s)
            _, s = jax.lax.scan(step, jnp.zeros_like(x[0]), x)
            return s

        def bn(y, g, b, m, var):
            return (y - m) * (g * jax.lax.rsqrt(var + BN_EPS)) + b
        T, B, N, C = x.shape
        H = NUM_HEADS
        D = C // H

        def branch(i):
            y = jnp.einsum('tbnc,dc->tbnd', x, lin_w[i]) + lin_b[i]
            y = bn(y, bn_g[i], bn_b[i], bn_m[i], bn_v[i])
            s = lif(y, 1.0)
            return s.reshape(T, B, N, H, D).transpose(0, 1, 3, 2, 4)
        q = branch(0)
        k = branch(1)
        v = branch(2)
        attn = jnp.einsum('tbhnd,tbhmd->tbhnm', q, k) * SCALE
        o = jnp.einsum('tbhnm,tbhmd->tbhnd', attn, v)
        o = o.transpose(0, 1, 3, 2, 4).reshape(T, B, N, C)
        o = lif(o, 0.5)
        y = jnp.einsum('tbnc,dc->tbnd', o, lin_w[3]) + lin_b[3]
        y = bn(y, bn_g[3], bn_b[3], bn_m[3], bn_v[3])
        return lif(y, 1.0)

    def _L1_ffn_ref(x, Wg, bg, W1, b1, W2, b2):
        import jax, jax.numpy as jnp
        import numpy as np
        B, S, D, DFF, E, K = (4, 512, 128, 256, 8, 2)
        n_experts = W1.shape[0]
        logits = jnp.einsum('bsd,de->bse', x, Wg) + bg
        topk_vals, topk_idx = jax.lax.top_k(logits, K)
        topk_w = jax.nn.softmax(topk_vals, axis=-1)
        one_hot = jax.nn.one_hot(topk_idx, n_experts, dtype=x.dtype)
        weights_per_expert = jnp.einsum('bske,bsk->bse', one_hot, topk_w)
        h = jnp.einsum('bsd,edf->bsef', x, W1) + b1
        a, g = jnp.split(h, 2, axis=-1)
        act = jax.nn.silu(a) * g
        expert_out = jnp.einsum('bsef,efd->bsed', act, W2) + b2
        return jnp.einsum('bse,bsed->bsd', weights_per_expert, expert_out)

    def _gn(v, G=32, eps=1e-05):
        B_, H_, W_, C_ = v.shape
        g = v.reshape(B_, H_, W_, G, C_ // G)
        m = jnp.mean(g, axis=(1, 2, 4), keepdims=True)
        s = jnp.var(g, axis=(1, 2, 4), keepdims=True)
        return ((g - m) / jnp.sqrt(s + eps)).reshape(v.shape)

    def _ln_c(v, eps=1e-06):
        m = jnp.mean(v, axis=-1, keepdims=True)
        s = jnp.var(v, axis=-1, keepdims=True)
        return (v - m) / jnp.sqrt(s + eps)

    def _ln_t(v, eps=1e-05):
        m = jnp.mean(v, axis=-1, keepdims=True)
        s = jnp.var(v, axis=-1, keepdims=True)
        return (v - m) / jnp.sqrt(s + eps)

    def _to_tokens(v):
        B_, H_, W_, C_ = v.shape
        return v.reshape(B_, H_ * W_, C_)

    def _from_tokens(t, like):
        return t.reshape(like.shape)
    x = x + _L0_conv_ref(_ln_c(x), L0_conv_w1r, L0_conv_w1i, L0_conv_w2r, L0_conv_w2i)
    t = _to_tokens(x)
    t = t + _L0_ffn_ref(_ln_t(t))
    x = _from_tokens(t, x)
    x = x + _L1_conv_ref(_ln_c(x), L1_conv_lin_w, L1_conv_lin_b, L1_conv_bn_g, L1_conv_bn_b, L1_conv_bn_m, L1_conv_bn_v)
    t = _to_tokens(x)
    t = t + _L1_ffn_ref(_ln_t(t), L1_ffn_Wg, L1_ffn_bg, L1_ffn_W1, L1_ffn_b1, L1_ffn_W2, L1_ffn_b2)
    x = _from_tokens(t, x)
    return x

_drawn_inputs = setup_inputs


def setup_inputs(seed=0):
    import zlib

    import numpy as np

    out = dict(_drawn_inputs(seed))
    spreads = {'L1_conv_lin_b': (0.0, 0.1),
     'L1_conv_bn_g': (1.0, 0.2),
     'L1_conv_bn_b': (0.0, 0.1),
     'L1_conv_bn_v': (1.0, 0.2),
     'L1_ffn_bg': (0.0, 0.341),
     'L1_ffn_b1': (0.0, 0.8),
     'L1_ffn_b2': (0.0, 0.571)}
    factors = {'L0_conv_w1r': 8.0,
     'L0_conv_w1i': 8.0,
     'L0_conv_w2r': 8.0,
     'L0_conv_w2i': 8.0,
     'L1_ffn_W1': 8.0,
     'L1_ffn_W2': 8.0}
    for name, (base, spread) in spreads.items():
        noise = np.random.default_rng([zlib.crc32(name.encode()), seed]).standard_normal(out[name].shape)
        drawn = base * np.exp(spread * noise) if base else spread * noise
        out[name] = jnp.asarray(drawn.astype(out[name].dtype))
    for name, factor in factors.items():
        out[name] = (out[name] * factor).astype(out[name].dtype)
    return out
```

```python
from contextlib import ExitStack

import numpy as np

import concourse.bass as bass
from concourse import mybir

F32 = mybir.dt.float32
BF16 = mybir.dt.bfloat16
I32 = mybir.dt.int32
U32 = mybir.dt.uint32
ALU = mybir.AluOpType
ACT = mybir.ActivationFunctionType
AXX = mybir.AxisListType.X

P = 128
B, H, W, C = 8, 32, 64, 128
HP = H // 2
G = 4
L, M = 64, 32
L2 = L // 2
O = 32
RB = 2 * B
MQ = 8
LQ = 4
NCH = L2 // LQ
NTILES = B * HP
E, DFF = 8, 256
NG = NTILES // G
HEADS = 8
ATTN_SCALE = 0.125
NP2 = HP // 2
NT = 2 * B


def spectral_tables():
    nlat = W
    theta = np.pi * (np.arange(nlat) + 0.5) / nlat
    ct, st = np.cos(theta), np.sin(theta)
    p = np.zeros((L, C // 2 + 1, nlat), dtype=np.float64)
    p[0, 0] = 1.0 / np.sqrt(2.0)
    for m in range(L):
        if m > 0:
            p[m, m] = np.sqrt((2.0 * m + 1.0) / (2.0 * m)) * st * p[m - 1, m - 1]
        if m + 1 < L:
            p[m + 1, m] = np.sqrt(2.0 * m + 3.0) * ct * p[m, m]
        for l in range(m + 2, L):
            a = np.sqrt((4.0 * l * l - 1.0) / (l * l - m * m))
            b = np.sqrt((2.0 * l + 1.0) * (l - 1 - m) * (l - 1 + m) / ((2.0 * l - 3.0) * (l * l - m * m)))
            p[l, m] = a * ct * p[l - 1, m] - b * p[l - 2, m]
    weight = (st * np.pi / nlat).astype(np.float32)
    syn = p[:, :M].astype(np.float32)
    ana = syn * weight[None, None, :]
    ana_bd = np.zeros((P, M, P), np.float32)
    syn_bd = np.zeros((P, M, P), np.float32)
    for i in range(2):
        s = slice(i * 64, i * 64 + 64)
        ana_bd[s, :, s] = ana.transpose(2, 1, 0)
        syn_bd[s, :, s] = syn.transpose(0, 1, 2)
    n = np.arange(C)[:, None] * np.arange(M)[None, :] * (2 * np.pi / C)
    fwd = np.concatenate([np.cos(n), -np.sin(n)], 1) * (np.sqrt(2 * np.pi) / C)
    twice = np.where(np.arange(M) == 0, 1.0, 2.0)[None, :]
    inv = np.concatenate([np.cos(n) * twice, -np.sin(n) * twice], 1) / np.sqrt(2 * np.pi)
    inv[:, M] = 0.0
    inv_bd = np.zeros((P, 2 * C), np.float32)
    inv_bd[:64, :C] = inv_bd[64:, C:] = inv.T
    return {
        "identity": np.eye(P, dtype=np.float32),
        "first_rank": np.tile(16.0 - np.arange(16), (P, NT)).astype(np.float32),
        "expert_number": np.tile(np.arange(E), (P, NTILES)).astype(np.float32),
        "nibble_key": np.tile(np.arange(16) - 16.0, (P, NT)).astype(np.float32),
        "head_mask": np.tile(np.kron(np.eye(HEADS), np.full((C // HEADS,) * 2, ATTN_SCALE / 2)), (1, G)).astype(np.float32),
        "legendre_analysis": ana_bd.reshape(P, M * P),
        "legendre_synthesis": syn_bd.reshape(P, M * P),
        "fourier_forward": fwd.astype(np.float32),
        "fourier_inverse": inv_bd,
    }


def build(nc, t, out):
    with ExitStack() as ctx:
        def sb(name, shape, dt=F32, at=ctx):
            return at.enter_context(nc.sbuf_tensor(name, shape, dt))

        def pb(name, shape, dt=F32, at=ctx):
            return at.enter_context(nc.psum_tensor(name, shape, dt))

        def sem(name):
            return ctx.enter_context(nc.semaphore(name))

        x_sb = sb("x_sb", [P, B * HP, C])
        ident = sb("ident", [P, P])
        minus_half = sb("minus_half", [P, 2 * HP])
        x_view = t["x"].rearrange("b (hp ip) w c -> b (ip w) hp c", ip=2)

        spectral_conv(nc, t, sb, pb, sem, x_sb, ident, minus_half, x_view)
        with ExitStack() as a:
            weights = spiking_weights(nc, t, sb, pb, sem, ident, minus_half, a)
            opcode_and_spikes(nc, t, sb, pb, sem, x_sb, ident, minus_half, weights)
        experts(nc, t, sb, pb, sem, x_sb, ident, minus_half, out)


class Chain:

    def __init__(self, eng, s, base=0):
        self.eng, self.s, self.n, self.base = eng, s, 0, base

    def link(self, ins):
        self.n += 1
        ins.then_inc(self.s, 1)
        self.eng.wait_ge(self.s, self.base + self.n)


def layer_norm_stats(nc, chain, st, tmp, src, n, eps):
    for q in range(n):
        ins = nc.vector.bn_stats(st[:, q, :], src(q))
    chain.link(ins)
    nc.vector.tensor_tensor(tmp[:, 0, :], st[:, :, 1], st[:, :, 4], ALU.add)
    nc.vector.tensor_tensor(tmp[:, 2, :], st[:, :, 2], st[:, :, 5], ALU.add)
    chain.link(nc.vector.tensor_tensor(tmp[:, 1, :], st[:, :, 1], st[:, :, 4], ALU.subtract))
    nc.vector.tensor_scalar(tmp[:, 0, :], tmp[:, 0, :], 0.5, None, ALU.mult)
    chain.link(nc.vector.scalar_tensor_tensor(tmp[:, 1, :], tmp[:, 1, :], 0.25, tmp[:, 1, :], ALU.mult, ALU.mult))
    chain.link(nc.vector.scalar_tensor_tensor(tmp[:, 2, :], tmp[:, 2, :], 1.0 / C, tmp[:, 1, :], ALU.mult, ALU.add))
    return nc.vector.tensor_scalar(tmp[:, 2, :], tmp[:, 2, :], eps, None, ALU.add)


LN_LINKS = 4


def inverse_deviation(nc, tmp, minus_half):
    return nc.gpsimd.tensor_tensor(tmp[:, 3, :], tmp[:, 2, :], minus_half[:, 0:tmp.shape[2]], ALU.pow)


def spectral_conv(nc, t, sb, pb, sem, x_sb, ident, minus_half, x_view):
    spectral_w = [t["L0_conv_w1r"], t["L0_conv_w1i"], t["L0_conv_w2r"], t["L0_conv_w2i"]]
    coef = nc.dram_tensor("coefficients", [2, M // MQ, H, L, MQ * RB], F32, kind="Internal").ap()
    mixed = nc.dram_tensor("mixed", [NCH, 2, P, M * 16], F32, kind="Internal").ap()

    with ExitStack() as both:
        wc = sb("wc", [P, 2, O, LQ, M], at=both)
        s_w = [sem("mix_weights_0"), sem("mix_weights_1")]
        w_view = [w.rearrange("i o (k l) m -> k i o (l m)", l=LQ) for w in spectral_w]

        def load_w(eng, chunk, slot):
            for g in range(4):
                src = w_view[g][bass.ds(chunk, 1)] if not isinstance(chunk, int) else w_view[g][chunk:chunk + 1]
                eng.dma_start(wc[32 * g:32 * g + 32, slot].rearrange("i o l m -> i o (l m)"),
                              src.rearrange("k i o f -> (k i) o f")).then_inc(s_w[slot], 16)

        with ExitStack() as a:
            efwd = sb("efwd", [P, 2 * M], at=a)
            pana = sb("pana", [P, M, P], at=a)
            y = sb("y", [P, 2, HP, C], at=a)
            yT = sb("yT", [P, 2, G * P], at=a)
            f_sb = sb("f_sb", [P, M, HP, 2, B], at=a)
            c1 = sb("c1", [P, 2, HP, MQ, RB], at=a)
            c2 = sb("c2", [P, 2, HP, MQ, RB], at=a)
            st = sb("st", [P, 2, HP, 6], at=a)
            tmp = sb("tmp", [P, 2, 4, HP], at=a)
            ps_t = pb("ps_t", [P, 2, G * P], at=a)
            ps_f = pb("ps_f", [P, 2, 2 * G, 2 * M], at=a)
            ps_l = pb("ps_l", [P, 2, 2, 256], at=a)

            s_const = sem("a_constants")
            s_x = [sem("x_loaded_0"), sem("x_loaded_1")]
            s_chain = sem("a_vector_chain")
            s_half = sem("a_exponent")
            s_var = sem("a_variance")
            s_rstd = sem("a_inverse_deviation")
            s_y = sem("a_normalised")
            s_tr = sem("a_transposed")
            s_yT = sem("a_channel_major")
            s_dft = sem("a_fourier")
            s_dftfree = sem("a_fourier_bank_free")
            s_leg = sem("a_legendre")
            s_c1 = sem("a_coefficients")
            s_c2 = sem("a_rotated_coefficients")
            s_cw = [sem("coefficients_stored_0"), sem("coefficients_stored_1")]

            with nc.Block() as block:
                @block.sync
                def _(sp):
                    sp.dma_start(ident[:, :], t["identity"]).then_inc(s_const, 16)
                    sp.dma_start(efwd[:, :], t["fourier_forward"]).then_inc(s_const, 16)
                    for b in range(B):
                        if b >= 2:
                            sp.wait_ge(s_x[b % 2], 16 * (b // 2))
                        sp.dma_start(x_sb[:, b * HP:(b + 1) * HP, :], x_view[b]).then_inc(s_x[b % 2], 16)
                    sp.dma_start(pana[:, :, :], t["legendre_analysis"].rearrange("p (m q) -> p m q", m=M)).then_inc(s_const, 16)
                    load_w(sp, 0, 0)
                    load_w(sp, 1, 1)
                    for mq in range(M // MQ):
                        for v, (c, s) in enumerate(((c1, s_c1), (c2, s_c2))):
                            sp.wait_ge(s, (mq + 1) * (MQ // 2 if v == 0 else 1))
                            sp.dma_start(coef[v, mq].rearrange("(ih ip) l f -> (ip l) ih f", ip=2),
                                         c[:, mq % 2].rearrange("p ih m f -> p ih (m f)")).then_inc(s_cw[mq % 2], 16)
                    for k in range(2):
                        sp.wait_ge(s_cw[k], 64)

                @block.vector
                def _(dve):
                    with dve.Fori(0, B // 2) as pair:
                        for k in range(2):
                            dve.wait_ge(s_x[k], pair * 16 + 16)
                            chain = Chain(dve, s_chain, (pair * 2 + k) * LN_LINKS)
                            tile0 = (pair * 2 + k) * HP
                            layer_norm_stats(nc, chain, st[:, k], tmp[:, k],
                                             lambda q: x_sb[:, bass.ds(tile0 + q, 1), :], HP, 1e-6).then_inc(s_var, 1)
                            dve.wait_ge(s_rstd, pair * 2 + k + 1)
                            dve.wait_ge(s_tr, (pair * 2 + k) * G + 1)
                            for q in range(HP):
                                ins = nc.vector.tensor_scalar(y[:, k, q, :], x_sb[:, bass.ds(tile0 + q, 1), :],
                                                              tmp[:, k, 0, q:q + 1], tmp[:, k, 3, q:q + 1],
                                                              ALU.subtract, ALU.mult)
                            ins.then_inc(s_y, 1)
                    for mq in range(M // MQ):
                        k = mq % 2
                        dve.wait_ge(s_c1, (mq + 1) * (MQ // 2))
                        if mq >= 2:
                            dve.wait_ge(s_cw[k], 32)
                        a1 = c1[:, k].rearrange("p ih m f -> p (ih m) f")
                        a2 = c2[:, k].rearrange("p ih m f -> p (ih m) f")
                        nc.vector.tensor_scalar(a2[:, :, 0:B], a1[:, :, B:RB], -1.0, None, ALU.mult)
                        nc.vector.tensor_copy(a2[:, :, B:RB], a1[:, :, 0:B]).then_inc(s_c2, 1)

                @block.gpsimd
                def _(pool):
                    nc.gpsimd.memset(minus_half[:, :], -0.5).then_inc(s_half, 1)
                    pool.wait_ge(s_half, 1)
                    with pool.Fori(0, B // 2) as pair:
                        for k in range(2):
                            pool.wait_ge(s_var, pair * 2 + k + 1)
                            inverse_deviation(nc, tmp[:, k], minus_half).then_inc(s_rstd, 1)

                @block.tensor
                def _(pe):
                    pe.sem_inc(s_tr, G + 1)
                    pe.sem_inc(s_dft, 2)
                    pe.wait_ge(s_const, 48)
                    with pe.Fori(0, B // 2) as pair:
                        for k in range(2):
                            g0 = (pair * 2 + k) * G

                            def transposes(g):
                                pe.wait_ge(s_yT, g0 + g + 1)
                                for q in range(G):
                                    ins = nc.tensor.transpose(ps_t[:, g % 2, q * P:(q + 1) * P],
                                                              y[:, k, g * G + q, :], ident[:, :])
                                ins.then_inc(s_tr, 1)

                            def fourier(g):
                                pe.wait_ge(s_yT, g0 + g + 3)
                                if g % 2 == 0:
                                    pe.wait_ge(s_dftfree, (pair * 2 + k) * 2 + g // 2 + 1)
                                for q in range(G):
                                    ins = nc.tensor.matmul(ps_f[:, g // 2, (g % 2) * G + q, :],
                                                           yT[:, g % 2, q * P:(q + 1) * P], efwd[:, :],
                                                           start=True, stop=True)
                                ins.then_inc(s_dft, 1)

                            pe.wait_ge(s_y, pair * 2 + k + 1)
                            for g in range(HP // G):
                                transposes(g)
                                if g:
                                    fourier(g - 1)
                            fourier(HP // G - 1)
                    pe.wait_ge(s_dftfree, 2 * B + 2)
                    for m in range(M):
                        if m % 2 == 0 and m >= 4:
                            pe.wait_ge(s_c1, m // 2 - 1)
                        ins = nc.tensor.matmul(ps_l[:, (m // 2) % 2, m % 2, :], pana[:, m, :],
                                               f_sb[:, m].rearrange("p h r b -> p (h r b)"), start=True, stop=True)
                        if m % 2:
                            ins.then_inc(s_leg, 1)

                @block.scalar
                def _(act):
                    act.sem_inc(s_yT, 2)
                    act.sem_inc(s_dftfree, 2)
                    with act.Fori(0, B // 2) as pair:
                        for k in range(2):
                            bb = pair * 2 + k
                            for g in range(HP // G):
                                act.wait_ge(s_tr, bb * G + g + 2 + G)
                                act.wait_ge(s_dft, bb * G + g + 1)
                                nc.scalar.activation(yT[:, g % 2, :], ps_t[:, g % 2, :], ACT.Copy)\
                                    .then_inc(s_yT, 1)
                                if g % 2:
                                    act.wait_ge(s_dft, bb * G + g + 3)
                                    q0 = (g - 1) * G
                                    nc.scalar.activation(
                                        f_sb[:, :, q0:q0 + 2 * G, :, bb].rearrange("p m q r -> p q r m"),
                                        ps_f[:, g // 2].rearrange("p q (r m) -> p q r m", r=2), ACT.Copy)\
                                        .then_inc(s_dftfree, 1)

                    for m2 in range(M // 2):
                        k = (2 * m2 // MQ) % 2
                        act.wait_ge(s_leg, m2 + 1)
                        if 2 * m2 % MQ == 0 and 2 * m2 >= 2 * MQ:
                            act.wait_ge(s_cw[k], 32)
                        ml = 2 * m2 % MQ
                        nc.scalar.activation(c1[:, k, :, ml:ml + 2, :].rearrange("p ih m f -> p m ih f"),
                                             ps_l[:, m2 % 2].rearrange("p m (ih f) -> p m ih f", ih=HP), ACT.Copy)\
                            .then_inc(s_c1, 1)

        with ExitStack() as a:
            coefc = sb("coefc", [P, 2, M // MQ, LQ, MQ, RB], at=a)
            sblk = sb("sblk", [P, 2, LQ, M, 2 * RB], at=a)
            mo = sb("mo", [P, 2, 2, M, 16], at=a)
            ps_m = pb("ps_m", [P, 2, 2, 512], at=a)
            s_cc = [sem("coefficients_loaded_0"), sem("coefficients_loaded_1")]
            s_zero = sem("m_blocks_zeroed")
            s_sd = sem("m_lower_blocks")
            s_sa = sem("m_upper_blocks")
            s_mm = sem("m_mixed")
            s_ed = sem("m_first_orders_out")
            s_ea = sem("m_last_orders_out")
            s_mw = [sem("mixed_stored_0"), sem("mixed_stored_1")]

            def load_coef(eng, chunk, slot):
                for g in range(4):
                    half, part = g // 2, g % 2
                    base = coef[part].rearrange("q i l f -> i q (l f)")
                    off = (half * L2 + chunk * LQ) * MQ * RB
                    eng.dma_start(coefc[32 * g:32 * g + 32, slot].rearrange("i q l m f -> i q (l m f)"),
                                  base[:, :, bass.ds(off, LQ * MQ * RB)]).then_inc(s_cc[slot], 16)

            def store_mixed(eng, chunk, slot):
                eng.wait_ge(s_ed, chunk + 3)
                eng.wait_ge(s_ea, chunk + 3)
                eng.dma_start(mixed[bass.ds(chunk, 1)].rearrange("k op p f -> p (k op) f"),
                              mo[:, slot].rearrange("p op m o -> p op (m o)")).then_inc(s_mw[slot], 16)

            with nc.Block() as block:
                @block.sync
                def _(sp):
                    for k in range(2):
                        sp.sem_inc(s_mw[k], 1)
                    load_coef(sp, 0, 0)
                    load_coef(sp, 1, 1)
                    with sp.Fori(1, NCH // 2) as pair:
                        for k in range(2):
                            n = pair * 2 + k
                            sp.wait_ge(s_mm, n + 1)
                            load_w(sp, n, k)
                            sp.wait_ge(s_sd, n - 1)
                            sp.wait_ge(s_sa, n - 1)
                            load_coef(sp, n, k)
                            store_mixed(sp, n - 2, k)
                    for k in range(2):
                        store_mixed(sp, NCH - 2 + k, k)
                    for k in range(2):
                        sp.wait_ge(s_mw[k], 16 * NCH // 2 + 1)

                @block.gpsimd
                def _(pool):
                    nc.gpsimd.memset(sblk[:, 0], 0.0).then_inc(s_zero, 1)
                    nc.gpsimd.memset(sblk[:, 1], 0.0).then_inc(s_zero, 1)

                @block.vector
                def _(dve):
                    dve.sem_inc(s_ed, 2)
                    dve.wait_ge(s_zero, 2)

                    with dve.Fori(0, NCH // 2) as pair:
                        for k in range(2):
                            n = pair * 2 + k
                            dve.wait_ge(s_cc[k], pair * 64 + 64)
                            dve.wait_ge(s_mm, n + 1)
                            for l in range(LQ):
                                ins = nc.vector.tensor_copy(
                                    sblk[0:64, k, l, :, 0:RB].rearrange("p (q m) f -> p q m f", q=M // MQ),
                                    coefc[0:64, k, :, l])
                            ins.then_inc(s_sd, 1)
                            dve.wait_ge(s_mm, n + 3)
                            dve.wait_ge(s_mw[k], pair * 16 + 1)
                            nc.vector.tensor_copy(
                                mo[:, k, :, 0:M // 2, :],
                                ps_m[:, k, 0, :].rearrange("p (m o op) -> p op m o", op=2, o=16))\
                                .then_inc(s_ed, 1)

                @block.scalar
                def _(act):
                    act.sem_inc(s_ea, 2)
                    act.wait_ge(s_zero, 2)
                    with act.Fori(0, NCH // 2) as pair:
                        for k in range(2):
                            n = pair * 2 + k
                            act.wait_ge(s_cc[k], pair * 64 + 64)
                            act.wait_ge(s_mm, n + 1)
                            for l in range(LQ):
                                ins = nc.scalar.activation(
                                    sblk[64:128, k, l, :, RB:2 * RB].rearrange("p (q m) f -> p q m f", q=M // MQ),
                                    coefc[64:128, k, :, l], ACT.Copy)
                            ins.then_inc(s_sa, 1)
                            act.wait_ge(s_mm, n + 3)
                            act.wait_ge(s_mw[k], pair * 16 + 1)
                            nc.scalar.activation(
                                mo[:, k, :, M // 2:M, :],
                                ps_m[:, k, 1, :].rearrange("p (m o op) -> p op m o", op=2, o=16), ACT.Copy)\
                                .then_inc(s_ea, 1)

                @block.tensor
                def _(pe):
                    pe.sem_inc(s_mm, 2)
                    with pe.Fori(0, NCH // 2) as pair:
                        for k in range(2):
                            n = pair * 2 + k
                            pe.wait_ge(s_w[k], pair * 64 + 64)
                            pe.wait_ge(s_sd, n + 1)
                            pe.wait_ge(s_sa, n + 1)
                            pe.wait_ge(s_ed, n + 1)
                            pe.wait_ge(s_ea, n + 1)
                            for l in range(LQ):
                                for m in range(M):
                                    half, col = m // (M // 2), (m % (M // 2)) * O
                                    ins = nc.tensor.matmul(ps_m[32 * l:32 * l + 32, k, half, col:col + O],
                                                           sblk[:, k, l, m, :], wc[:, k, :, l, m],
                                                           start=True, stop=True)
                            ins.then_inc(s_mm, 1)

    with ExitStack() as a:
        psyn = sb("psyn", [P, M, P], at=a)
        einv = sb("einv", [P, 2 * C], at=a)
        gin = sb("gin", [P, M // MQ, RB, MQ, 16], at=a)
        h_sb = sb("h_sb", [P, B, HP, 2, M], at=a)
        hc = sb("hc", [P, 2, HP, 2, M], at=a)
        hT = sb("hT", [P, 2, G * P], at=a)
        ps_g = pb("ps_g", [P, 2, 2, 256], at=a)
        ps_t = pb("ps_t2", [P, 2, G * P], at=a)
        ps_y = pb("ps_y", [P, 2, G, 2 * C], at=a)
        s_const = sem("c_constants")
        s_gin = [sem(f"mixed_loaded_{q}") for q in range(M // MQ)]
        s_leg = sem("c_legendre")
        s_h = [sem("c_orders_even"), sem("c_orders_odd")]
        s_hc = sem("c_batch_copied")
        s_tr = sem("c_transposed")
        s_hT = sem("c_orders_major")
        s_y = sem("c_grid")
        s_yfree = sem("c_grid_bank_free")

        def evacuate(copy, m2):
            return copy(h_sb[:, :, :, :, 2 * m2:2 * m2 + 2].rearrange("p b h r m -> p m r (b h)"),
                        ps_g[:, m2 % 2].rearrange("p m (r bh) -> p m r bh", r=2))

        with nc.Block() as block:
            @block.sync
            def _(sp):
                sp.dma_start(psyn[:, :, :], t["legendre_synthesis"].rearrange("p (m q) -> p m q", m=M)).then_inc(s_const, 16)
                sp.dma_start(einv[:, :], t["fourier_inverse"]).then_inc(s_const, 16)
                for q in range(M // MQ):
                    for op in range(2):
                        for half in range(2):
                            src = mixed[:, op].rearrange("k (l h r) (q f) -> h q k l r f", l=LQ, h=2, q=M // MQ)[half, q]
                            p0 = op * 64 + half * L2
                            for k in range(NCH):
                                sp.dma_start(gin[p0 + k * LQ:p0 + k * LQ + LQ, q].rearrange("p r m o -> p r (m o)"), src[k])\
                                    .then_inc(s_gin[q], 16)

            @block.tensor
            def _(pe):
                pe.sem_inc(s_tr, 3)
                pe.sem_inc(s_y, 2)
                pe.wait_ge(s_const, 32)
                for m in range(M):
                    if m % MQ == 0:
                        pe.wait_ge(s_gin[m // MQ], 16 * 4 * NCH)
                    if m % 2 == 0 and m >= 4:
                        pe.wait_ge(s_h[(m // 2) % 2], m // 4)
                    ins = nc.tensor.matmul(ps_g[:, (m // 2) % 2, m % 2, :], psyn[:, m, :],
                                           gin[:, m // MQ, :, m % MQ, :], start=True, stop=True)
                    if m % 2:
                        ins.then_inc(s_leg, 1)

                with pe.Fori(0, B // 2) as pair:
                    for k in range(2):
                        b = pair * 2 + k

                        def transposes(g):
                            pe.wait_ge(s_hT, b * 2 + g + 1)
                            for q in range(G):
                                t0 = (g * G + q) * 2
                                ins = nc.tensor.transpose(ps_t[:, g % 2, q * P:(q + 1) * P],
                                                          hc[:, k, t0:t0 + 2].rearrange("p q r m -> p (q r m)"), ident[:, :])
                            ins.then_inc(s_tr, 1)

                        def grid(g):
                            pe.wait_ge(s_hT, b * 2 + g + 3)
                            pe.wait_ge(s_yfree, b * 2 + g + 1)
                            for q in range(G):
                                ins = nc.tensor.matmul(ps_y[:, g, q], hT[:, g, q * P:(q + 1) * P], einv[:, :],
                                                       start=True, stop=True)
                            ins.then_inc(s_y, 1)

                        pe.wait_ge(s_hc, b + 1)
                        transposes(0)
                        transposes(1)
                        grid(0)
                        grid(1)

            @block.scalar
            def _(act):
                act.sem_inc(s_hT, 2)
                for m2 in range(0, M // 2, 2):
                    act.wait_ge(s_leg, m2 + 1)
                    evacuate(lambda o, i: nc.scalar.activation(o, i, ACT.Copy), m2).then_inc(s_h[0], 1)
                with act.Fori(0, B // 2) as pair:
                    for k in range(2):
                        for g in range(2):
                            n = (pair * 2 + k) * 2 + g
                            act.wait_ge(s_tr, n + 4)
                            act.wait_ge(s_y, n + 1)
                            nc.scalar.activation(hT[:, g % 2, :], ps_t[:, g % 2, :], ACT.Copy)\
                                .then_inc(s_hT, 1)

            @block.gpsimd
            def _(pool):
                pool.wait_ge(s_h[0], M // 4)
                pool.wait_ge(s_h[1], M // 4)
                with pool.Fori(0, B // 2) as pair:
                    for k in range(2):
                        b = pair * 2 + k
                        pool.wait_ge(s_tr, b * 2 + 1)
                        nc.gpsimd.tensor_copy(hc[:, k], h_sb[:, b]).then_inc(s_hc, 1)

            @block.vector
            def _(dve):
                dve.sem_inc(s_yfree, 2)
                for m2 in range(1, M // 2, 2):
                    dve.wait_ge(s_leg, m2 + 1)
                    evacuate(nc.vector.tensor_copy, m2).then_inc(s_h[1], 1)
                with dve.Fori(0, B // 2) as pair:
                    for k in range(2):
                        for g in range(2):
                            n = (pair * 2 + k) * 2 + g
                            dve.wait_ge(s_y, n + 3)
                            for bank in range(2):
                                rows = x_sb[:, bass.ds(n * 2 * G + bank * G, G), :].rearrange("p q c -> p (q c)")
                                ins = nc.vector.tensor_tensor(
                                    rows, rows, ps_y[:, g, bank * 2:bank * 2 + 2].rearrange("p q c -> p (q c)"), ALU.add)
                            ins.then_inc(s_yfree, 1)


def split3(nc, chain, parts, x, rest):
    chain.link(nc.vector.tensor_copy(parts[0], x))
    chain.link(nc.vector.tensor_tensor(rest, x, parts[0], ALU.subtract))
    chain.link(nc.vector.tensor_copy(parts[1], rest))
    return nc.vector.tensor_tensor(parts[2], rest, parts[1], ALU.subtract)


def spiking_weights(nc, t, sb, pb, sem, ident, minus_half, keep):
    wqkv = sb("wqkv", [P, 3 * C], at=keep)
    wo = sb("wo", [P, 3, C], BF16, at=keep)
    bias = sb("bias", [3, 4 * C], BF16, at=keep)
    ones = sb("ones", [3, P], BF16, at=keep)
    with ExitStack() as a:
        lw = sb("lw", [P, 4, C], at=a)
        par = sb("par", [P, 5, 4], at=a)
        col = sb("col", [P, 3, 4], at=a)
        bpart = sb("bpart", [P, 4, 3], at=a)
        bhalf = sb("bhalf", [P, 3, 4], BF16, at=a)
        rest = sb("rest", [P, C], at=a)
        rest4 = sb("rest4", [P, 4], at=a)
        ps_w = pb("ps_w", [P, 4 * C], at=a)
        ps_b = pb("ps_b", [3, 4 * C], at=a)
        s_load = sem("w_loaded")
        s_chain = sem("w_chain")
        s_var = sem("w_variance")
        s_rstd = sem("w_inverse_deviation")
        s_scaled = sem("w_scaled")
        s_t = sem("w_transposed")

        with nc.Block() as block:
            @block.sync
            def _(sp):
                sp.dma_start(lw[:, :, :], t["L1_conv_lin_w"].rearrange("i d c -> d i c")).then_inc(s_load, 16)
                for n, name in enumerate(("lin_b", "bn_g", "bn_b", "bn_m", "bn_v")):
                    with nc.allow_non_contiguous_dma(reason="512 parameters, once"):
                        sp.dma_start(par[:, n, :], t[f"L1_conv_{name}"].rearrange("i d -> d i")).then_inc(s_load, 16)

            @block.gpsimd
            def _(pool):
                pool.wait_ge(s_var, 1)
                nc.gpsimd.tensor_tensor(col[:, 0, :], col[:, 0, :], minus_half[:, 0:4], ALU.pow).then_inc(s_rstd, 1)

            @block.vector
            def _(dve):
                chain = Chain(dve, s_chain)
                dve.wait_ge(s_load, 96)
                nc.vector.memset(ones[:, :], 1.0)
                nc.vector.tensor_scalar(col[:, 0, :], par[:, 4, :], 1e-5, None, ALU.add).then_inc(s_var, 1)
                dve.wait_ge(s_rstd, 1)
                nc.vector.tensor_tensor(col[:, 1, :], par[:, 1, :], col[:, 0, :], ALU.mult)
                chain.link(nc.vector.tensor_tensor(col[:, 2, :], par[:, 0, :], par[:, 3, :], ALU.subtract))
                chain.link(nc.vector.tensor_tensor(col[:, 2, :], col[:, 2, :], col[:, 1, :], ALU.mult))
                chain.link(nc.vector.tensor_tensor(col[:, 2, :], col[:, 2, :], par[:, 2, :], ALU.add))
                chain.link(nc.vector.tensor_scalar(col[:, 2, :], col[:, 2, :], 0.5, None, ALU.mult))
                for i in range(4):
                    ins = nc.vector.tensor_scalar(lw[:, i, :], lw[:, i, :], col[:, 1, i:i + 1], 0.5, ALU.mult, ALU.mult)
                chain.link(ins)
                chain.link(split3(nc, chain, [bhalf[:, n, :] for n in range(3)], col[:, 2, :], rest4[:, :]))
                nc.vector.tensor_copy(bpart[:, :, :].rearrange("p i n -> p n i"), bhalf[:, :, :]).then_inc(s_scaled, 1)
                dve.wait_ge(s_t, 1)
                nc.vector.tensor_copy(wqkv[:, :], ps_w[:, 0:3 * C])
                nc.vector.tensor_copy(bias[:, :], ps_b[:, :])
                split3(nc, chain, [wo[:, n, :] for n in range(3)], ps_w[:, 3 * C:4 * C], rest[:, :])

            @block.tensor
            def _(pe):
                pe.wait_ge(s_scaled, 1)
                for i in range(4):
                    nc.tensor.transpose(ps_w[:, i * C:(i + 1) * C], lw[:, i, :], ident[:, :])
                for i in range(4):
                    ins = nc.tensor.transpose(ps_b[:, i * C:(i + 1) * C], bpart[:, i, :], ident[:, :])
                ins.then_inc(s_t, 1)
    return wqkv, wo, bias, ones


def opcode_and_spikes(nc, t, sb, pb, sem, x_sb, ident, minus_half, weights):
    wqkv, wo, bias, ones = weights
    xv = x_sb[:, :, :].rearrange("p (b i j) c -> p b i j c", b=B, j=2)
    with ExitStack() as a:
        rank = sb("rank", [P, NT, 16], at=a)
        key = sb("key", [P, NT, 16], at=a)
        mask = sb("mask", [P, G * C], at=a)
        st = sb("e_st", [P, NT, 6], at=a)
        tmp = sb("e_tmp", [P, 2, 4, NT], at=a)
        u = sb("u", [P, NT, C], at=a)
        win = sb("win", [P, 3, NT, 16], at=a)
        first = sb("first", [P, 3, NT], at=a)
        fl = sb("fl", [P, 4, NT], at=a)
        ints = sb("ints", [P, 10, NT], I32, at=a)
        flt = sb("flt", [P, 4, NT], at=a)
        eq = sb("eq", [P, 2, NT, 16], at=a)
        z = sb("z", [P, NT, C], at=a)
        zT = sb("zT", [P, NT, P], at=a)
        v1 = sb("v1", [P, 2, 2, 3 * C], at=a)
        r1 = sb("r1", [P, 2, 3 * C], at=a)
        spk = sb("spk", [P, B, 2, 3 * C], BF16, at=a)
        kvm = sb("kvm", [P, 2, 2, G * C], BF16, at=a)
        vo = sb("vo", [P, 2, 2 * P], at=a)
        ro = sb("ro", [P, 2 * P], at=a)
        so = sb("so", [P, 2, 2 * P], BF16, at=a)
        vy = sb("vy", [P, 2, C], at=a)
        ry = sb("ry", [P, 2, C], at=a)
        ps_q = pb("ps_q", [P, 2, 2, 512], at=a)
        ps_kv = pb("ps_kv", [P, 2, G * C], at=a)
        ps_o = pb("ps_o", [P, 512], at=a)
        ps_y = pb("ps_y2", [P, 512], at=a)

        s_const = sem("e_constants")
        s_chain = sem("e_chain")
        s_var = sem("e_variance")
        s_rstd = sem("e_inverse_deviation")
        s_beat = sem("e_beat")
        s_z = sem("e_normalised")
        s_tr = sem("e_transposed")
        s_zT = sem("e_channel_major")
        s_qkv = sem("e_projected")
        s_v = sem("e_membranes")
        s_spk = sem("e_spikes")
        s_kv = sem("e_key_values")
        s_kvm = sem("e_key_values_masked")
        s_o = sem("e_attended")
        s_vo = sem("e_attended_membranes")
        s_so = sem("e_attended_spikes")
        s_y = sem("e_output_projected")
        s_vy = sem("e_output_membranes")

        PREP_LINKS = 2 * LN_LINKS + 17

        def prepare(dve, i):
            chain = Chain(dve, s_chain, i * PREP_LINKS)
            tile = lambda q: xv[:, q // 2, i, q % 2, :]
            layer_norm_stats(nc, chain, st, tmp[:, 0], tile, NT, 1e-5).then_inc(s_var, 1)
            dve.wait_ge(s_rstd, i * 2 + 1)
            for q in range(NT):
                ins = nc.vector.tensor_scalar(u[:, q, :], tile(q), tmp[:, 0, 0, q:q + 1], tmp[:, 0, 3, q:q + 1],
                                              ALU.subtract, ALU.mult)
            chain.link(ins)
            nc.vector.tensor_scalar(fl[:, 0, :], u[:, :, 0], 0.5, None, ALU.is_gt)
            for n, lo in enumerate((16, 20, 24)):
                ins = nc.vector.scalar_tensor_tensor(win[:, n], u[:, :, lo:lo + 16], 0.5, rank[:, :, :], ALU.is_gt, ALU.mult)
            chain.link(ins)
            nc.vector.tensor_reduce(first[:, :, :], win[:, :, :, :], AXX, ALU.max)
            nc.vector.scalar_tensor_tensor(fl[:, 1, :], u[:, :, 39], 0.5, fl[:, 0, :], ALU.is_gt, ALU.mult)
            chain.link(nc.vector.scalar_tensor_tensor(fl[:, 2, :], u[:, :, 39], 0.5, fl[:, 0, :], ALU.is_le, ALU.mult))
            chain.link(nc.vector.scalar_tensor_tensor(fl[:, 2, :], u[:, :, 40], 0.5, fl[:, 2, :], ALU.is_gt, ALU.mult))
            chain.link(nc.vector.tensor_scalar(ints[:, 0:3, :], first[:, :, :], -1.0, 16.0, ALU.mult, ALU.add))
            nc.vector.tensor_tensor(fl[:, 3, :], fl[:, 1, :], fl[:, 2, :], ALU.add)
            chain.link(nc.vector.tensor_scalar(ints[:, 0:3, :], ints[:, 0:3, :], 15, None, ALU.bitwise_and))
            lo, hi, sa, val, shl, shr, res, rlo, rhi = (ints[:, n, :] for n in range(9))
            chain.link(nc.vector.scalar_tensor_tensor(val, hi, 4, lo, ALU.logical_shift_left, ALU.bitwise_or))
            nc.vector.tensor_tensor(shr, val, sa, ALU.logical_shift_right)
            chain.link(nc.vector.tensor_tensor(shl, val, sa, ALU.logical_shift_left))
            chain.link(nc.vector.tensor_scalar(shl, shl, 255, None, ALU.bitwise_and))
            nc.vector.tensor_tensor(flt[:, 0, :], shl, fl[:, 1, :], ALU.mult)
            chain.link(nc.vector.tensor_tensor(flt[:, 1, :], shr, fl[:, 2, :], ALU.mult))
            chain.link(nc.vector.tensor_tensor(res, flt[:, 0, :], flt[:, 1, :], ALU.add))
            nc.vector.tensor_scalar(rlo, res, 15, None, ALU.bitwise_and)
            chain.link(nc.vector.tensor_scalar(rhi, res, 4, None, ALU.logical_shift_right))
            nc.vector.scalar_tensor_tensor(flt[:, 2, :], fl[:, 3, :], -16.0, rlo, ALU.mult, ALU.add)
            chain.link(nc.vector.scalar_tensor_tensor(flt[:, 3, :], fl[:, 3, :], -16.0, rhi, ALU.mult, ALU.add))
            for n in range(2):
                ins = nc.vector.tensor_tensor(eq[:, n], key[:, :, :], flt[:, 2 + n, :].unsqueeze(2).broadcast_to([P, NT, 16]),
                                              ALU.is_equal)
            chain.link(ins)
            for n, lo in enumerate((32, 36)):
                part = u[:, :, lo:lo + 16]
                chain.link(nc.vector.scalar_tensor_tensor(part, eq[:, n], 2.0, part, ALU.mult, ALU.add))
            rows = xv[:, :, i, :, :]
            chain.link(nc.vector.tensor_tensor(rows, rows, u[:, :, :].rearrange("p (b j) c -> p b j c", j=2), ALU.add))
            dve.sem_inc(s_beat, 1)
            layer_norm_stats(nc, chain, st, tmp[:, 1], tile, NT, 1e-6).then_inc(s_var, 1)
            dve.wait_ge(s_rstd, i * 2 + 2)
            dve.wait_ge(s_tr, i * 4 + 1)
            for q in range(NT):
                ins = nc.vector.tensor_scalar(z[:, q, :], tile(q), tmp[:, 1, 0, q:q + 1], tmp[:, 1, 3, q:q + 1],
                                              ALU.subtract, ALU.mult)
            ins.then_inc(s_z, 1)
            assert chain.n == PREP_LINKS, chain.n

        s_reset = sem("e_reset")

        def neurons(dve, i):
            resets = [i * (3 * B)]

            def reset(ins):
                resets.append(1)
                ins.then_inc(s_reset, 1)

            def resets_done(n):
                dve.wait_ge(s_reset, resets[0] + n)

            for b in range(B):
                dve.wait_ge(s_qkv, i * B + b + 1 + 1)
                dve.wait_ge(s_spk, i * B + max(b - 1, 0) + 1)
                src = ps_q[:, b % 2, :, 0:3 * C]
                if b == 0:
                    nc.vector.tensor_copy(v1[:, 0], src).then_inc(s_v, 1)
                else:
                    resets_done(b)
                    nc.vector.scalar_tensor_tensor(v1[:, b % 2], r1[:, :, :], 0.5, src, ALU.mult, ALU.add).then_inc(s_v, 1)
                dve.wait_ge(s_v, i * B + b + 1 + 1)
                reset(nc.vector.scalar_tensor_tensor(r1[:, :, :], v1[:, b % 2], 1.0, v1[:, b % 2], ALU.is_lt, ALU.mult))

            def masked(bp):
                dve.wait_ge(s_kv, i * 4 + bp + 1 + 1)
                dve.wait_ge(s_o, i * B + max(2 * bp - 2, 0) + 1)
                for ip in range(2):
                    ins = nc.vector.tensor_tensor(kvm[:, bp % 2, ip], ps_kv[:, ip], mask[:, :], ALU.mult)
                ins.then_inc(s_kvm, 1)

            def attended(b):
                dve.wait_ge(s_o, i * B + b + 1 + 1)
                dve.wait_ge(s_so, i * B + max(b - 1, 0) + 1)
                if b == 0:
                    nc.vector.tensor_copy(vo[:, 0], ps_o[:, 0:2 * P]).then_inc(s_vo, 1)
                else:
                    resets_done(B + max(2 * b - 2, 1))
                    nc.vector.scalar_tensor_tensor(vo[:, b % 2], ro[:, :], 0.5, ps_o[:, 0:2 * P], ALU.mult, ALU.add)\
                        .then_inc(s_vo, 1)
                dve.wait_ge(s_vo, i * B + b + 1 + 1)
                reset(nc.vector.scalar_tensor_tensor(ro[:, :], vo[:, b % 2], 0.5, vo[:, b % 2], ALU.is_lt, ALU.mult))

            def output(b):
                dve.wait_ge(s_y, i * B + b + 1 + 1)
                src = ps_y[:, 0:2 * C].rearrange("p (j c) -> p j c", j=2)
                if b == 0:
                    nc.vector.tensor_copy(vy[:, :, :], src).then_inc(s_vy, 1)
                else:
                    resets_done(B + 2 * b + 1)
                    nc.vector.scalar_tensor_tensor(vy[:, :, :], ry[:, :, :], 0.5, src, ALU.mult, ALU.add).then_inc(s_vy, 1)
                dve.wait_ge(s_vy, i * B + b + 1 + 1)
                rows = xv[:, b, i, :, :]
                nc.vector.scalar_tensor_tensor(rows, vy[:, :, :], 1.0, rows, ALU.is_ge, ALU.add)
                reset(nc.vector.scalar_tensor_tensor(ry[:, :, :], vy[:, :, :], 1.0, vy[:, :, :], ALU.is_lt, ALU.mult))

            masked(0)
            for b in range(B):
                if b % 2 == 0 and b // 2 + 1 < 4:
                    masked(b // 2 + 1)
                attended(b)
                if b:
                    output(b - 1)
            output(B - 1)
            assert len(resets) == 1 + 3 * B

        def project(pe, i):
            for b in range(B):
                if b < 2:
                    pe.wait_ge(s_zT, i * 4 + 2 * b + 2 + 1)
                else:
                    if b == 2:
                        pe.wait_ge(s_zT, i * 4 + 4 + 1)
                    pe.wait_ge(s_v, i * B + b - 1 + 1)
                for j in range(2):
                    q = 2 * b + j
                    dst = ps_q[:, b % 2, j]
                    nc.tensor.matmul(dst[:, 0:P], wqkv[:, 0:C], zT[:, q, :], start=True, stop=False)
                    nc.tensor.matmul(dst[:, 0:P], bias[:, 0:C], ones[:, :], start=False, stop=True)
                    nc.tensor.matmul(dst[:, P:3 * P], zT[:, q, :], wqkv[:, C:3 * C], start=True, stop=False)
                    ins = nc.tensor.matmul(dst[:, P:3 * P], ones[:, :], bias[:, C:3 * C], start=False, stop=True)
                ins.then_inc(s_qkv, 1)

        def attend(pe, i):
            def key_values(bp):
                pe.wait_ge(s_spk, i * B + 2 * bp + 2 + 1)
                pe.wait_ge(s_kvm, i * 4 + bp + 1)
                for n in range(4):
                    b, j = 2 * bp + n // 2, n % 2
                    for ip in range(2):
                        rows = slice(64 * ip, 64 * ip + 64)
                        ins = nc.tensor.matmul(ps_kv[:, ip, n * C:(n + 1) * C], spk[rows, b, j, C:2 * C],
                                               spk[rows, b, j, 2 * C:3 * C], start=True, stop=True)
                ins.then_inc(s_kv, 1)

            def attended(b):
                pe.wait_ge(s_kvm, i * 4 + b // 2 + 1 + 1)
                pe.wait_ge(s_vo, i * B + b + 1)
                for j in range(2):
                    for ip in range(2):
                        n = (b % 2) * 2 + j
                        ins = nc.tensor.matmul(ps_o[:, j * P + ip * 64:j * P + ip * 64 + 64],
                                               kvm[:, (b // 2) % 2, ip, n * C:(n + 1) * C],
                                               spk[:, b, j, ip * 64:ip * 64 + 64], start=True, stop=True)
                ins.then_inc(s_o, 1)

            def output(b):
                pe.wait_ge(s_so, i * B + b + 1 + 1)
                pe.wait_ge(s_vy, i * B + b + 1)
                for j in range(2):
                    for n in range(3):
                        nc.tensor.matmul(ps_y[:, j * C:(j + 1) * C], so[:, b % 2, j * P:(j + 1) * P], wo[:, n, :],
                                         start=(n == 0), stop=False)
                    ins = nc.tensor.matmul(ps_y[:, j * C:(j + 1) * C], ones[:, :], bias[:, 3 * C:4 * C],
                                           start=False, stop=True)
                ins.then_inc(s_y, 1)

            key_values(0)
            for b in range(B):
                if b % 2 == 0 and b // 2 + 1 < 4:
                    key_values(b // 2 + 1)
                attended(b)
                if b:
                    output(b - 1)
            output(B - 1)

        def turn(pe, i):
            pe.wait_ge(s_z, i + 1 + 1)
            pe.wait_ge(s_v, i * B + 1)
            for g in range(4):
                for q in range(G):
                    ins = nc.tensor.transpose(ps_q[:, g // 2, g % 2, q * P:(q + 1) * P], z[:, g * G + q, :], ident[:, :])
                ins.then_inc(s_tr, 1)

        def fire(pool, i):
            for b in range(B):
                pool.wait_ge(s_v, i * B + b + 1 + 1)
                if b == 0:
                    pool.wait_ge(s_o, i * B + 1)
                pool.sem_inc(s_beat, 1)
                nc.gpsimd.tensor_scalar(spk[:, b], v1[:, b % 2], 1.0, None, ALU.is_ge).then_inc(s_spk, 1)
            for b in range(B):
                pool.wait_ge(s_vo, i * B + b + 1 + 1)
                pool.wait_ge(s_y, i * B + max(b - 1, 0) + 1)
                pool.sem_inc(s_beat, 1)
                nc.gpsimd.tensor_scalar(so[:, b % 2], vo[:, b % 2], 0.5, None, ALU.is_ge).then_inc(s_so, 1)

        def deviations(pool, i):
            for n in range(2):
                pool.wait_ge(s_var, i * 2 + n + 1)
                inverse_deviation(nc, tmp[:, n], minus_half).then_inc(s_rstd, 1)

        with nc.Block() as block:
            @block.sync
            def _(sp):
                sp.dma_start(rank[:, :, :], t["first_rank"].rearrange("p (q k) -> p q k", k=16)).then_inc(s_const, 16)
                sp.dma_start(key[:, :, :], t["nibble_key"].rearrange("p (q k) -> p q k", k=16)).then_inc(s_const, 16)
                sp.dma_start(mask[:, :], t["head_mask"]).then_inc(s_const, 16)

            @block.vector
            def _(dve):
                for s in (s_z, s_v, s_kvm, s_vo, s_vy):
                    dve.sem_inc(s, 1)
                dve.wait_ge(s_const, 48)
                prepare(dve, 0)
                with dve.Fori(0, NP2 - 1) as i:
                    prepare(dve, i + 1)
                    neurons(dve, i)
                neurons(dve, NP2 - 1)

            @block.gpsimd
            def _(pool):
                for s in (s_spk, s_so):
                    pool.sem_inc(s, 1)
                deviations(pool, 0)
                with pool.Fori(0, NP2 - 1) as i:
                    deviations(pool, i + 1)
                    fire(pool, i)
                fire(pool, NP2 - 1)

            @block.scalar
            def _(act):
                act.sem_inc(s_zT, 1)
                with act.Fori(0, NP2) as i:
                    for g in range(4):
                        act.wait_ge(s_tr, i * 4 + g + 1 + 1)
                        nc.scalar.activation(zT[:, g * G:(g + 1) * G, :].rearrange("p q k -> p (q k)"),
                                             ps_q[:, g // 2, g % 2, :], ACT.Copy).then_inc(s_zT, 1)

            @block.tensor
            def _(pe):
                for s in (s_tr, s_qkv, s_kv, s_o, s_y):
                    pe.sem_inc(s, 1)
                with pe.Fori(0, NP2) as i:
                    turn(pe, i)
                    project(pe, i)
                    attend(pe, i)


def experts(nc, t, sb, pb, sem, x_sb, ident, minus_half, out):
    out_view = out.rearrange("b (hp ip) w c -> (ip w) (b hp) c", ip=2)
    with ExitStack() as keep:
        uT = sb("uT", [P, NTILES * P], at=keep)
        w1 = sb("w1", [P, E, 2 * DFF], at=keep)
        w2 = sb("w2", [P, E, 2, C], at=keep)
        b1 = sb("b1", [P, E, 4], at=keep)
        b2p = sb("b2p", [3, E * C], BF16, at=keep)
        ones = sb("m_ones", [3, P], BF16, at=keep)
        gate = sb("gate", [P, NTILES, E], at=keep)
        s_load = sem("f_weights")

        with ExitStack() as a:
            wg = sb("wg", [P, E], at=a)
            bg = sb("bg", [P, G, E], at=a)
            b1r = sb("b1r", [4 * E, P], at=a)
            b2r = sb("b2r", [3, E * C], at=a)
            st = sb("f_st", [P, HP, 6], at=a)
            tmp = sb("f_tmp", [P, 4, HP], at=a)
            y = sb("f_y", [P, HP, C], at=a)
            stage = sb("f_stage", [P, 2, G * P], at=a)
            lg = sb("lg", [P, NTILES, E], at=a)
            top = sb("top", [P, 4, NTILES], at=a)
            b2h = sb("b2h", [3, 3, E * C], BF16, at=a)
            b2s = sb("b2s", [3, 2, E * C], at=a)
            wt = sb("wt", [P, 4, NTILES], at=a)
            num = sb("num", [P, NTILES, E], at=a)
            pick = sb("pick", [P, NTILES, E], at=a)
            ps_t = pb("ps_t3", [P, 2, G * P], at=a)
            ps_l = pb("ps_l3", [P, 2, 512], at=a)
            ps_b = pb("ps_b3", [P, 512], at=a)
            s_chain = sem("f_chain")
            s_var = sem("f_variance")
            s_rstd = sem("f_inverse_deviation")
            s_y = sem("f_normalised")
            s_tr = sem("f_transposed")
            s_st = sem("f_staged")
            s_lg = sem("f_logits")
            s_lgo = sem("f_logits_out")
            s_b = sem("f_bias_turned")
            s_dif = sem("f_difference")
            s_exp = sem("f_exponential")
            s_b2 = sem("f_bias_parts")
            LINKS = LN_LINKS

            with nc.Block() as block:
                @block.sync
                def _(sp):
                    sp.dma_start(wg[:, :], t["L1_ffn_Wg"]).then_inc(s_load, 16)
                    bgv = t["L1_ffn_bg"].rearrange("(a e) -> a e", a=1)
                    for g in range(G):
                        sp.dma_start(bg[:, g, :], bgv.broadcast_to([P, E])).then_inc(s_load, 16)
                    sp.dma_start(b1r[:, :], t["L1_ffn_b1"].rearrange("e (k f) -> (e k) f", f=P)).then_inc(s_load, 16)
                    sp.dma_start(b2r[:, :], t["L1_ffn_b2"].rearrange("(a e) c -> a (e c)", a=1).broadcast_to([3, E * C])).then_inc(s_load, 16)
                    sp.dma_start(num[:, :, :], t["expert_number"].rearrange("p (q e) -> p q e", e=E)).then_inc(s_load, 16)
                    sp.dma_start(w1[:, :, :], t["L1_ffn_W1"].rearrange("e c f -> c e f")).then_inc(s_load, 16)
                    sp.dma_start(w2[:, :, :, :], t["L1_ffn_W2"].rearrange("e (k f) c -> f e k c", f=P)).then_inc(s_load, 16)

                @block.vector
                def _(dve):
                    dve.wait_ge(s_load, 160)
                    dve.sem_inc(s_y, 1)
                    dve.sem_inc(s_lgo, 2)
                    nc.vector.memset(ones[:, :], 1.0)
                    with dve.Fori(0, B) as b:
                        chain = Chain(dve, s_chain, b * LINKS)
                        tile = lambda q: x_sb[:, bass.ds(b * HP + q, 1), :]
                        layer_norm_stats(nc, chain, st, tmp, tile, HP, 1e-5).then_inc(s_var, 1)
                        dve.wait_ge(s_rstd, b + 1)
                        dve.wait_ge(s_tr, b * 4 + 1)
                        for q in range(HP):
                            ins = nc.vector.tensor_scalar(y[:, q, :], tile(q), tmp[:, 0, q:q + 1], tmp[:, 3, q:q + 1],
                                                          ALU.subtract, ALU.mult)
                        ins.then_inc(s_y, 1)
                        for g in range(4):
                            n = b * 4 + g
                            dve.wait_ge(s_lg, n + 2)
                            nc.vector.tensor_tensor(lg[:, bass.ds(n * G, G), :],
                                                    ps_l[:, g % 2, 0:G * E].rearrange("p (q e) -> p q e", e=E), bg[:, :, :], ALU.add)\
                                .then_inc(s_lgo, 1)
                    chain = Chain(dve, s_chain, B * LINKS)
                    dve.wait_ge(s_lgo, NG + 2)
                    wide = lambda x: x.unsqueeze(2).broadcast_to([P, NTILES, E])

                    def largest(values, out, at):
                        chain.link(nc.vector.tensor_reduce(out, values, AXX, ALU.max))
                        chain.link(nc.vector.tensor_tensor(pick[:, :, :], values, wide(out), ALU.is_lt))
                        chain.link(nc.vector.scalar_tensor_tensor(pick[:, :, :], pick[:, :, :], float(E), num[:, :, :], ALU.mult, ALU.add))
                        chain.link(nc.vector.tensor_reduce(at, pick[:, :, :], AXX, ALU.min))
                        return nc.vector.tensor_tensor(pick[:, :, :], num[:, :, :], wide(at), ALU.is_equal)

                    chain.link(largest(lg[:, :, :], top[:, 0, :], top[:, 2, :]))
                    nc.vector.tensor_copy(gate[:, :, :], pick[:, :, :])
                    chain.link(nc.vector.scalar_tensor_tensor(lg[:, :, :], pick[:, :, :], -3e38, lg[:, :, :], ALU.mult, ALU.add))
                    chain.link(largest(lg[:, :, :], top[:, 1, :], top[:, 3, :]))
                    nc.vector.tensor_tensor(wt[:, 0, :], top[:, 1, :], top[:, 0, :], ALU.subtract).then_inc(s_dif, 1)
                    dve.wait_ge(s_exp, 1)
                    chain.link(nc.vector.tensor_scalar(wt[:, 2, :], wt[:, 1, :], 1.0, None, ALU.add))
                    chain.link(nc.vector.reciprocal(wt[:, 0, :], wt[:, 2, :]))
                    chain.link(nc.vector.tensor_tensor(wt[:, 1, :], wt[:, 1, :], wt[:, 0, :], ALU.mult))
                    chain.link(nc.vector.tensor_tensor(gate[:, :, :], gate[:, :, :], wide(wt[:, 0, :]), ALU.mult))
                    chain.link(nc.vector.tensor_tensor(pick[:, :, :], pick[:, :, :], wide(wt[:, 1, :]), ALU.mult))
                    nc.vector.tensor_tensor(gate[:, :, :], gate[:, :, :], pick[:, :, :], ALU.add)
                    dve.wait_ge(s_b, 1)
                    nc.vector.tensor_copy(b1[:, :, :].rearrange("p e k -> p (e k)"), ps_b[:, 0:4 * E])
                    chain.link(split3(nc, chain, [b2h[:, n, :] for n in range(3)], b2r[:, :], b2s[:, 0, :]))
                    chain.link(nc.vector.tensor_scalar(b2s[:, 0, :], b2h[:, 0, :], ident[0:3, 0:1], None, ALU.mult))
                    chain.link(nc.vector.scalar_tensor_tensor(b2s[:, 1, :], b2h[:, 1, :], ident[0:3, 1:2], b2s[:, 0, :], ALU.mult, ALU.add))
                    nc.vector.scalar_tensor_tensor(b2p[:, :], b2h[:, 2, :], ident[0:3, 2:3], b2s[:, 1, :], ALU.mult, ALU.add)

                @block.gpsimd
                def _(pool):
                    with pool.Fori(0, B) as b:
                        pool.wait_ge(s_var, b + 1)
                        inverse_deviation(nc, tmp, minus_half).then_inc(s_rstd, 1)

                @block.scalar
                def _(act):
                    act.sem_inc(s_st, 2)
                    with act.Fori(0, B) as b:
                        for g in range(4):
                            n = b * 4 + g
                            act.wait_ge(s_tr, n + 2)
                            nc.scalar.activation(uT[:, bass.ds(n * G * P, G * P)], ps_t[:, g % 2, :], ACT.Copy)
                            nc.scalar.activation(stage[:, g % 2, :], ps_t[:, g % 2, :], ACT.Copy).then_inc(s_st, 1)
                    act.wait_ge(s_dif, 1)
                    nc.scalar.activation(wt[:, 1, :], wt[:, 0, :], ACT.Exp).then_inc(s_exp, 1)

                @block.tensor
                def _(pe):
                    pe.wait_ge(s_load, 160)
                    pe.sem_inc(s_tr, 1)
                    pe.sem_inc(s_lg, 1)
                    nc.tensor.transpose(ps_b[:, 0:4 * E], b1r[:, :], ident[0:4 * E, 0:4 * E]).then_inc(s_b, 1)
                    with pe.Fori(0, B) as b:
                        def turn(g):
                            pe.wait_ge(s_st, b * 4 + g + 1)
                            for q in range(G):
                                ins = nc.tensor.transpose(ps_t[:, g % 2, q * P:(q + 1) * P], y[:, g * G + q, :], ident[:, :])
                            ins.then_inc(s_tr, 1)

                        def logits(g):
                            pe.wait_ge(s_st, b * 4 + g + 3)
                            pe.wait_ge(s_lgo, b * 4 + g + 1)
                            for q in range(G):
                                ins = nc.tensor.matmul(ps_l[:, g % 2, q * E:(q + 1) * E], stage[:, g % 2, q * P:(q + 1) * P],
                                                       wg[:, :], start=True, stop=True)
                            ins.then_inc(s_lg, 1)

                        pe.wait_ge(s_y, b + 2)
                        turn(0)
                        for g in range(1, 4):
                            turn(g)
                            logits(g - 1)
                        logits(3)

        with ExitStack() as a:
            sil = sb("sil", [P, 2, G * P], at=a)
            hid = sb("hid", [P, 2, 2, G * P], at=a)
            ps_h = pb("ps_h", [P, 2, 2, G * P], at=a)
            ps_y = pb("ps_y3", [P, 2, G * C], at=a)
            s_h = sem("f_hidden")
            s_sil = sem("f_silu")
            s_hid = sem("f_gated")
            s_ye = sem("f_expert_out")
            s_acc = sem("f_accumulated")
            s_out = sem("f_stored")
            UNITS = 2 * E

            with nc.Block() as block:
                @block.sync
                def _(sp):
                    with sp.Fori(0, NG) as n:
                        sp.wait_ge(s_acc, n * E + E + 2)
                        sp.dma_start(out_view[:, bass.ds(n * G, G), :], x_sb[:, bass.ds(n * G, G), :]).then_inc(s_out, 16)
                    sp.wait_ge(s_out, 16 * NG)

                @block.tensor
                def _(pe):
                    pe.sem_inc(s_ye, 1)
                    pe.sem_inc(s_h, 1)

                    def hidden(n, m):
                        e, j = m // 2, m % 2
                        pe.wait_ge(s_hid, n * UNITS + m + 1)
                        rhs = uT[:, bass.ds(n * G * P, G * P)]
                        for part in range(2):
                            f0 = part * DFF + j * P
                            ins = nc.tensor.matmul(ps_h[:, m % 2, part, :], w1[:, e, f0:f0 + P], rhs, start=True, stop=True)
                        ins.then_inc(s_h, 1)

                    def expert_out(n, e):
                        pe.wait_ge(s_hid, n * UNITS + 2 * e + 4)
                        pe.wait_ge(s_acc, n * E + e + 1)
                        for q in range(G):
                            dst = ps_y[:, e % 2, q * C:(q + 1) * C]
                            for j in range(2):
                                nc.tensor.matmul(dst, hid[:, e % 2, j, q * P:(q + 1) * P], w2[:, e, j, :],
                                                 start=(j == 0), stop=False)
                            ins = nc.tensor.matmul(dst, ones[:, :], b2p[:, e * C:(e + 1) * C], start=False, stop=True)
                        ins.then_inc(s_ye, 1)

                    with pe.Fori(0, NG) as n:
                        for m in range(UNITS):
                            hidden(n, m)
                            if m >= 2 and m % 2 == 0:
                                expert_out(n, m // 2 - 1)
                        expert_out(n, E - 1)

                @block.scalar
                def _(act):
                    act.sem_inc(s_sil, 1)
                    with act.Fori(0, NG) as n:
                        for m in range(UNITS):
                            act.wait_ge(s_h, n * UNITS + m + 2)
                            act.wait_ge(s_hid, n * UNITS + m + 1)
                            nc.scalar.activation(sil[:, m % 2, :], ps_h[:, m % 2, 0, :], ACT.Silu,
                                                 bias=b1[:, m // 2, m % 2:m % 2 + 1]).then_inc(s_sil, 1)

                @block.vector
                def _(dve):
                    dve.sem_inc(s_hid, 2)
                    dve.sem_inc(s_acc, 2)

                    def accumulate(n, e):
                        dve.wait_ge(s_ye, n * E + e + 2)
                        dve.wait_ge(s_acc, n * E + e + 2)
                        for q in range(G):
                            row = x_sb[:, bass.ds(n * G + q, 1), :].rearrange("p q c -> p (q c)")
                            ins = nc.vector.scalar_tensor_tensor(row, ps_y[:, e % 2, q * C:(q + 1) * C],
                                                                 gate[:, bass.ds(n * G + q, 1), e], row, ALU.mult, ALU.add)
                        ins.then_inc(s_acc, 1)

                    with dve.Fori(0, NG) as n:
                        for m in range(UNITS):
                            e, j = m // 2, m % 2
                            dve.wait_ge(s_sil, n * UNITS + m + 2)
                            nc.vector.scalar_tensor_tensor(hid[:, e % 2, j, :], ps_h[:, m % 2, 1, :], b1[:, e, 2 + j:3 + j],
                                                           sil[:, m % 2, :], ALU.add, ALU.mult).then_inc(s_hid, 1)
                            if m >= 2 and m % 2 == 1:
                                accumulate(n, m // 2 - 1)
                        accumulate(n, E - 1)


_CONSTANTS = spectral_tables()
_OUT = ((B, H, W, C), "float32")


def kernel(**inputs):
    import concourse.bacc as bacc
    from concourse.bass_utils import run_bass_kernel_spmd

    nc = bacc.Bacc("TRN2", target_bir_lowering=False, num_devices=1)
    arrays, tensors = {}, {}
    for name, a in {**inputs, **_CONSTANTS}.items():
        a = np.ascontiguousarray(a)
        arrays[f"in_{name}"] = a
        tensors[name] = nc.dram_tensor(f"in_{name}", a.shape, mybir.dt.from_np(a.dtype), kind="ExternalInput").ap()
    out = nc.dram_tensor("out_dram", _OUT[0], F32, kind="ExternalOutput").ap()
    build(nc, tensors, out)
    r = run_bass_kernel_spmd(nc, [arrays], core_ids=[0])
    return r.results[0]["out_dram"]
```

```python
from contextlib import ExitStack

import numpy as np

import concourse.bass as bass
from concourse import mybir

F32 = mybir.dt.float32
F32R = mybir.dt.float32r
BF16 = mybir.dt.bfloat16
I32 = mybir.dt.int32
U32 = mybir.dt.uint32
ALU = mybir.AluOpType
ACT = mybir.ActivationFunctionType
AXX = mybir.AxisListType.X

P = 128
B, H, W, C = 8, 32, 64, 128
HP = H // 2
G = 4
L, M = 64, 32
L2 = L // 2
O = 32
RB = 2 * B
MQ = 8
LQ = 4
NCH = L2 // LQ
NTILES = B * HP
E, DFF = 8, 256
EW = 2 * DFF + 2 * C
SLOT_TILES = 40
NG = NTILES // G
HEADS = 8
ATTN_SCALE = 0.125
NP2 = HP // 2
NT = 2 * B


def spectral_tables():
    nlat = W
    theta = np.pi * (np.arange(nlat) + 0.5) / nlat
    ct, st = np.cos(theta), np.sin(theta)
    p = np.zeros((L, C // 2 + 1, nlat), dtype=np.float64)
    p[0, 0] = 1.0 / np.sqrt(2.0)
    for m in range(L):
        if m > 0:
            p[m, m] = np.sqrt((2.0 * m + 1.0) / (2.0 * m)) * st * p[m - 1, m - 1]
        if m + 1 < L:
            p[m + 1, m] = np.sqrt(2.0 * m + 3.0) * ct * p[m, m]
        for l in range(m + 2, L):
            a = np.sqrt((4.0 * l * l - 1.0) / (l * l - m * m))
            b = np.sqrt((2.0 * l + 1.0) * (l - 1 - m) * (l - 1 + m) / ((2.0 * l - 3.0) * (l * l - m * m)))
            p[l, m] = a * ct * p[l - 1, m] - b * p[l - 2, m]
    weight = (st * np.pi / nlat).astype(np.float32)
    syn = p[:, :M].astype(np.float32)
    ana = syn * weight[None, None, :]
    ana_bd = np.zeros((P, M, P), np.float32)
    syn_bd = np.zeros((P, M, P), np.float32)
    for i in range(2):
        s = slice(i * 64, i * 64 + 64)
        ana_bd[s, :, s] = ana.transpose(2, 1, 0)
        syn_bd[s, :, s] = syn.transpose(0, 1, 2)
    n = np.arange(C)[:, None] * np.arange(M)[None, :] * (2 * np.pi / C)
    fwd = np.concatenate([np.cos(n), -np.sin(n)], 1) * (np.sqrt(2 * np.pi) / C)
    twice = np.where(np.arange(M) == 0, 1.0, 2.0)[None, :]
    inv = np.concatenate([np.cos(n) * twice, -np.sin(n) * twice], 1) / np.sqrt(2 * np.pi)
    inv[:, M] = 0.0
    inv_bd = np.zeros((P, 2 * C), np.float32)
    inv_bd[:64, :C] = inv_bd[64:, C:] = inv.T
    return {
        "identity": np.eye(P, dtype=np.float32),
        "first_rank": np.tile(16.0 - np.arange(16), (P, NT)).astype(np.float32),
        "expert_number": np.tile(np.arange(E), (P, HP)).astype(np.float32),
        "expert_up_to": np.tile(np.tril(np.ones((E, E))).reshape(-1), (P, 1)).astype(np.float32),
        "slot_tile_number": np.tile(np.repeat(np.arange(SLOT_TILES), E), (P, 1)).astype(np.float32),
        "window_first_slot": np.tile(np.arange(B) * SLOT_TILES * P, (P, 1)).astype(np.float32),
        "token_before": np.triu(np.ones((P, P)), 1).astype(np.float32),
        "nibble_key": np.tile(np.arange(16) - 16.0, (P, NT)).astype(np.float32),
        "head_mask": np.tile(np.kron(np.eye(HEADS), np.full((C // HEADS,) * 2, ATTN_SCALE / 2)), (1, G)).astype(np.float32),
        "legendre_analysis": ana_bd.reshape(P, M * P),
        "legendre_synthesis": syn_bd.reshape(P, M * P),
        "fourier_forward": fwd.astype(np.float32),
        "fourier_inverse": inv_bd,
    }


def build(nc, t, out):
    with ExitStack() as ctx:
        def sb(name, shape, dt=F32, at=ctx):
            return at.enter_context(nc.sbuf_tensor(name, shape, dt))

        def pb(name, shape, dt=F32, at=ctx):
            return at.enter_context(nc.psum_tensor(name, shape, dt))

        def sem(name):
            return ctx.enter_context(nc.semaphore(name))

        x_sb = sb("x_sb", [P, B * HP, C])
        ident = sb("ident", [P, P])
        minus_half = sb("minus_half", [P, 2 * HP])
        x_view = t["x"].rearrange("b (hp ip) w c -> b (ip w) hp c", ip=2)

        slots = nc.dram_tensor("slots", [B * SLOT_TILES * P, C], F32, kind="Internal").ap()
        spectral_conv(nc, t, sb, pb, sem, x_sb, ident, minus_half, x_view)
        with ExitStack() as a:
            weights = spiking_weights(nc, t, sb, pb, sem, ident, minus_half, a)
            opcode_and_spikes(nc, t, sb, pb, sem, x_sb, ident, minus_half, weights, slots)
        experts(nc, t, sb, pb, sem, x_sb, ident, minus_half, slots, out)


class Chain:

    def __init__(self, eng, s, base=0):
        self.eng, self.s, self.n, self.base = eng, s, 0, base

    def link(self, ins):
        self.n += 1
        ins.then_inc(self.s, 1)
        self.eng.wait_ge(self.s, self.base + self.n)


def moments(nc, chain, st, tmp, eps):
    nc.vector.tensor_tensor(tmp[:, 0, :], st[:, :, 1], st[:, :, 4], ALU.add)
    nc.vector.tensor_tensor(tmp[:, 2, :], st[:, :, 2], st[:, :, 5], ALU.add)
    chain.link(nc.vector.tensor_tensor(tmp[:, 1, :], st[:, :, 1], st[:, :, 4], ALU.subtract))
    nc.vector.tensor_scalar(tmp[:, 0, :], tmp[:, 0, :], 0.5, None, ALU.mult)
    chain.link(nc.vector.scalar_tensor_tensor(tmp[:, 1, :], tmp[:, 1, :], 0.25, tmp[:, 1, :], ALU.mult, ALU.mult))
    chain.link(nc.vector.scalar_tensor_tensor(tmp[:, 2, :], tmp[:, 2, :], 1.0 / C, tmp[:, 1, :], ALU.mult, ALU.add))
    return nc.vector.tensor_scalar(tmp[:, 2, :], tmp[:, 2, :], eps, None, ALU.add)


def layer_norm_stats(nc, chain, st, tmp, src, n, eps):
    for q in range(n):
        ins = nc.vector.bn_stats(st[:, q, :], src(q))
    chain.link(ins)
    return moments(nc, chain, st, tmp, eps)


LN_LINKS = 4


def inverse_deviation(nc, tmp, minus_half):
    return nc.gpsimd.tensor_tensor(tmp[:, 3, :], tmp[:, 2, :], minus_half[:, 0:tmp.shape[2]], ALU.pow)


def spectral_conv(nc, t, sb, pb, sem, x_sb, ident, minus_half, x_view):
    spectral_w = [t["L0_conv_w1r"], t["L0_conv_w1i"], t["L0_conv_w2r"], t["L0_conv_w2i"]]
    coef = nc.dram_tensor("coefficients", [2, M // MQ, H, L, MQ * RB], F32, kind="Internal").ap()
    mixed = nc.dram_tensor("mixed", [NCH, 2, P, M * 16], F32, kind="Internal").ap()

    with ExitStack() as both:
        wc = sb("wc", [P, 2, O, LQ, M], at=both)
        s_w = [sem("mix_weights_0"), sem("mix_weights_1")]
        w_view = [w.rearrange("i o (k l) m -> k i o (l m)", l=LQ) for w in spectral_w]

        def load_w(eng, chunk, slot):
            for g in range(4):
                src = w_view[g][bass.ds(chunk, 1)] if not isinstance(chunk, int) else w_view[g][chunk:chunk + 1]
                eng.dma_start(wc[32 * g:32 * g + 32, slot].rearrange("i o l m -> i o (l m)"),
                              src.rearrange("k i o f -> (k i) o f")).then_inc(s_w[slot], 16)

        with ExitStack() as a:
            efwd = sb("efwd", [P, 2 * M], at=a)
            pana = sb("pana", [P, M, P], at=a)
            y = sb("y", [P, 2, HP, C], at=a)
            yT = sb("yT", [P, 2, G * P], at=a)
            f_sb = sb("f_sb", [P, M, HP, 2, B], at=a)
            c1 = sb("c1", [P, 2, HP, MQ, RB], at=a)
            c2 = sb("c2", [P, 2, HP, MQ, RB], at=a)
            st = sb("st", [P, 2, HP, 6], at=a)
            tmp = sb("tmp", [P, 2, 4, HP], at=a)
            ps_t = pb("ps_t", [P, 2, G * P], at=a)
            ps_f = pb("ps_f", [P, 2, 2 * G, 2 * M], at=a)
            ps_l = pb("ps_l", [P, 2, 2, 256], at=a)

            s_const = sem("a_constants")
            s_x = [sem("x_loaded_0"), sem("x_loaded_1")]
            s_chain = sem("a_vector_chain")
            s_half = sem("a_exponent")
            s_var = sem("a_variance")
            s_rstd = sem("a_inverse_deviation")
            s_y = sem("a_normalised")
            s_tr = sem("a_transposed")
            s_yT = sem("a_channel_major")
            s_dft = sem("a_fourier")
            s_dftfree = sem("a_fourier_bank_free")
            s_leg = sem("a_legendre")
            s_c1 = sem("a_coefficients")
            s_c2 = sem("a_rotated_coefficients")
            s_cw = [sem("coefficients_stored_0"), sem("coefficients_stored_1")]

            with nc.Block() as block:
                @block.sync
                def _(sp):
                    sp.dma_start(ident[:, :], t["identity"]).then_inc(s_const, 16)
                    sp.dma_start(efwd[:, :], t["fourier_forward"]).then_inc(s_const, 16)
                    for b in range(B):
                        if b >= 2:
                            sp.wait_ge(s_x[b % 2], 16 * (b // 2))
                        sp.dma_start(x_sb[:, b * HP:(b + 1) * HP, :], x_view[b]).then_inc(s_x[b % 2], 16)
                    sp.dma_start(pana[:, :, :], t["legendre_analysis"].rearrange("p (m q) -> p m q", m=M)).then_inc(s_const, 16)
                    load_w(sp, 0, 0)
                    load_w(sp, 1, 1)
                    for mq in range(M // MQ):
                        for v, (c, s) in enumerate(((c1, s_c1), (c2, s_c2))):
                            sp.wait_ge(s, (mq + 1) * (MQ // 2 if v == 0 else 1))
                            sp.dma_start(coef[v, mq].rearrange("(ih ip) l f -> (ip l) ih f", ip=2),
                                         c[:, mq % 2].rearrange("p ih m f -> p ih (m f)")).then_inc(s_cw[mq % 2], 16)
                    for k in range(2):
                        sp.wait_ge(s_cw[k], 64)

                @block.vector
                def _(dve):
                    with dve.Fori(0, B // 2) as pair:
                        for k in range(2):
                            dve.wait_ge(s_x[k], pair * 16 + 16)
                            chain = Chain(dve, s_chain, (pair * 2 + k) * LN_LINKS)
                            tile0 = (pair * 2 + k) * HP
                            layer_norm_stats(nc, chain, st[:, k], tmp[:, k],
                                             lambda q: x_sb[:, bass.ds(tile0 + q, 1), :], HP, 1e-6).then_inc(s_var, 1)
                            dve.wait_ge(s_rstd, pair * 2 + k + 1)
                            dve.wait_ge(s_tr, (pair * 2 + k) * G + 1)
                            for q in range(HP):
                                ins = nc.vector.tensor_scalar(y[:, k, q, :], x_sb[:, bass.ds(tile0 + q, 1), :],
                                                              tmp[:, k, 0, q:q + 1], tmp[:, k, 3, q:q + 1],
                                                              ALU.subtract, ALU.mult)
                            ins.then_inc(s_y, 1)
                    for mq in range(M // MQ):
                        k = mq % 2
                        dve.wait_ge(s_c1, (mq + 1) * (MQ // 2))
                        if mq >= 2:
                            dve.wait_ge(s_cw[k], 32)
                        a1 = c1[:, k].rearrange("p ih m f -> p (ih m) f")
                        a2 = c2[:, k].rearrange("p ih m f -> p (ih m) f")
                        nc.vector.tensor_scalar(a2[:, :, 0:B], a1[:, :, B:RB], -1.0, None, ALU.mult)
                        nc.vector.tensor_copy(a2[:, :, B:RB], a1[:, :, 0:B]).then_inc(s_c2, 1)

                @block.gpsimd
                def _(pool):
                    nc.gpsimd.memset(minus_half[:, :], -0.5).then_inc(s_half, 1)
                    pool.wait_ge(s_half, 1)
                    with pool.Fori(0, B // 2) as pair:
                        for k in range(2):
                            pool.wait_ge(s_var, pair * 2 + k + 1)
                            inverse_deviation(nc, tmp[:, k], minus_half).then_inc(s_rstd, 1)

                @block.tensor
                def _(pe):
                    pe.sem_inc(s_tr, G + 1)
                    pe.sem_inc(s_dft, 2)
                    pe.wait_ge(s_const, 48)
                    with pe.Fori(0, B // 2) as pair:
                        for k in range(2):
                            g0 = (pair * 2 + k) * G

                            def transposes(g):
                                pe.wait_ge(s_yT, g0 + g + 1)
                                for q in range(G):
                                    ins = nc.tensor.transpose(ps_t[:, g % 2, q * P:(q + 1) * P],
                                                              y[:, k, g * G + q, :], ident[:, :])
                                ins.then_inc(s_tr, 1)

                            def fourier(g):
                                pe.wait_ge(s_yT, g0 + g + 3)
                                if g % 2 == 0:
                                    pe.wait_ge(s_dftfree, (pair * 2 + k) * 2 + g // 2 + 1)
                                for q in range(G):
                                    ins = nc.tensor.matmul(ps_f[:, g // 2, (g % 2) * G + q, :],
                                                           yT[:, g % 2, q * P:(q + 1) * P], efwd[:, :],
                                                           start=True, stop=True)
                                ins.then_inc(s_dft, 1)

                            pe.wait_ge(s_y, pair * 2 + k + 1)
                            for g in range(HP // G):
                                transposes(g)
                                if g:
                                    fourier(g - 1)
                            fourier(HP // G - 1)
                    pe.wait_ge(s_dftfree, 2 * B + 2)
                    for m in range(M):
                        if m % 2 == 0 and m >= 4:
                            pe.wait_ge(s_c1, m // 2 - 1)
                        ins = nc.tensor.matmul(ps_l[:, (m // 2) % 2, m % 2, :], pana[:, m, :],
                                               f_sb[:, m].rearrange("p h r b -> p (h r b)"), start=True, stop=True)
                        if m % 2:
                            ins.then_inc(s_leg, 1)

                @block.scalar
                def _(act):
                    act.sem_inc(s_yT, 2)
                    act.sem_inc(s_dftfree, 2)
                    with act.Fori(0, B // 2) as pair:
                        for k in range(2):
                            bb = pair * 2 + k
                            for g in range(HP // G):
                                act.wait_ge(s_tr, bb * G + g + 2 + G)
                                act.wait_ge(s_dft, bb * G + g + 1)
                                nc.scalar.activation(yT[:, g % 2, :], ps_t[:, g % 2, :], ACT.Copy)\
                                    .then_inc(s_yT, 1)
                                if g % 2:
                                    act.wait_ge(s_dft, bb * G + g + 3)
                                    q0 = (g - 1) * G
                                    nc.scalar.activation(
                                        f_sb[:, :, q0:q0 + 2 * G, :, bb].rearrange("p m q r -> p q r m"),
                                        ps_f[:, g // 2].rearrange("p q (r m) -> p q r m", r=2), ACT.Copy)\
                                        .then_inc(s_dftfree, 1)

                    for m2 in range(M // 2):
                        k = (2 * m2 // MQ) % 2
                        act.wait_ge(s_leg, m2 + 1)
                        if 2 * m2 % MQ == 0 and 2 * m2 >= 2 * MQ:
                            act.wait_ge(s_cw[k], 32)
                        ml = 2 * m2 % MQ
                        nc.scalar.activation(c1[:, k, :, ml:ml + 2, :].rearrange("p ih m f -> p m ih f"),
                                             ps_l[:, m2 % 2].rearrange("p m (ih f) -> p m ih f", ih=HP), ACT.Copy)\
                            .then_inc(s_c1, 1)

        with ExitStack() as a:
            coefc = sb("coefc", [P, 2, M // MQ, LQ, MQ, RB], at=a)
            sblk = sb("sblk", [P, 2, LQ, M, 2 * RB], at=a)
            mo = sb("mo", [P, 2, 2, M, 16], at=a)
            ps_m = pb("ps_m", [P, 2, 2, 512], at=a)
            s_cc = [sem("coefficients_loaded_0"), sem("coefficients_loaded_1")]
            s_zero = sem("m_blocks_zeroed")
            s_sd = sem("m_lower_blocks")
            s_sa = sem("m_upper_blocks")
            s_mm = sem("m_mixed")
            s_ed = sem("m_first_orders_out")
            s_ea = sem("m_last_orders_out")
            s_mw = [sem("mixed_stored_0"), sem("mixed_stored_1")]

            def load_coef(eng, chunk, slot):
                for g in range(4):
                    half, part = g // 2, g % 2
                    base = coef[part].rearrange("q i l f -> i q (l f)")
                    off = (half * L2 + chunk * LQ) * MQ * RB
                    eng.dma_start(coefc[32 * g:32 * g + 32, slot].rearrange("i q l m f -> i q (l m f)"),
                                  base[:, :, bass.ds(off, LQ * MQ * RB)]).then_inc(s_cc[slot], 16)

            def store_mixed(eng, chunk, slot):
                eng.wait_ge(s_ed, chunk + 3)
                eng.wait_ge(s_ea, chunk + 3)
                eng.dma_start(mixed[bass.ds(chunk, 1)].rearrange("k op p f -> p (k op) f"),
                              mo[:, slot].rearrange("p op m o -> p op (m o)")).then_inc(s_mw[slot], 16)

            with nc.Block() as block:
                @block.sync
                def _(sp):
                    for k in range(2):
                        sp.sem_inc(s_mw[k], 1)
                    load_coef(sp, 0, 0)
                    load_coef(sp, 1, 1)
                    with sp.Fori(1, NCH // 2) as pair:
                        for k in range(2):
                            n = pair * 2 + k
                            sp.wait_ge(s_mm, n + 1)
                            load_w(sp, n, k)
                            sp.wait_ge(s_sd, n - 1)
                            sp.wait_ge(s_sa, n - 1)
                            load_coef(sp, n, k)
                            store_mixed(sp, n - 2, k)
                    for k in range(2):
                        store_mixed(sp, NCH - 2 + k, k)
                    for k in range(2):
                        sp.wait_ge(s_mw[k], 16 * NCH // 2 + 1)

                @block.gpsimd
                def _(pool):
                    nc.gpsimd.memset(sblk[:, 0], 0.0).then_inc(s_zero, 1)
                    nc.gpsimd.memset(sblk[:, 1], 0.0).then_inc(s_zero, 1)

                @block.vector
                def _(dve):
                    dve.sem_inc(s_ed, 2)
                    dve.wait_ge(s_zero, 2)

                    with dve.Fori(0, NCH // 2) as pair:
                        for k in range(2):
                            n = pair * 2 + k
                            dve.wait_ge(s_cc[k], pair * 64 + 64)
                            dve.wait_ge(s_mm, n + 1)
                            for l in range(LQ):
                                ins = nc.vector.tensor_copy(
                                    sblk[0:64, k, l, :, 0:RB].rearrange("p (q m) f -> p q m f", q=M // MQ),
                                    coefc[0:64, k, :, l])
                            ins.then_inc(s_sd, 1)
                            dve.wait_ge(s_mm, n + 3)
                            dve.wait_ge(s_mw[k], pair * 16 + 1)
                            nc.vector.tensor_copy(
                                mo[:, k, :, 0:M // 2, :],
                                ps_m[:, k, 0, :].rearrange("p (m o op) -> p op m o", op=2, o=16))\
                                .then_inc(s_ed, 1)

                @block.scalar
                def _(act):
                    act.sem_inc(s_ea, 2)
                    act.wait_ge(s_zero, 2)
                    with act.Fori(0, NCH // 2) as pair:
                        for k in range(2):
                            n = pair * 2 + k
                            act.wait_ge(s_cc[k], pair * 64 + 64)
                            act.wait_ge(s_mm, n + 1)
                            for l in range(LQ):
                                ins = nc.scalar.activation(
                                    sblk[64:128, k, l, :, RB:2 * RB].rearrange("p (q m) f -> p q m f", q=M // MQ),
                                    coefc[64:128, k, :, l], ACT.Copy)
                            ins.then_inc(s_sa, 1)
                            act.wait_ge(s_mm, n + 3)
                            act.wait_ge(s_mw[k], pair * 16 + 1)
                            nc.scalar.activation(
                                mo[:, k, :, M // 2:M, :],
                                ps_m[:, k, 1, :].rearrange("p (m o op) -> p op m o", op=2, o=16), ACT.Copy)\
                                .then_inc(s_ea, 1)

                @block.tensor
                def _(pe):
                    pe.sem_inc(s_mm, 2)
                    with pe.Fori(0, NCH // 2) as pair:
                        for k in range(2):
                            n = pair * 2 + k
                            pe.wait_ge(s_w[k], pair * 64 + 64)
                            pe.wait_ge(s_sd, n + 1)
                            pe.wait_ge(s_sa, n + 1)
                            pe.wait_ge(s_ed, n + 1)
                            pe.wait_ge(s_ea, n + 1)
                            for l in range(LQ):
                                for m in range(M):
                                    half, col = m // (M // 2), (m % (M // 2)) * O
                                    ins = nc.tensor.matmul(ps_m[32 * l:32 * l + 32, k, half, col:col + O],
                                                           sblk[:, k, l, m, :], wc[:, k, :, l, m],
                                                           start=True, stop=True)
                            ins.then_inc(s_mm, 1)

    with ExitStack() as a:
        psyn = sb("psyn", [P, M, P], at=a)
        einv = sb("einv", [P, 2 * C], at=a)
        gin = sb("gin", [P, M // MQ, RB, MQ, 16], at=a)
        h_sb = sb("h_sb", [P, B, HP, 2, M], at=a)
        hc = sb("hc", [P, 2, HP, 2, M], at=a)
        hT = sb("hT", [P, 2, G * P], at=a)
        ps_g = pb("ps_g", [P, 2, 2, 256], at=a)
        ps_t = pb("ps_t2", [P, 2, G * P], at=a)
        ps_y = pb("ps_y", [P, 2, G, 2 * C], at=a)
        s_const = sem("c_constants")
        s_gin = [sem(f"mixed_loaded_{q}") for q in range(M // MQ)]
        s_leg = sem("c_legendre")
        s_h = [sem("c_orders_even"), sem("c_orders_odd")]
        s_hc = sem("c_batch_copied")
        s_tr = sem("c_transposed")
        s_hT = sem("c_orders_major")
        s_y = sem("c_grid")
        s_yfree = sem("c_grid_bank_free")

        def evacuate(copy, m2):
            return copy(h_sb[:, :, :, :, 2 * m2:2 * m2 + 2].rearrange("p b h r m -> p m r (b h)"),
                        ps_g[:, m2 % 2].rearrange("p m (r bh) -> p m r bh", r=2))

        with nc.Block() as block:
            @block.sync
            def _(sp):
                sp.dma_start(psyn[:, :, :], t["legendre_synthesis"].rearrange("p (m q) -> p m q", m=M)).then_inc(s_const, 16)
                sp.dma_start(einv[:, :], t["fourier_inverse"]).then_inc(s_const, 16)
                for q in range(M // MQ):
                    for op in range(2):
                        for half in range(2):
                            src = mixed[:, op].rearrange("k (l h r) (q f) -> h q k l r f", l=LQ, h=2, q=M // MQ)[half, q]
                            p0 = op * 64 + half * L2
                            for k in range(NCH):
                                sp.dma_start(gin[p0 + k * LQ:p0 + k * LQ + LQ, q].rearrange("p r m o -> p r (m o)"), src[k])\
                                    .then_inc(s_gin[q], 16)

            @block.tensor
            def _(pe):
                pe.sem_inc(s_tr, 3)
                pe.sem_inc(s_y, 2)
                pe.wait_ge(s_const, 32)
                for m in range(M):
                    if m % MQ == 0:
                        pe.wait_ge(s_gin[m // MQ], 16 * 4 * NCH)
                    if m % 2 == 0 and m >= 4:
                        pe.wait_ge(s_h[(m // 2) % 2], m // 4)
                    ins = nc.tensor.matmul(ps_g[:, (m // 2) % 2, m % 2, :], psyn[:, m, :],
                                           gin[:, m // MQ, :, m % MQ, :], start=True, stop=True)
                    if m % 2:
                        ins.then_inc(s_leg, 1)

                with pe.Fori(0, B // 2) as pair:
                    for k in range(2):
                        b = pair * 2 + k

                        def transposes(g):
                            pe.wait_ge(s_hT, b * 2 + g + 1)
                            for q in range(G):
                                t0 = (g * G + q) * 2
                                ins = nc.tensor.transpose(ps_t[:, g % 2, q * P:(q + 1) * P],
                                                          hc[:, k, t0:t0 + 2].rearrange("p q r m -> p (q r m)"), ident[:, :])
                            ins.then_inc(s_tr, 1)

                        def grid(g):
                            pe.wait_ge(s_hT, b * 2 + g + 3)
                            pe.wait_ge(s_yfree, b * 2 + g + 1)
                            for q in range(G):
                                ins = nc.tensor.matmul(ps_y[:, g, q], hT[:, g, q * P:(q + 1) * P], einv[:, :],
                                                       start=True, stop=True)
                            ins.then_inc(s_y, 1)

                        pe.wait_ge(s_hc, b + 1)
                        transposes(0)
                        transposes(1)
                        grid(0)
                        grid(1)

            @block.scalar
            def _(act):
                act.sem_inc(s_hT, 2)
                for m2 in range(0, M // 2, 2):
                    act.wait_ge(s_leg, m2 + 1)
                    evacuate(lambda o, i: nc.scalar.activation(o, i, ACT.Copy), m2).then_inc(s_h[0], 1)
                with act.Fori(0, B // 2) as pair:
                    for k in range(2):
                        for g in range(2):
                            n = (pair * 2 + k) * 2 + g
                            act.wait_ge(s_tr, n + 4)
                            act.wait_ge(s_y, n + 1)
                            nc.scalar.activation(hT[:, g % 2, :], ps_t[:, g % 2, :], ACT.Copy)\
                                .then_inc(s_hT, 1)

            @block.gpsimd
            def _(pool):
                pool.wait_ge(s_h[0], M // 4)
                pool.wait_ge(s_h[1], M // 4)
                with pool.Fori(0, B // 2) as pair:
                    for k in range(2):
                        b = pair * 2 + k
                        pool.wait_ge(s_tr, b * 2 + 1)
                        nc.gpsimd.tensor_copy(hc[:, k], h_sb[:, b]).then_inc(s_hc, 1)

            @block.vector
            def _(dve):
                dve.sem_inc(s_yfree, 2)
                for m2 in range(1, M // 2, 2):
                    dve.wait_ge(s_leg, m2 + 1)
                    evacuate(nc.vector.tensor_copy, m2).then_inc(s_h[1], 1)
                with dve.Fori(0, B // 2) as pair:
                    for k in range(2):
                        for g in range(2):
                            n = (pair * 2 + k) * 2 + g
                            dve.wait_ge(s_y, n + 3)
                            for bank in range(2):
                                rows = x_sb[:, bass.ds(n * 2 * G + bank * G, G), :].rearrange("p q c -> p (q c)")
                                ins = nc.vector.tensor_tensor(
                                    rows, rows, ps_y[:, g, bank * 2:bank * 2 + 2].rearrange("p q c -> p (q c)"), ALU.add)
                            ins.then_inc(s_yfree, 1)


def split3(nc, chain, parts, x, rest):
    chain.link(nc.vector.tensor_copy(parts[0], x))
    chain.link(nc.vector.tensor_tensor(rest, x, parts[0], ALU.subtract))
    chain.link(nc.vector.tensor_copy(parts[1], rest))
    return nc.vector.tensor_tensor(parts[2], rest, parts[1], ALU.subtract)


def spiking_weights(nc, t, sb, pb, sem, ident, minus_half, keep):
    wqkv = sb("wqkv", [P, 3 * C], at=keep)
    wo = sb("wo", [P, 3, C], BF16, at=keep)
    bias = sb("bias", [3, 4 * C], BF16, at=keep)
    ones = sb("ones", [3, P], BF16, at=keep)
    with ExitStack() as a:
        lw = sb("lw", [P, 4, C], at=a)
        par = sb("par", [P, 5, 4], at=a)
        col = sb("col", [P, 3, 4], at=a)
        bpart = sb("bpart", [P, 4, 3], at=a)
        bhalf = sb("bhalf", [P, 3, 4], BF16, at=a)
        rest = sb("rest", [P, C], at=a)
        rest4 = sb("rest4", [P, 4], at=a)
        ps_w = pb("ps_w", [P, 4 * C], at=a)
        ps_b = pb("ps_b", [3, 4 * C], at=a)
        s_load = sem("w_loaded")
        s_chain = sem("w_chain")
        s_var = sem("w_variance")
        s_rstd = sem("w_inverse_deviation")
        s_scaled = sem("w_scaled")
        s_t = sem("w_transposed")

        with nc.Block() as block:
            @block.sync
            def _(sp):
                sp.dma_start(lw[:, :, :], t["L1_conv_lin_w"].rearrange("i d c -> d i c")).then_inc(s_load, 16)
                for n, name in enumerate(("lin_b", "bn_g", "bn_b", "bn_m", "bn_v")):
                    with nc.allow_non_contiguous_dma(reason="512 parameters, once"):
                        sp.dma_start(par[:, n, :], t[f"L1_conv_{name}"].rearrange("i d -> d i")).then_inc(s_load, 16)

            @block.gpsimd
            def _(pool):
                pool.wait_ge(s_var, 1)
                nc.gpsimd.tensor_tensor(col[:, 0, :], col[:, 0, :], minus_half[:, 0:4], ALU.pow).then_inc(s_rstd, 1)

            @block.vector
            def _(dve):
                chain = Chain(dve, s_chain)
                dve.wait_ge(s_load, 96)
                nc.vector.memset(ones[:, :], 1.0)
                nc.vector.tensor_scalar(col[:, 0, :], par[:, 4, :], 1e-5, None, ALU.add).then_inc(s_var, 1)
                dve.wait_ge(s_rstd, 1)
                nc.vector.tensor_tensor(col[:, 1, :], par[:, 1, :], col[:, 0, :], ALU.mult)
                chain.link(nc.vector.tensor_tensor(col[:, 2, :], par[:, 0, :], par[:, 3, :], ALU.subtract))
                chain.link(nc.vector.tensor_tensor(col[:, 2, :], col[:, 2, :], col[:, 1, :], ALU.mult))
                chain.link(nc.vector.tensor_tensor(col[:, 2, :], col[:, 2, :], par[:, 2, :], ALU.add))
                chain.link(nc.vector.tensor_scalar(col[:, 2, :], col[:, 2, :], 0.5, None, ALU.mult))
                for i in range(4):
                    ins = nc.vector.tensor_scalar(lw[:, i, :], lw[:, i, :], col[:, 1, i:i + 1], 0.5, ALU.mult, ALU.mult)
                chain.link(ins)
                chain.link(split3(nc, chain, [bhalf[:, n, :] for n in range(3)], col[:, 2, :], rest4[:, :]))
                nc.vector.tensor_copy(bpart[:, :, :].rearrange("p i n -> p n i"), bhalf[:, :, :]).then_inc(s_scaled, 1)
                dve.wait_ge(s_t, 1)
                nc.vector.tensor_copy(wqkv[:, :], ps_w[:, 0:3 * C])
                nc.vector.tensor_copy(bias[:, :], ps_b[:, :])
                split3(nc, chain, [wo[:, n, :] for n in range(3)], ps_w[:, 3 * C:4 * C], rest[:, :])

            @block.tensor
            def _(pe):
                pe.wait_ge(s_scaled, 1)
                for i in range(4):
                    nc.tensor.transpose(ps_w[:, i * C:(i + 1) * C], lw[:, i, :], ident[:, :])
                for i in range(4):
                    ins = nc.tensor.transpose(ps_b[:, i * C:(i + 1) * C], bpart[:, i, :], ident[:, :])
                ins.then_inc(s_t, 1)
    return wqkv, wo, bias, ones


def opcode_and_spikes(nc, t, sb, pb, sem, x_sb, ident, minus_half, weights, slots):
    wqkv, wo, bias, ones = weights
    xv = x_sb[:, :, :].rearrange("p (b i j) c -> p b i j c", b=B, j=2)
    with ExitStack() as a:
        rank = sb("rank", [P, NT, 16], at=a)
        key = sb("key", [P, NT, 16], at=a)
        mask = sb("mask", [P, G * C], at=a)
        st = sb("e_st", [P, NT, 6], at=a)
        tmp = sb("e_tmp", [P, 2, 4, NT], at=a)
        u = sb("u", [P, NT, C], at=a)
        win = sb("win", [P, 3, NT, 16], at=a)
        first = sb("first", [P, 3, NT], at=a)
        fl = sb("fl", [P, 4, NT], at=a)
        ints = sb("ints", [P, 10, NT], I32, at=a)
        flt = sb("flt", [P, 4, NT], at=a)
        eq = sb("eq", [P, 2, NT, 16], at=a)
        z = sb("z", [P, NT, C], at=a)
        zT = sb("zT", [P, NT, P], at=a)
        v1 = sb("v1", [P, 2, 2, 3 * C], at=a)
        r1 = sb("r1", [P, 2, 3 * C], at=a)
        spk = sb("spk", [P, B, 2, 3 * C], BF16, at=a)
        kvm = sb("kvm", [P, 2, 2, G * C], BF16, at=a)
        vo = sb("vo", [P, 2, 2 * P], at=a)
        ro = sb("ro", [P, 2 * P], at=a)
        so = sb("so", [P, 2, 2 * P], BF16, at=a)
        vy = sb("vy", [P, 2, C], at=a)
        ry = sb("ry", [P, 2, C], at=a)
        ps_q = pb("ps_q", [P, 2, 2, 512], at=a)
        ps_kv = pb("ps_kv", [P, 2, G * C], at=a)
        ps_o = pb("ps_o", [P, 512], at=a)
        ps_y = pb("ps_y2", [P, 512], at=a)

        zero = sb("zero", [P, C], at=a)
        s_zero = sem("e_zero")
        s_clear = sem("slots_cleared")
        s_const = sem("e_constants")
        s_chain = sem("e_chain")
        s_var = sem("e_variance")
        s_rstd = sem("e_inverse_deviation")
        s_beat = sem("e_beat")
        s_z = sem("e_normalised")
        s_tr = sem("e_transposed")
        s_zT = sem("e_channel_major")
        s_qkv = sem("e_projected")
        s_v = sem("e_membranes")
        s_spk = sem("e_spikes")
        s_kv = sem("e_key_values")
        s_kvm = sem("e_key_values_masked")
        s_o = sem("e_attended")
        s_vo = sem("e_attended_membranes")
        s_so = sem("e_attended_spikes")
        s_y = sem("e_output_projected")
        s_vy = sem("e_output_membranes")

        PREP_LINKS = 2 * LN_LINKS + 17

        def prepare(dve, i):
            chain = Chain(dve, s_chain, i * PREP_LINKS)
            tile = lambda q: xv[:, q // 2, i, q % 2, :]
            layer_norm_stats(nc, chain, st, tmp[:, 0], tile, NT, 1e-5).then_inc(s_var, 1)
            dve.wait_ge(s_rstd, i * 2 + 1)
            for q in range(NT):
                ins = nc.vector.tensor_scalar(u[:, q, :], tile(q), tmp[:, 0, 0, q:q + 1], tmp[:, 0, 3, q:q + 1],
                                              ALU.subtract, ALU.mult)
            chain.link(ins)
            nc.vector.tensor_scalar(fl[:, 0, :], u[:, :, 0], 0.5, None, ALU.is_gt)
            for n, lo in enumerate((16, 20, 24)):
                ins = nc.vector.scalar_tensor_tensor(win[:, n], u[:, :, lo:lo + 16], 0.5, rank[:, :, :], ALU.is_gt, ALU.mult)
            chain.link(ins)
            nc.vector.tensor_reduce(first[:, :, :], win[:, :, :, :], AXX, ALU.max)
            nc.vector.scalar_tensor_tensor(fl[:, 1, :], u[:, :, 39], 0.5, fl[:, 0, :], ALU.is_gt, ALU.mult)
            chain.link(nc.vector.scalar_tensor_tensor(fl[:, 2, :], u[:, :, 39], 0.5, fl[:, 0, :], ALU.is_le, ALU.mult))
            chain.link(nc.vector.scalar_tensor_tensor(fl[:, 2, :], u[:, :, 40], 0.5, fl[:, 2, :], ALU.is_gt, ALU.mult))
            chain.link(nc.vector.tensor_scalar(ints[:, 0:3, :], first[:, :, :], -1.0, 16.0, ALU.mult, ALU.add))
            nc.vector.tensor_tensor(fl[:, 3, :], fl[:, 1, :], fl[:, 2, :], ALU.add)
            chain.link(nc.vector.tensor_scalar(ints[:, 0:3, :], ints[:, 0:3, :], 15, None, ALU.bitwise_and))
            lo, hi, sa, val, shl, shr, res, rlo, rhi = (ints[:, n, :] for n in range(9))
            chain.link(nc.vector.scalar_tensor_tensor(val, hi, 4, lo, ALU.logical_shift_left, ALU.bitwise_or))
            nc.vector.tensor_tensor(shr, val, sa, ALU.logical_shift_right)
            chain.link(nc.vector.tensor_tensor(shl, val, sa, ALU.logical_shift_left))
            chain.link(nc.vector.tensor_scalar(shl, shl, 255, None, ALU.bitwise_and))
            nc.vector.tensor_tensor(flt[:, 0, :], shl, fl[:, 1, :], ALU.mult)
            chain.link(nc.vector.tensor_tensor(flt[:, 1, :], shr, fl[:, 2, :], ALU.mult))
            chain.link(nc.vector.tensor_tensor(res, flt[:, 0, :], flt[:, 1, :], ALU.add))
            nc.vector.tensor_scalar(rlo, res, 15, None, ALU.bitwise_and)
            chain.link(nc.vector.tensor_scalar(rhi, res, 4, None, ALU.logical_shift_right))
            nc.vector.scalar_tensor_tensor(flt[:, 2, :], fl[:, 3, :], -16.0, rlo, ALU.mult, ALU.add)
            chain.link(nc.vector.scalar_tensor_tensor(flt[:, 3, :], fl[:, 3, :], -16.0, rhi, ALU.mult, ALU.add))
            for n in range(2):
                ins = nc.vector.tensor_tensor(eq[:, n], key[:, :, :], flt[:, 2 + n, :].unsqueeze(2).broadcast_to([P, NT, 16]),
                                              ALU.is_equal)
            chain.link(ins)
            for n, lo in enumerate((32, 36)):
                part = u[:, :, lo:lo + 16]
                chain.link(nc.vector.scalar_tensor_tensor(part, eq[:, n], 2.0, part, ALU.mult, ALU.add))
            rows = xv[:, :, i, :, :]
            chain.link(nc.vector.tensor_tensor(rows, rows, u[:, :, :].rearrange("p (b j) c -> p b j c", j=2), ALU.add))
            dve.sem_inc(s_beat, 1)
            layer_norm_stats(nc, chain, st, tmp[:, 1], tile, NT, 1e-6).then_inc(s_var, 1)
            dve.wait_ge(s_rstd, i * 2 + 2)
            dve.wait_ge(s_tr, i * 4 + 1)
            for q in range(NT):
                ins = nc.vector.tensor_scalar(z[:, q, :], tile(q), tmp[:, 1, 0, q:q + 1], tmp[:, 1, 3, q:q + 1],
                                              ALU.subtract, ALU.mult)
            ins.then_inc(s_z, 1)
            assert chain.n == PREP_LINKS, chain.n

        s_reset = sem("e_reset")

        def neurons(dve, i):
            resets = [i * (3 * B)]

            def reset(ins):
                resets.append(1)
                ins.then_inc(s_reset, 1)

            def resets_done(n):
                dve.wait_ge(s_reset, resets[0] + n)

            for b in range(B):
                dve.wait_ge(s_qkv, i * B + b + 1 + 1)
                dve.wait_ge(s_spk, i * B + max(b - 1, 0) + 1)
                src = ps_q[:, b % 2, :, 0:3 * C]
                if b == 0:
                    nc.vector.tensor_copy(v1[:, 0], src).then_inc(s_v, 1)
                else:
                    resets_done(b)
                    nc.vector.scalar_tensor_tensor(v1[:, b % 2], r1[:, :, :], 0.5, src, ALU.mult, ALU.add).then_inc(s_v, 1)
                dve.wait_ge(s_v, i * B + b + 1 + 1)
                reset(nc.vector.scalar_tensor_tensor(r1[:, :, :], v1[:, b % 2], 1.0, v1[:, b % 2], ALU.is_lt, ALU.mult))

            def masked(bp):
                dve.wait_ge(s_kv, i * 4 + bp + 1 + 1)
                dve.wait_ge(s_o, i * B + max(2 * bp - 2, 0) + 1)
                for ip in range(2):
                    ins = nc.vector.tensor_tensor(kvm[:, bp % 2, ip], ps_kv[:, ip], mask[:, :], ALU.mult)
                ins.then_inc(s_kvm, 1)

            def attended(b):
                dve.wait_ge(s_o, i * B + b + 1 + 1)
                dve.wait_ge(s_so, i * B + max(b - 1, 0) + 1)
                if b == 0:
                    nc.vector.tensor_copy(vo[:, 0], ps_o[:, 0:2 * P]).then_inc(s_vo, 1)
                else:
                    resets_done(B + max(2 * b - 2, 1))
                    nc.vector.scalar_tensor_tensor(vo[:, b % 2], ro[:, :], 0.5, ps_o[:, 0:2 * P], ALU.mult, ALU.add)\
                        .then_inc(s_vo, 1)
                dve.wait_ge(s_vo, i * B + b + 1 + 1)
                reset(nc.vector.scalar_tensor_tensor(ro[:, :], vo[:, b % 2], 0.5, vo[:, b % 2], ALU.is_lt, ALU.mult))

            def output(b):
                dve.wait_ge(s_y, i * B + b + 1 + 1)
                src = ps_y[:, 0:2 * C].rearrange("p (j c) -> p j c", j=2)
                if b == 0:
                    nc.vector.tensor_copy(vy[:, :, :], src).then_inc(s_vy, 1)
                else:
                    resets_done(B + 2 * b + 1)
                    nc.vector.scalar_tensor_tensor(vy[:, :, :], ry[:, :, :], 0.5, src, ALU.mult, ALU.add).then_inc(s_vy, 1)
                dve.wait_ge(s_vy, i * B + b + 1 + 1)
                rows = xv[:, b, i, :, :]
                nc.vector.scalar_tensor_tensor(rows, vy[:, :, :], 1.0, rows, ALU.is_ge, ALU.add)
                reset(nc.vector.scalar_tensor_tensor(ry[:, :, :], vy[:, :, :], 1.0, vy[:, :, :], ALU.is_lt, ALU.mult))

            masked(0)
            for b in range(B):
                if b % 2 == 0 and b // 2 + 1 < 4:
                    masked(b // 2 + 1)
                attended(b)
                if b:
                    output(b - 1)
            output(B - 1)
            assert len(resets) == 1 + 3 * B

        def project(pe, i):
            for b in range(B):
                if b < 2:
                    pe.wait_ge(s_zT, i * 4 + 2 * b + 2 + 1)
                else:
                    if b == 2:
                        pe.wait_ge(s_zT, i * 4 + 4 + 1)
                    pe.wait_ge(s_v, i * B + b - 1 + 1)
                for j in range(2):
                    q = 2 * b + j
                    dst = ps_q[:, b % 2, j]
                    nc.tensor.matmul(dst[:, 0:P], wqkv[:, 0:C], zT[:, q, :], start=True, stop=False)
                    nc.tensor.matmul(dst[:, 0:P], bias[:, 0:C], ones[:, :], start=False, stop=True)
                    nc.tensor.matmul(dst[:, P:3 * P], zT[:, q, :], wqkv[:, C:3 * C], start=True, stop=False)
                    ins = nc.tensor.matmul(dst[:, P:3 * P], ones[:, :], bias[:, C:3 * C], start=False, stop=True)
                ins.then_inc(s_qkv, 1)

        def attend(pe, i):
            def key_values(bp):
                pe.wait_ge(s_spk, i * B + 2 * bp + 2 + 1)
                pe.wait_ge(s_kvm, i * 4 + bp + 1)
                for n in range(4):
                    b, j = 2 * bp + n // 2, n % 2
                    for ip in range(2):
                        rows = slice(64 * ip, 64 * ip + 64)
                        ins = nc.tensor.matmul(ps_kv[:, ip, n * C:(n + 1) * C], spk[rows, b, j, C:2 * C],
                                               spk[rows, b, j, 2 * C:3 * C], start=True, stop=True)
                ins.then_inc(s_kv, 1)

            def attended(b):
                pe.wait_ge(s_kvm, i * 4 + b // 2 + 1 + 1)
                pe.wait_ge(s_vo, i * B + b + 1)
                for j in range(2):
                    for ip in range(2):
                        n = (b % 2) * 2 + j
                        ins = nc.tensor.matmul(ps_o[:, j * P + ip * 64:j * P + ip * 64 + 64],
                                               kvm[:, (b // 2) % 2, ip, n * C:(n + 1) * C],
                                               spk[:, b, j, ip * 64:ip * 64 + 64], start=True, stop=True)
                ins.then_inc(s_o, 1)

            def output(b):
                pe.wait_ge(s_so, i * B + b + 1 + 1)
                pe.wait_ge(s_vy, i * B + b + 1)
                for j in range(2):
                    for n in range(3):
                        nc.tensor.matmul(ps_y[:, j * C:(j + 1) * C], so[:, b % 2, j * P:(j + 1) * P], wo[:, n, :],
                                         start=(n == 0), stop=False)
                    ins = nc.tensor.matmul(ps_y[:, j * C:(j + 1) * C], ones[:, :], bias[:, 3 * C:4 * C],
                                           start=False, stop=True)
                ins.then_inc(s_y, 1)

            key_values(0)
            for b in range(B):
                if b % 2 == 0 and b // 2 + 1 < 4:
                    key_values(b // 2 + 1)
                attended(b)
                if b:
                    output(b - 1)
            output(B - 1)

        def turn(pe, i):
            pe.wait_ge(s_z, i + 1 + 1)
            pe.wait_ge(s_v, i * B + 1)
            for g in range(4):
                for q in range(G):
                    ins = nc.tensor.transpose(ps_q[:, g // 2, g % 2, q * P:(q + 1) * P], z[:, g * G + q, :], ident[:, :])
                ins.then_inc(s_tr, 1)

        def fire(pool, i):
            for b in range(B):
                pool.wait_ge(s_v, i * B + b + 1 + 1)
                if b == 0:
                    pool.wait_ge(s_o, i * B + 1)
                pool.sem_inc(s_beat, 1)
                nc.gpsimd.tensor_scalar(spk[:, b], v1[:, b % 2], 1.0, None, ALU.is_ge).then_inc(s_spk, 1)
            for b in range(B):
                pool.wait_ge(s_vo, i * B + b + 1 + 1)
                pool.wait_ge(s_y, i * B + max(b - 1, 0) + 1)
                pool.sem_inc(s_beat, 1)
                nc.gpsimd.tensor_scalar(so[:, b % 2], vo[:, b % 2], 0.5, None, ALU.is_ge).then_inc(s_so, 1)

        def deviations(pool, i):
            for n in range(2):
                pool.wait_ge(s_var, i * 2 + n + 1)
                inverse_deviation(nc, tmp[:, n], minus_half).then_inc(s_rstd, 1)

        with nc.Block() as block:
            @block.sync
            def _(sp):
                sp.dma_start(rank[:, :, :], t["first_rank"].rearrange("p (q k) -> p q k", k=16)).then_inc(s_const, 16)
                sp.dma_start(key[:, :, :], t["nibble_key"].rearrange("p (q k) -> p q k", k=16)).then_inc(s_const, 16)
                sp.dma_start(mask[:, :], t["head_mask"]).then_inc(s_const, 16)
                sp.wait_ge(s_zero, 1)
                for w in range(B):
                    sp.dma_start(slots.rearrange("(w q p) c -> w p q c", w=B, p=P)[w],
                                 zero[:, :].unsqueeze(1).broadcast_to([P, SLOT_TILES, C])).then_inc(s_clear, 16)
                sp.wait_ge(s_clear, 16 * B)

            @block.vector
            def _(dve):
                for s in (s_z, s_v, s_kvm, s_vo, s_vy):
                    dve.sem_inc(s, 1)
                nc.vector.memset(zero[:, :], 0.0).then_inc(s_zero, 1)
                dve.wait_ge(s_const, 48)
                prepare(dve, 0)
                with dve.Fori(0, NP2 - 1) as i:
                    prepare(dve, i + 1)
                    neurons(dve, i)
                neurons(dve, NP2 - 1)

            @block.gpsimd
            def _(pool):
                for s in (s_spk, s_so):
                    pool.sem_inc(s, 1)
                deviations(pool, 0)
                with pool.Fori(0, NP2 - 1) as i:
                    deviations(pool, i + 1)
                    fire(pool, i)
                fire(pool, NP2 - 1)

            @block.scalar
            def _(act):
                act.sem_inc(s_zT, 1)
                with act.Fori(0, NP2) as i:
                    for g in range(4):
                        act.wait_ge(s_tr, i * 4 + g + 1 + 1)
                        nc.scalar.activation(zT[:, g * G:(g + 1) * G, :].rearrange("p q k -> p (q k)"),
                                             ps_q[:, g // 2, g % 2, :], ACT.Copy).then_inc(s_zT, 1)

            @block.tensor
            def _(pe):
                for s in (s_tr, s_qkv, s_kv, s_o, s_y):
                    pe.sem_inc(s, 1)
                with pe.Fori(0, NP2) as i:
                    turn(pe, i)
                    project(pe, i)
                    attend(pe, i)


def experts(nc, t, sb, pb, sem, x_sb, ident, minus_half, slots, out):
    out_view = out.rearrange("b (hp ip) w c -> (ip w) (b hp) c", ip=2)
    slots_view = slots.rearrange("(g q p) c -> p g q c", q=G, p=P)
    LAG = 3
    with ExitStack() as a:
        wp = sb("wp", [P, 2, E * EW], F32R, at=a)
        wh, wl = wp[:, 0], wp[:, 1]
        bp = sb("bp", [3, E * EW], BF16, at=a)
        ones = sb("m_ones", [P, P], BF16, at=a)
        before = sb("before", [P, P], BF16, at=a)
        ring = sb("ring", [P, 4 * HP * C], at=a)
        y = sb("f_y", [P, 2, G * 2, C], at=a)
        stage = sb("f_stage", [P, 2, G * P], at=a)
        rows_in, rows_out = y[:, 0].rearrange("p (k q) c -> p k q c", k=2), y[:, 1].rearrange("p (k q) c -> p k q c", k=2)
        sil = stage[:, 0].rearrange("p (k f) -> p k f", k=2)
        act_rows = stage[:, 1].rearrange("p (k f) -> p k f", k=2)
        uTh = sb("uTh", [P, 2, G * P], F32R, at=a)
        uTl = sb("uTl", [P, 2, G * P], F32R, at=a)
        aTh = sb("aTh", [P, 2, DFF], F32R, at=a)
        aTl = sb("aTl", [P, 2, DFF], F32R, at=a)
        wg = sb("wg", [P, E], at=a)
        bg = sb("bg", [P, E], at=a)
        braw = sb("braw", [5 * E, P], at=a)
        bpart = sb("bpart_m", [5 * E, 3, P], BF16, at=a)
        brest = sb("brest", [5 * E, P], at=a)
        num = sb("num", [P, HP, E], at=a)
        upto = sb("upto", [P, E, E], at=a)
        slot_no = sb("slot_no", [P, SLOT_TILES, E], at=a)
        first_slot = sb("first_slot", [P, B], at=a)
        before_f = sb("before_f", [P, P], at=a)
        st = sb("f_st", [P, NTILES, 6], at=a)
        tmp = sb("f_tmp", [P, 4, NTILES], at=a)
        lg = sb("lg", [P, HP, E], at=a)
        pick = sb("pick", [P, 2, HP, E], at=a)
        low = sb("low", [P, HP, E], at=a)
        chosen = sb("chosen", [P, HP + 1, E], BF16, at=a)
        lead = sb("lead", [P, HP], at=a)
        top = sb("top", [P, 2, NTILES], at=a)
        wt = sb("wt", [P, 2, NTILES], at=a)
        pos = sb("pos", [P, 2, NTILES], U32, at=a)
        index = sb("index", [P, 4, 2, HP], U32, at=a)
        cnt = sb("cnt", [P, 2, E], I32, at=a)
        base = sb("base", [P, 3, E], at=a)
        prod = sb("prod", [P, E, E], at=a)
        place = sb("place", [P, HP, E], at=a)
        pp = sb("pp", [P, 2, HP, E], at=a)
        ppr = sb("ppr", [P, 2, HP], at=a)
        past = sb("past", [1, SLOT_TILES, E], at=a)
        pastr = sb("pastr", [1, SLOT_TILES], at=a)
        offset = sb("offset", [1, LAG + B * SLOT_TILES], I32, at=a)
        ps_u = pb("ps_u", [P, 2, G * P], at=a)
        ps_h = pb("ps_h", [P, 2, 2 * DFF], at=a)
        ps_a = pb("ps_a", [P, 2, 512], at=a)
        ps_y = pb("ps_y3", [P, 2, 2, 2, C], at=a)
        ps_log, ps_rank = ps_a[:, 0, 0:HP * E], ps_a[:, 1, 0:(HP + 1) * E]

        s_load = sem("f_constants")
        s_raw = sem("f_raw_weights")
        s_wh = sem("f_weights_upper")
        s_wl = sem("f_weights_rest")
        s_b = sem("f_bias_parts")
        s_bp = sem("f_bias_rows")
        s_chain = sem("f_chain")
        s_var = sem("f_variance")
        s_rstd = sem("f_inverse_deviation")
        s_y = sem("f_normalised")
        s_tr = sem("f_transposed")
        s_st = sem("f_staged")
        s_cp = sem("f_row_copied")
        s_lg = sem("f_logits")
        s_ch = sem("f_chosen")
        s_rk = sem("f_ranked")
        s_pos = sem("f_slots_known")
        s_free = sem("f_ring_free")
        s_dif = sem("f_difference")
        s_exp = sem("f_exponential")
        s_index = sem("f_index")
        s_beat = sem("f_beat")
        s_sc = [sem(f"scattered_{k}") for k in range(4)]
        s_in = [sem("slot_rows_0"), sem("slot_rows_1")]
        s_turn = sem("slot_transposed")
        s_uh = sem("slot_upper")
        s_ul = sem("slot_rest")
        s_h = sem("slot_hidden")
        s_sil = sem("slot_silu")
        s_act = sem("slot_gated")
        s_at = sem("slot_gated_transposed")
        s_ah = sem("slot_gated_upper")
        s_al = sem("slot_gated_rest")
        s_ey = sem("slot_expert_out")
        s_yf = sem("slot_out_first_addend")
        s_yc = sem("slot_out_added")
        s_ys = [sem("slot_out_stored_0"), sem("slot_out_stored_1")]
        s_g = [sem("gathered_0"), sem("gathered_1")]
        s_one = sem("f_first_added")
        s_sum = sem("f_combined")
        s_out = sem("f_stored")

        raw = ring[:, HP * C:HP * C + E * EW]
        raw_by_expert = raw.rearrange("p (e f) -> p e f", e=E)
        bias_rows = bp[:, :].rearrange("p (e k f) -> p e k f", e=E, f=P)
        STEPS = 2 * G
        TURNS = B * SLOT_TILES // STEPS
        TW = SLOT_TILES // STEPS
        WIN = 2 * HP * 16
        LINKS = 21

        def need(eng, s, value):
            if not isinstance(value, int) or value > 0:
                eng.wait_ge(s, value)

        with nc.Block() as block:
            @block.sync
            def _(sp):
                sp.dma_start(raw_by_expert[:, :, 0:2 * DFF], t["L1_ffn_W1"].rearrange("e c f -> c e f")).then_inc(s_raw, 16)
                for k in range(2):
                    at = 2 * DFF + k * C
                    sp.dma_start(raw_by_expert[:, :, at:at + C],
                                 t["L1_ffn_W2"][:, k * P:(k + 1) * P, :].rearrange("e f c -> f e c")).then_inc(s_raw, 16)
                sp.dma_start(wg[:, :], t["L1_ffn_Wg"]).then_inc(s_load, 16)
                sp.dma_start(bg[:, :], t["L1_ffn_bg"].rearrange("(a e) -> a e", a=1).broadcast_to([P, E])).then_inc(s_load, 16)
                for k in range(4):
                    sp.dma_start(braw[k * E:(k + 1) * E, :], t["L1_ffn_b1"][:, k * P:(k + 1) * P]).then_inc(s_load, 16)
                sp.dma_start(braw[4 * E:5 * E, :], t["L1_ffn_b2"]).then_inc(s_load, 16)
                sp.dma_start(num[:, :, :], t["expert_number"].rearrange("p (q e) -> p q e", e=E)).then_inc(s_load, 16)
                sp.dma_start(upto[:, :, :], t["expert_up_to"].rearrange("p (q e) -> p q e", e=E)).then_inc(s_load, 16)
                sp.dma_start(slot_no[:, :, :], t["slot_tile_number"].rearrange("p (q e) -> p q e", e=E)).then_inc(s_load, 16)
                sp.dma_start(first_slot[:, :], t["window_first_slot"]).then_inc(s_load, 16)
                sp.dma_start(before_f[:, :], t["token_before"]).then_inc(s_load, 16)
                sp.wait_ge(s_b, 1)
                for n in range(3):
                    for k in range(5):
                        sp.dma_start(bias_rows[n:n + 1, :, k, :], bpart[k * E:(k + 1) * E, n, :]).then_inc(s_bp, 16)

                def load_window(w):
                    sp.wait_ge(s_sc[w % 4], (w // 4 + 1) * WIN)

                    def load(n, j):
                        g = (w * TW + n) * 2 + j
                        need(sp, s_turn, g - 1)
                        src = slots_view[:, bass.ds(g, 1)] if not isinstance(g, int) else slots_view[:, g:g + 1]
                        sp.dma_start(rows_in[:, j:j + 1], src).then_inc(s_in[j], 16)

                    if w == 0:
                        load(0, 0)
                        load(0, 1)
                    with sp.Fori(1 if w == 0 else 0, TW) as n:
                        for j in range(2):
                            load(n, j)

                def store(w):
                    sp.wait_ge(s_sum, w * HP + 3 * HP)
                    tiles = bass.ds(w * HP, HP)
                    sp.dma_start(out_view[:, tiles, :], x_sb[:, tiles, :]).then_inc(s_out, 16)

                sp.wait_ge(s_tr, B * 4 + 1)
                sp.wait_ge(s_cp, B + 1)
                for w in range(B):
                    if w >= 4:
                        store(w - 4)
                    load_window(w)
                for w in range(B - 4, B):
                    store(w)
                sp.wait_ge(s_out, 16 * B)

            @block.gpsimd
            def _(pool):
                pool.wait_ge(s_wh, 1)
                nc.gpsimd.tensor_tensor(wl, raw, wh.bitcast(F32), ALU.subtract).then_inc(s_wl, 1)
                pool.wait_ge(s_var, 1)
                nc.gpsimd.tensor_tensor(tmp[:, 3, :], tmp[:, 2, :], minus_half[:, 0:1].broadcast_to([P, NTILES]), ALU.pow)\
                    .then_inc(s_rstd, 1)

                def take_slots(w, at):
                    nc.gpsimd.tensor_copy(index[:, at], pos[:, :, bass.ds(w * HP, HP)]).then_inc(s_index, 1)

                with pool.Fori(0, B // 4) as r:
                    for k in range(4):
                        w = r * 4 + k
                        pool.wait_ge(s_pos, w + 1)
                        pool.sem_inc(s_beat, 1)
                        take_slots(w, k)
                        pool.wait_ge(s_index, w + 1)
                        pool.wait_ge(s_cp, w + 2)
                        pool.sem_inc(s_beat, 1)
                        for q in range(HP):
                            row = (k * HP + q) * C
                            for n in range(2):
                                nc.gpsimd.indirect_dma_start(
                                    slots, bass.IndirectOffsetOnAxis(index[:, k, n, q:q + 1], 0),
                                    ring[:, row:row + C], None).then_inc(s_sc[k], 16)
                        if k >= 2:
                            pool.wait_ge(s_sc[k - 2], r * WIN + WIN)
                            pool.sem_inc(s_free, 1)
                    for k in range(2, 4):
                        pool.wait_ge(s_sc[k], r * WIN + WIN)
                        pool.sem_inc(s_free, 1)

                with pool.Fori(0, B // 2) as m:
                    for k in range(2):
                        w = m * 2 + k
                        for j in range(2):
                            pool.wait_ge(s_ys[j], (w + 1) * (TW * 16))
                        pool.wait_ge(s_sum, w * HP + HP)
                        pool.sem_inc(s_beat, 1)
                        take_slots(w, k)
                        pool.wait_ge(s_index, w + B + 1)
                        pool.sem_inc(s_beat, 1)
                        for q in range(HP):
                            for n in range(2):
                                row = ((2 * k + n) * HP + q) * C
                                nc.gpsimd.indirect_dma_start(
                                    ring[:, row:row + C], None,
                                    slots, bass.IndirectOffsetOnAxis(index[:, k, n, q:q + 1], 0)).then_inc(s_g[k], 16)

            @block.vector
            def _(dve):
                with dve.Fori(0, B) as b:
                    for q in range(HP):
                        nc.vector.bn_stats(st[:, bass.ds(b * HP + q, 1), :], x_sb[:, bass.ds(b * HP + q, 1), :])
                nc.vector.memset(ones[:, :], 1.0)
                nc.vector.memset(offset[:, 0:LAG], 0)
                chain0 = Chain(dve, s_chain)
                chain0.link(nc.vector.memset(chosen[:, :, :], 0.0))
                moments(nc, chain0, st, tmp, 1e-5).then_inc(s_var, 1)
                dve.wait_ge(s_load, 12 * 16)
                chain0.link(split3(nc, chain0, [bpart[:, n, :] for n in range(3)], braw[:, :], brest[:, :]))
                nc.vector.tensor_copy(before[:, :], before_f[:, :]).then_inc(s_b, 1)
                dve.wait_ge(s_rstd, 1)
                dve.sem_inc(s_y, 1)
                dve.sem_inc(s_ch, 1)
                dve.sem_inc(s_sum, 2 * HP)

                wide = lambda v: v.unsqueeze(2).broadcast_to([P, HP, E])
                with dve.Fori(0, B) as w:
                    chain = Chain(dve, s_chain, w * LINKS + chain0.n)
                    dve.wait_ge(s_tr, w * 4 + 1)
                    dve.wait_ge(s_cp, w + 1)
                    for q in range(HP):
                        mean, rstd = tmp[:, 0, bass.ds(w * HP + q, 1)], tmp[:, 3, bass.ds(w * HP + q, 1)]
                        row = x_sb[:, bass.ds(w * HP + q, 1), :].rearrange("p q c -> p (q c)")
                        ins = nc.vector.tensor_scalar(y[:, q // 8, q % 8, :], row, mean, rstd, ALU.subtract, ALU.mult)
                    ins.then_inc(s_y, 1)
                    dve.wait_ge(s_lg, w + 1)
                    chain.link(nc.vector.tensor_tensor(lg[:, :, :], ps_log.rearrange("p (q e) -> p q e", e=E),
                                                       bg[:, :].unsqueeze(1).broadcast_to([P, HP, E]), ALU.add))

                    def largest(n):
                        val = top[:, n, bass.ds(w * HP, HP)]
                        chain.link(nc.vector.tensor_reduce(val, lg[:, :, :], AXX, ALU.max))
                        chain.link(nc.vector.tensor_tensor(low[:, :, :], lg[:, :, :], wide(val), ALU.is_lt))
                        chain.link(nc.vector.scalar_tensor_tensor(low[:, :, :], low[:, :, :], float(E), num[:, :, :], ALU.mult, ALU.add))
                        chain.link(nc.vector.tensor_reduce(lead[:, :], low[:, :, :], AXX, ALU.min))
                        chain.link(nc.vector.tensor_tensor(pick[:, n], num[:, :, :], wide(lead[:, :]), ALU.is_equal))

                    largest(0)
                    chain.link(nc.vector.scalar_tensor_tensor(lg[:, :, :], pick[:, 0], -3e38, lg[:, :, :], ALU.mult, ALU.add))
                    largest(1)
                    nc.vector.tensor_tensor(chosen[:, 0:HP, :], pick[:, 0], pick[:, 1], ALU.add).then_inc(s_ch, 1)
                    dve.wait_ge(s_rk, w + 1)
                    chain.link(nc.vector.tensor_scalar(cnt[:, 0], ps_rank[:, HP * E:], float(P - 1), None, ALU.add))
                    chain.link(nc.vector.tensor_scalar(cnt[:, 1], cnt[:, 0], 7, None, ALU.logical_shift_right))
                    chain.link(nc.vector.tensor_tensor(prod[:, :, :], upto[:, :, :], cnt[:, 1].unsqueeze(1).broadcast_to([P, E, E]), ALU.mult))
                    chain.link(nc.vector.tensor_reduce(base[:, 0], prod[:, :, :], AXX, ALU.add))
                    nc.vector.tensor_tensor(past[:, :, :], slot_no[0:1, :, :], base[0:1, 0].unsqueeze(1).broadcast_to([1, SLOT_TILES, E]), ALU.is_ge)
                    chain.link(nc.vector.tensor_tensor(base[:, 1], base[:, 0], cnt[:, 1], ALU.subtract))
                    nc.vector.tensor_reduce(pastr[:, :], past[:, :, :], AXX, ALU.add)
                    chain.link(nc.vector.scalar_tensor_tensor(base[:, 2], base[:, 1], float(P), first_slot[:, bass.ds(w, 1)].broadcast_to([P, E]), ALU.mult, ALU.add))
                    nc.vector.tensor_scalar(offset[:, bass.ds(w * SLOT_TILES + LAG, SLOT_TILES)], pastr[:, :], float(E - 1), float(EW), ALU.min, ALU.mult)
                    chain.link(nc.vector.tensor_tensor(place[:, :, :], ps_rank[:, 0:HP * E].rearrange("p (q e) -> p q e", e=E),
                                                       base[:, 2].unsqueeze(1).broadcast_to([P, HP, E]), ALU.add))
                    for n in range(2):
                        ins = nc.vector.tensor_tensor(pp[:, n], pick[:, n], place[:, :, :], ALU.mult)
                    chain.link(ins)
                    chain.link(nc.vector.tensor_reduce(ppr[:, :, :], pp[:, :, :, :], AXX, ALU.add))
                    nc.vector.tensor_copy(pos[:, :, bass.ds(w * HP, HP)], ppr[:, :, :]).then_inc(s_pos, 1)
                    assert chain.n == LINKS, chain.n
                chain = Chain(dve, s_chain, B * LINKS + chain0.n)
                nc.vector.tensor_tensor(wt[:, 0, :], top[:, 1, :], top[:, 0, :], ALU.subtract).then_inc(s_dif, 1)
                dve.wait_ge(s_exp, 1)
                chain.link(nc.vector.tensor_scalar(wt[:, 0, :], wt[:, 1, :], 1.0, None, ALU.add))
                chain.link(nc.vector.reciprocal(wt[:, 0, :], wt[:, 0, :]))
                chain.link(nc.vector.tensor_tensor(wt[:, 1, :], wt[:, 1, :], wt[:, 0, :], ALU.mult))

                def rest(g, j):
                    dve.wait_ge(s_uh, g + 1)
                    nc.vector.tensor_tensor(uTl[:, j], ps_u[:, j], uTh[:, j].bitcast(F32), ALU.subtract).then_inc(s_ul, 1)

                def gated(n, k):
                    dve.wait_ge(s_sil, n + 1)
                    need(dve, s_at, n - 1)
                    nc.vector.tensor_tensor(act_rows[:, k], ps_h[:, k, DFF:], sil[:, k], ALU.mult).then_inc(s_act, 1)

                def gated_rest(n, k):
                    dve.wait_ge(s_ah, n + 1)
                    nc.vector.tensor_tensor(aTl[:, k], ps_a[:, k, 0:DFF], aTh[:, k].bitcast(F32), ALU.subtract).then_inc(s_al, 1)

                def add_out(i, r):
                    pair, half, slot = i * 4 + r, r % 2, (r // 2) % 2
                    dve.wait_ge(s_yf, pair + 1)
                    dst = rows_out[:, slot, 2 * half:2 * half + 2, :]
                    nc.vector.tensor_tensor(dst, ps_y[:, half, :, 1, :], dst, ALU.add).then_inc(s_yc, 1)

                def turn(i, last=False, beside=lambda m: None):
                    head = isinstance(i, int) and i == 0
                    for m in range(STEPS):
                        n = i * STEPS + m
                        if m >= 2 or not head:
                            gated_rest(n - 2, m % 2)
                        gated(n, m % 2)
                        if m == 2:
                            rest(i * 2 + 1, 1)
                        if m == 6 and not last:
                            rest(i * 2 + 2, 0)
                        if m % 2 and (m >= 5 or not head):
                            add_out(i, (m - 5) // 2)
                        beside(m)

                def combine(w, par, quarter, half):
                    def part(m):
                        tile, n = quarter * 4 + m // 2, m % 2
                        if m == 0:
                            dve.wait_ge(s_g[par], half * WIN + WIN)
                        if n == 1:
                            dve.wait_ge(s_one, (w * 4 + quarter) * 4 + m // 2 + 1)
                        row = x_sb[:, bass.ds(w * HP + tile, 1), :].rearrange("p q c -> p (q c)")
                        ins = nc.vector.scalar_tensor_tensor(
                            row, ring[:, bass.ds((2 * par + n) * HP * C + tile * C, C)],
                            wt[:, n, bass.ds(w * HP + tile, 1)], row, ALU.mult, ALU.add)
                        ins.then_inc(s_sum if n else s_one, 1)
                    return part

                rest(0, 0)
                turn(0)
                with dve.Fori(1, 2 * TW) as i:
                    turn(i)

                def window(m, k, quarters=4):
                    first = (m * 2 + k) * TW
                    turn(first)
                    with dve.Fori(0, quarters) as quarter:
                        turn(first + quarter + 1, beside=combine((m - 1) * 2 + k, k, quarter, m - 1))

                with dve.Fori(1, B // 2 - 1) as m:
                    for k in range(2):
                        window(m, k)
                m = B // 2 - 1
                window(m, 0)
                window(m, 1, quarters=3)
                turn(TURNS - 1, last=True, beside=combine(m * 2 - 1, 1, 3, m - 1))
                for k in range(2):
                    gated_rest(B * SLOT_TILES - 2 + k, k)
                for r in (-2, -1):
                    add_out(TURNS, r)
                for k in range(2):
                    with dve.Fori(0, 4) as quarter:
                        for m in range(STEPS):
                            combine(B - 2 + k, k, quarter, B // 2 - 1)(m)

            @block.scalar
            def _(act):
                act.wait_ge(s_raw, 48)
                nc.scalar.activation(wh, raw, ACT.Copy).then_inc(s_wh, 1)
                act.sem_inc(s_cp, 1)
                act.sem_inc(s_st, 2)
                act.sem_inc(s_free, 4)
                with act.Fori(0, B // 4) as r:
                    for slot in range(4):
                        w = r * 4 + slot
                        for g in range(4):
                            act.wait_ge(s_tr, w * 4 + g + 2)
                            nc.scalar.activation(stage[:, g % 2, :], ps_h[:, g % 2, :], ACT.Copy).then_inc(s_st, 1)
                        act.wait_ge(s_free, w + 1)
                        if slot == 1:
                            act.wait_ge(s_wl, 1)
                        nc.scalar.activation(ring[:, slot * HP * C:(slot + 1) * HP * C],
                                             y[:, :, :, :].rearrange("p a q c -> p (a q c)"), ACT.Copy).then_inc(s_cp, 1)
                act.wait_ge(s_dif, 1)
                nc.scalar.activation(wt[:, 1, :], wt[:, 0, :], ACT.Exp).then_inc(s_exp, 1)

                def upper(g, j):
                    act.wait_ge(s_turn, g + 1)
                    need(act, s_h, g * G - G)
                    nc.scalar.activation(uTh[:, j], ps_u[:, j], ACT.Copy).then_inc(s_uh, 1)

                def silu(n, k):
                    act.wait_ge(s_h, n + 1)
                    need(act, s_act, n - 1)
                    nc.scalar.activation(sil[:, k], ps_h[:, k, 0:DFF], ACT.Silu).then_inc(s_sil, 1)

                def gated_upper(n, k):
                    act.wait_ge(s_at, n + 1)
                    need(act, s_ey, n - 1)
                    nc.scalar.activation(aTh[:, k], ps_a[:, k, 0:DFF], ACT.Copy).then_inc(s_ah, 1)

                def copy_out(i, r):
                    pair, half, slot = i * 4 + r, r % 2, (r // 2) % 2
                    act.wait_ge(s_ey, pair * 2 + 2)
                    if half == 0:
                        need(act, s_ys[slot], (i - slot) * 16)
                    nc.scalar.activation(rows_out[:, slot, 2 * half:2 * half + 2, :], ps_y[:, half, :, 0, :], ACT.Copy)\
                        .then_inc(s_yf, 1)

                def store(g, j):
                    act.wait_ge(s_yc, g * 2 + 2)
                    dst = slots_view[:, bass.ds(g, 1)] if not isinstance(g, int) else slots_view[:, g:g + 1]
                    act.dma_start(dst, rows_out[:, j:j + 1]).then_inc(s_ys[j], 16)

                def turn(i, last=False):
                    head = isinstance(i, int) and i == 0
                    for m in range(STEPS):
                        n = i * STEPS + m
                        if m >= 2 or not head:
                            gated_upper(n - 2, m % 2)
                        silu(n, m % 2)
                        if m == 2:
                            upper(i * 2 + 1, 1)
                        if m == 6 and not last:
                            upper(i * 2 + 2, 0)
                        if m % 2 and (m >= 5 or not head):
                            copy_out(i, (m - 5) // 2)
                        if m == 5 and not head:
                            store(i * 2 - 1, 1)
                        if m == 1 and not head:
                            store(i * 2 - 2, 0)

                upper(0, 0)
                turn(0)
                with act.Fori(1, TURNS - 1) as i:
                    turn(i)
                turn(TURNS - 1, last=True)
                n = B * SLOT_TILES
                store(n // G - 2, 0)
                for k in range(2):
                    gated_upper(n - 2 + k, k)
                for r in (-2, -1):
                    copy_out(TURNS, r)
                store(n // G - 1, 1)

            @block.tensor
            def _(pe):
                pe.wait_ge(s_b, 1)
                pe.sem_inc(s_tr, 1)
                with pe.Fori(0, B) as w:
                    def turn(g):
                        pe.wait_ge(s_st, w * 4 + g + 1)
                        for q in range(G):
                            row = g * G + q
                            ins = nc.tensor.transpose(ps_h[:, g % 2, q * P:(q + 1) * P], y[:, row // 8, row % 8, :], ident[:, :])
                        ins.then_inc(s_tr, 1)

                    def logits(g):
                        pe.wait_ge(s_st, w * 4 + g + 3)
                        for q in range(G):
                            row = g * G + q
                            ins = nc.tensor.matmul(ps_log[:, row * E:(row + 1) * E], stage[:, g % 2, q * P:(q + 1) * P],
                                                   wg[:, :], start=True, stop=True)
                        return ins

                    pe.wait_ge(s_y, w + 2)
                    turn(0)
                    for g in range(1, 4):
                        turn(g)
                        logits(g - 1)
                    logits(3).then_inc(s_lg, 1)
                    pe.wait_ge(s_ch, w + 2)
                    nc.tensor.matmul(ps_rank, before[:, :], chosen[:, :, :].rearrange("p q e -> p (q e)"), start=True, stop=False)
                    for d in range(1, HP + 1):
                        ins = nc.tensor.matmul(ps_rank[:, d * E:], ones[:, :],
                                               chosen[:, 0:HP + 1 - d, :].rearrange("p q e -> p (q e)"), start=False, stop=(d == HP))
                    ins.then_inc(s_rk, 1)

                def transposes(g, j, i):
                    pe.wait_ge(s_in[j], i * 16 + 16)
                    need(pe, s_ul, g - 1)
                    for q in range(G):
                        ins = nc.tensor.transpose(ps_u[:, j, q * P:(q + 1) * P], rows_in[:, j, q, :], ident[:, :])
                    ins.then_inc(s_turn, 1)

                def load_offsets(i, count):
                    at = slice(0, count) if isinstance(i, int) and i == 0 else bass.ds(i * STEPS, count)
                    where = [pe.alloc_register(f"weights_at_{i if isinstance(i, int) else "turn"}_{k}") for k in range(count)]
                    pe.load(where, offset[0:1, at])
                    return [pe.snap(r, donate=True, min_val=0, max_val=(E - 1) * EW) for r in where]

                def hidden(i, m, o):
                    n, j, q, k = i * STEPS + m, m // G, m % G, m % 2
                    if q == 0:
                        pe.wait_ge(s_ul, i * 2 + j + 1)
                    dst = ps_h[:, k]
                    hi, lo = uTh[:, j, q * P:(q + 1) * P], uTl[:, j, q * P:(q + 1) * P]
                    at = bass.ds(o, 2 * DFF)
                    nc.tensor.matmul(dst, hi, wh[:, at], start=True, stop=False)
                    nc.tensor.matmul(dst, hi, wl[:, at], start=False, stop=False)
                    nc.tensor.matmul(dst, lo, wh[:, at], start=False, stop=False)
                    nc.tensor.matmul(dst, ones[0:3, :], bp[:, at], start=False, stop=True).then_inc(s_h, 1)

                def turn_gated(n, k):
                    for h in range(2):
                        ins = nc.tensor.transpose(ps_a[:, k, h * P:(h + 1) * P], act_rows[:, k, h * P:(h + 1) * P], ident[:, :])
                    ins.then_inc(s_at, 1)

                def expert_out(pair, m, o):
                    half, q, k = (m // 2) % 2, m % 2, m % 2
                    if q == 0:
                        need(pe, s_yc, pair - 1)
                    both, first = ps_y[:, half, q].rearrange("p a c -> p (a c)"), ps_y[:, half, q, 0]
                    for h in range(2):
                        hi, lo = aTh[:, k, h * P:(h + 1) * P], aTl[:, k, h * P:(h + 1) * P]
                        at = bass.ds(o + 2 * DFF + h * C, C)
                        nc.tensor.matmul(both, hi, wp[:, :, at], start=(h == 0), stop=False)
                        ins = nc.tensor.matmul(first, lo, wp[:, 0, at], start=False, stop=(h == 1))
                        if h == 0:
                            nc.tensor.matmul(first, ones[0:3, :], bp[:, bass.ds(o + 2 * DFF, C)], start=False, stop=False)
                    ins.then_inc(s_ey, 1)

                def turn(i, head=False, last=False):
                    at = load_offsets(i, LAG + STEPS)
                    for m in range(STEPS):
                        n = i * STEPS + m
                        if head and m == 2:
                            pe.wait_ge(s_act, 1)
                        elif m >= 3 or not head:
                            pe.wait_ge(s_al, n - 2)
                        if m >= 2 or not head:
                            turn_gated(n - 2, m % 2)
                        hidden(i, m, at[LAG + m])
                        if m == 1:
                            transposes(i * 2 + 1, 1, i)
                        if m == 5 and not last:
                            transposes(i * 2 + 2, 0, i + 1)
                        if m >= 3 or not head:
                            expert_out(i * 4 + (m - 3) // 2, (m - 3) % STEPS, at[m])

                pe.wait_ge(s_pos, B)
                pe.wait_ge(s_wl, 1)
                pe.wait_ge(s_bp, 15 * 16)
                transposes(0, 0, 0)
                turn(0, head=True)
                with pe.Fori(1, TURNS - 1) as i:
                    turn(i)
                turn(TURNS - 1, last=True)
                at = load_offsets(TURNS, LAG)
                for m in range(3):
                    n = TURNS * STEPS + m
                    pe.wait_ge(s_al, n - 2)
                    if m < 2:
                        pe.wait_ge(s_act, n - 1)
                        turn_gated(n - 2, m % 2)
                    expert_out((n - 3) // 2, STEPS - 3 + m, at[m])


_CONSTANTS = spectral_tables()
_OUT = ((B, H, W, C), "float32")


def kernel(**inputs):
    import concourse.bacc as bacc
    from concourse.bass_utils import run_bass_kernel_spmd

    nc = bacc.Bacc("TRN2", target_bir_lowering=False, num_devices=1)
    arrays, tensors = {}, {}
    for name, a in {**inputs, **_CONSTANTS}.items():
        a = np.ascontiguousarray(a)
        arrays[f"in_{name}"] = a
        tensors[name] = nc.dram_tensor(f"in_{name}", a.shape, mybir.dt.from_np(a.dtype), kind="ExternalInput").ap()
    out = nc.dram_tensor("out_dram", _OUT[0], F32, kind="ExternalOutput").ap()
    build(nc, tensors, out)
    r = run_bass_kernel_spmd(nc, [arrays], core_ids=[0])
    return r.results[0]["out_dram"]
```

```python
from contextlib import ExitStack

import numpy as np

import concourse.bass as bass
from concourse import mybir

F32 = mybir.dt.float32
F32R = mybir.dt.float32r
BF16 = mybir.dt.bfloat16
I32 = mybir.dt.int32
U32 = mybir.dt.uint32
ALU = mybir.AluOpType
ACT = mybir.ActivationFunctionType
AXX = mybir.AxisListType.X

P = 128
B, H, W, C = 8, 32, 64, 128
HP = H // 2
G = 4
L, M = 64, 32
L2 = L // 2
O = 32
RB = 2 * B
MQ = 8
LQ = 4
NCH = L2 // LQ
NTILES = B * HP
E, DFF = 8, 256
EW = 2 * DFF + 2 * C
SLOT_TILES = 40
NG = NTILES // G
HEADS = 8
ATTN_SCALE = 0.125
NP2 = HP // 2
NT = 2 * B
QUARTER = 2 * G * 16
LAG = 3


def spectral_tables():
    nlat = W
    theta = np.pi * (np.arange(nlat) + 0.5) / nlat
    ct, st = np.cos(theta), np.sin(theta)
    p = np.zeros((L, C // 2 + 1, nlat), dtype=np.float64)
    p[0, 0] = 1.0 / np.sqrt(2.0)
    for m in range(L):
        if m > 0:
            p[m, m] = np.sqrt((2.0 * m + 1.0) / (2.0 * m)) * st * p[m - 1, m - 1]
        if m + 1 < L:
            p[m + 1, m] = np.sqrt(2.0 * m + 3.0) * ct * p[m, m]
        for l in range(m + 2, L):
            a = np.sqrt((4.0 * l * l - 1.0) / (l * l - m * m))
            b = np.sqrt((2.0 * l + 1.0) * (l - 1 - m) * (l - 1 + m) / ((2.0 * l - 3.0) * (l * l - m * m)))
            p[l, m] = a * ct * p[l - 1, m] - b * p[l - 2, m]
    weight = (st * np.pi / nlat).astype(np.float32)
    syn = p[:, :M].astype(np.float32)
    ana = syn * weight[None, None, :]
    ana_bd = np.zeros((P, M, P), np.float32)
    syn_bd = np.zeros((P, M, P), np.float32)
    for i in range(2):
        s = slice(i * 64, i * 64 + 64)
        ana_bd[s, :, s] = ana.transpose(2, 1, 0)
        syn_bd[s, :, s] = syn.transpose(0, 1, 2)
    n = np.arange(C)[:, None] * np.arange(M)[None, :] * (2 * np.pi / C)
    fwd = np.concatenate([np.cos(n), -np.sin(n)], 1) * (np.sqrt(2 * np.pi) / C)
    twice = np.where(np.arange(M) == 0, 1.0, 2.0)[None, :]
    inv = np.concatenate([np.cos(n) * twice, -np.sin(n) * twice], 1) / np.sqrt(2 * np.pi)
    inv[:, M] = 0.0
    inv_bd = np.zeros((P, 2 * C), np.float32)
    inv_bd[:64, :C] = inv_bd[64:, C:] = inv.T
    return {
        "identity": np.eye(P, dtype=np.float32),
        "first_rank": np.tile(16.0 - np.arange(16), (P, NT)).astype(np.float32),
        "expert_number": np.tile(np.arange(E), (P, NT)).astype(np.float32),
        "expert_up_to": np.tile(np.tril(np.ones((E, E))).reshape(-1), (P, 1)).astype(np.float32),
        "slot_tile_number": np.tile(np.repeat(np.arange(SLOT_TILES), E), (P, 1)).astype(np.float32),
        "window_first_slot": np.tile(np.arange(NP2) * SLOT_TILES * P, (P, 1)).astype(np.float32),
        "token_before": np.triu(np.ones((P, P)), 1).astype(np.float32),
        "nibble_key": np.tile(np.arange(16) - 16.0, (P, NT)).astype(np.float32),
        "head_mask": np.tile(np.kron(np.eye(HEADS), np.full((C // HEADS,) * 2, ATTN_SCALE / 2)), (1, G)).astype(np.float32),
        "legendre_analysis": ana_bd.reshape(P, M * P),
        "legendre_synthesis": syn_bd.reshape(P, M * P),
        "fourier_forward": fwd.astype(np.float32),
        "fourier_inverse": inv_bd,
    }


def build(nc, t, out):
    with ExitStack() as ctx:
        def sb(name, shape, dt=F32, at=ctx):
            return at.enter_context(nc.sbuf_tensor(name, shape, dt))

        def pb(name, shape, dt=F32, at=ctx):
            return at.enter_context(nc.psum_tensor(name, shape, dt))

        def sem(name):
            return ctx.enter_context(nc.semaphore(name))

        x_sb = sb("x_sb", [P, B * HP, C])
        ident = sb("ident", [P, P])
        minus_half = sb("minus_half", [P, 2 * HP])
        x_view = t["x"].rearrange("b (hp ip) w c -> b (ip w) hp c", ip=2)

        slots = nc.dram_tensor("slots", [B * SLOT_TILES * P, C], F32, kind="Internal").ap()
        spectral_conv(nc, t, sb, pb, sem, x_sb, ident, minus_half, x_view)
        routing = Routing(sb, sem)
        with ExitStack() as a:
            weights = spiking_weights(nc, t, sb, pb, sem, ident, minus_half, a, routing)
            opcode_and_spikes(nc, t, sb, pb, sem, x_sb, ident, minus_half, weights, slots, routing)
        experts(nc, t, sb, pb, sem, x_sb, ident, minus_half, slots, routing, out)


class Routing:

    def __init__(self, sb, sem):
        self.scale = sb("r_scale", [P, NTILES])
        self.shift = sb("r_shift", [P, NTILES])
        self.top = sb("r_top", [P, 2, NTILES])
        self.pos = sb("r_pos", [P, 2, NTILES], U32)
        self.offset = sb("r_offset", [1, LAG + NP2 * SLOT_TILES], I32)
        self.rows = sb("r_rows", [P, 2 * NT * C])
        self.raw = sb("r_raw", [P, E * EW])
        self.index = sb("r_index", [P, 2, 2, G], U32)
        self.bias = sb("r_bias", [3, E * EW], BF16)
        self.braw = sb("r_bias_raw", [5 * E, P])
        self.bpart = sb("r_bias_part", [5 * E, 3, P], BF16)
        self.brest = sb("r_bias_rest", [5 * E, P])
        self.s_braw = sem("bias_raw")
        self.s_bias = sem("bias_rows")
        self.s_raw = sem("f_raw_weights")
        self.s_cp = sem("f_rows_ready")
        self.s_index = sem("f_index")
        self.s_beat = sem("f_beat")
        self.s_sc = [sem("scattering_0"), sem("scattering_1")]
        self.s_scq = sem("scattered")

    def normalise(self, nc, act, x_sb, w, quarter, q):
        tile = quarter * G + q
        at = bass.ds(tile + w * NT, 1)
        place = tile * C + (w % 2) * NT * C
        x_at = quarter * 2 * HP + w * 2 + (q // 2) * HP + q % 2
        ins = nc.scalar.activation(self.rows[:, bass.ds(place, C)], x_sb[:, bass.ds(x_at, 1), :].rearrange("p q c -> p (q c)"),
                                   ACT.Identity, bias=self.shift[:, at], scale=self.scale[:, at])
        if q == G - 1:
            ins.then_inc(self.s_cp, 1)

    def transfers(self, nc, pool, w, turn, s_transfer, move, ready, arrived):
        for quarter in range(4):
            k = quarter % 2
            ready(quarter)
            pool.sem_inc(self.s_beat, 1)
            nc.gpsimd.tensor_copy(self.index[:, k], self.pos[:, :, bass.ds(w * NT + quarter * G, G)]).then_inc(self.s_index, 1)
            pool.wait_ge(self.s_index, turn * 4 + quarter + 1)
            pool.sem_inc(self.s_beat, 1)
            for q in range(G):
                for n in range(2):
                    move(n, quarter * G + q, self.index[:, k, n, q:q + 1]).then_inc(s_transfer[k], 16)
            if quarter:
                pool.wait_ge(s_transfer[1 - k], (w * 2 + (quarter + 1) // 2) * QUARTER)
                arrived()
        pool.wait_ge(s_transfer[1], (w * 2 + 2) * QUARTER)
        arrived()

    def scatter(self, nc, pool, slots, w, slot, turn):
        self.transfers(nc, pool, w, turn, self.s_sc,
                       lambda n, tile, at: nc.gpsimd.indirect_dma_start(
                           slots, bass.IndirectOffsetOnAxis(at, 0),
                           self.rows[:, (slot * NT + tile) * C:(slot * NT + tile + 1) * C], None),
                       lambda quarter: pool.wait_ge(self.s_cp, w * 4 + quarter + 1),
                       lambda: pool.sem_inc(self.s_scq, 1))


class Chain:

    def __init__(self, eng, s, base=0):
        self.eng, self.s, self.n, self.base = eng, s, 0, base

    def link(self, ins):
        self.n += 1
        ins.then_inc(self.s, 1)
        self.eng.wait_ge(self.s, self.base + self.n)


def moments(nc, chain, st, tmp, eps, sign=1.0):
    nc.vector.tensor_tensor(tmp[:, 0, :], st[:, :, 1], st[:, :, 4], ALU.add)
    nc.vector.tensor_tensor(tmp[:, 2, :], st[:, :, 2], st[:, :, 5], ALU.add)
    chain.link(nc.vector.tensor_tensor(tmp[:, 1, :], st[:, :, 1], st[:, :, 4], ALU.subtract))
    nc.vector.tensor_scalar(tmp[:, 0, :], tmp[:, 0, :], 0.5 * sign, None, ALU.mult)
    chain.link(nc.vector.scalar_tensor_tensor(tmp[:, 1, :], tmp[:, 1, :], 0.25, tmp[:, 1, :], ALU.mult, ALU.mult))
    chain.link(nc.vector.scalar_tensor_tensor(tmp[:, 2, :], tmp[:, 2, :], 1.0 / C, tmp[:, 1, :], ALU.mult, ALU.add))
    return nc.vector.tensor_scalar(tmp[:, 2, :], tmp[:, 2, :], eps, None, ALU.add)


def layer_norm_stats(nc, chain, st, tmp, src, n, eps, sign=1.0):
    for q in range(n):
        ins = nc.vector.bn_stats(st[:, q, :], src(q))
    chain.link(ins)
    return moments(nc, chain, st, tmp, eps, sign)


LN_LINKS = 4


def inverse_deviation(nc, tmp, minus_half):
    return nc.gpsimd.tensor_tensor(tmp[:, 3, :], tmp[:, 2, :], minus_half[:, 0:tmp.shape[2]], ALU.pow)


def spectral_conv(nc, t, sb, pb, sem, x_sb, ident, minus_half, x_view):
    spectral_w = [t["L0_conv_w1r"], t["L0_conv_w1i"], t["L0_conv_w2r"], t["L0_conv_w2i"]]
    coef = nc.dram_tensor("coefficients", [2, M // MQ, H, L, MQ * RB], F32, kind="Internal").ap()
    mixed = nc.dram_tensor("mixed", [2, NCH, P, M * 16], F32, kind="Internal").ap()

    with ExitStack() as both:
        wc = sb("wc", [P, 2, O, LQ, M], at=both)
        s_w = [sem("mix_weights_0"), sem("mix_weights_1")]
        w_view = [w.rearrange("i o (k l) m -> k i o (l m)", l=LQ) for w in spectral_w]

        def load_w(eng, chunk, slot):
            for g in range(4):
                src = w_view[g][bass.ds(chunk, 1)] if not isinstance(chunk, int) else w_view[g][chunk:chunk + 1]
                eng.dma_start(wc[32 * g:32 * g + 32, slot].rearrange("i o l m -> i o (l m)"),
                              src.rearrange("k i o f -> (k i) o f")).then_inc(s_w[slot], 16)

        with ExitStack() as a:
            efwd = sb("efwd", [P, 2 * M], at=a)
            pana = sb("pana", [P, M, P], at=a)
            y = sb("y", [P, 2, HP, C], at=a)
            yT = sb("yT", [P, 2, G * P], at=a)
            f_sb = sb("f_sb", [P, M, HP, 2, B], at=a)
            c1 = sb("c1", [P, 2, HP, MQ, RB], at=a)
            c2 = sb("c2", [P, 2, HP, MQ, RB], at=a)
            st = sb("st", [P, 2, HP, 6], at=a)
            tmp = sb("tmp", [P, 2, 4, HP], at=a)
            ps_t = pb("ps_t", [P, 2, G * P], at=a)
            ps_f = pb("ps_f", [P, 2, 2 * G, 2 * M], at=a)
            ps_l = pb("ps_l", [P, 2, 2, 256], at=a)

            s_const = sem("a_constants")
            s_pana = sem("a_legendre_loaded")
            s_x = [sem("x_loaded_0"), sem("x_loaded_1")]
            s_chain = sem("a_vector_chain")
            s_half = sem("a_exponent")
            s_var = sem("a_variance")
            s_rstd = sem("a_inverse_deviation")
            s_y = sem("a_normalised")
            s_tr = sem("a_transposed")
            s_yT = sem("a_channel_major")
            s_dft = sem("a_fourier")
            s_dftfree = sem("a_fourier_bank_free")
            s_leg = sem("a_legendre")
            s_c1 = sem("a_coefficients")
            s_c2 = sem("a_rotated_coefficients")
            s_cw = [sem("coefficients_stored_0"), sem("coefficients_stored_1")]

            with nc.Block() as block:
                @block.sync
                def _(sp):
                    sp.dma_start(ident[:, :], t["identity"]).then_inc(s_const, 16)
                    sp.dma_start(efwd[:, :], t["fourier_forward"]).then_inc(s_const, 16)
                    for b in range(B):
                        if b >= 2:
                            sp.wait_ge(s_x[b % 2], 16 * (b // 2))
                        sp.dma_start(x_sb[:, b * HP:(b + 1) * HP, :], x_view[b]).then_inc(s_x[b % 2], 16)
                    sp.dma_start(pana[:, :, :], t["legendre_analysis"].rearrange("p (m q) -> p m q", m=M)).then_inc(s_pana, 16)
                    load_w(sp, 0, 0)
                    load_w(sp, 1, 1)
                    for mq in range(M // MQ):
                        for v, (c, s) in enumerate(((c1, s_c1), (c2, s_c2))):
                            sp.wait_ge(s, (mq + 1) * (MQ // 2 if v == 0 else 1))
                            sp.dma_start(coef[v, mq].rearrange("(ih ip) l f -> (ip l) ih f", ip=2),
                                         c[:, mq % 2].rearrange("p ih m f -> p ih (m f)")).then_inc(s_cw[mq % 2], 16)
                    for k in range(2):
                        sp.wait_ge(s_cw[k], 64)

                @block.vector
                def _(dve):
                    def statistics(pair, k):
                        b = pair * 2 + k
                        dve.wait_ge(s_x[k], pair * 16 + 16)
                        layer_norm_stats(nc, Chain(dve, s_chain, b * LN_LINKS), st[:, k], tmp[:, k],
                                         lambda q: x_sb[:, bass.ds(b * HP + q, 1), :], HP, 1e-6).then_inc(s_var, 1)

                    def normalise(pair, k):
                        b = pair * 2 + k
                        dve.wait_ge(s_rstd, b + 1)
                        dve.wait_ge(s_tr, b * G + 1)
                        for q in range(HP):
                            ins = nc.vector.tensor_scalar(y[:, k, q, :], x_sb[:, bass.ds(b * HP + q, 1), :],
                                                          tmp[:, k, 0, q:q + 1], tmp[:, k, 3, q:q + 1],
                                                          ALU.subtract, ALU.mult)
                        ins.then_inc(s_y, 1)

                    statistics(0, 0)
                    with dve.Fori(0, B // 2 - 1) as pair:
                        statistics(pair, 1)
                        normalise(pair, 0)
                        statistics(pair + 1, 0)
                        normalise(pair, 1)
                    statistics(B // 2 - 1, 1)
                    normalise(B // 2 - 1, 0)
                    normalise(B // 2 - 1, 1)
                    for mq in range(M // MQ):
                        k = mq % 2
                        dve.wait_ge(s_c1, (mq + 1) * (MQ // 2))
                        if mq >= 2:
                            dve.wait_ge(s_cw[k], 32)
                        a1 = c1[:, k].rearrange("p ih m f -> p (ih m) f")
                        a2 = c2[:, k].rearrange("p ih m f -> p (ih m) f")
                        nc.vector.tensor_scalar(a2[:, :, 0:B], a1[:, :, B:RB], -1.0, None, ALU.mult)
                        nc.vector.tensor_copy(a2[:, :, B:RB], a1[:, :, 0:B]).then_inc(s_c2, 1)

                @block.gpsimd
                def _(pool):
                    nc.gpsimd.memset(minus_half[:, :], -0.5).then_inc(s_half, 1)
                    pool.wait_ge(s_half, 1)
                    with pool.Fori(0, B // 2) as pair:
                        for k in range(2):
                            pool.wait_ge(s_var, pair * 2 + k + 1)
                            inverse_deviation(nc, tmp[:, k], minus_half).then_inc(s_rstd, 1)

                @block.tensor
                def _(pe):
                    pe.sem_inc(s_tr, G + 1)
                    pe.sem_inc(s_dft, 2)
                    pe.wait_ge(s_const, 32)
                    with pe.Fori(0, B // 2) as pair:
                        for k in range(2):
                            g0 = (pair * 2 + k) * G

                            def transposes(g):
                                pe.wait_ge(s_yT, g0 + g + 1)
                                for q in range(G):
                                    ins = nc.tensor.transpose(ps_t[:, g % 2, q * P:(q + 1) * P],
                                                              y[:, k, g * G + q, :], ident[:, :])
                                ins.then_inc(s_tr, 1)

                            def fourier(g):
                                pe.wait_ge(s_yT, g0 + g + 3)
                                if g % 2 == 0:
                                    pe.wait_ge(s_dftfree, (pair * 2 + k) * 2 + g // 2 + 1)
                                for q in range(G):
                                    ins = nc.tensor.matmul(ps_f[:, g // 2, (g % 2) * G + q, :],
                                                           yT[:, g % 2, q * P:(q + 1) * P], efwd[:, :],
                                                           start=True, stop=True)
                                ins.then_inc(s_dft, 1)

                            pe.wait_ge(s_y, pair * 2 + k + 1)
                            for g in range(HP // G):
                                transposes(g)
                                if g:
                                    fourier(g - 1)
                            fourier(HP // G - 1)
                    pe.wait_ge(s_pana, 16)
                    pe.wait_ge(s_dftfree, 2 * B + 2)
                    for m in range(M):
                        if m % 2 == 0 and m >= 4:
                            pe.wait_ge(s_c1, m // 2 - 1)
                        ins = nc.tensor.matmul(ps_l[:, (m // 2) % 2, m % 2, :], pana[:, m, :],
                                               f_sb[:, m].rearrange("p h r b -> p (h r b)"), start=True, stop=True)
                        if m % 2:
                            ins.then_inc(s_leg, 1)

                @block.scalar
                def _(act):
                    act.sem_inc(s_yT, 2)
                    act.sem_inc(s_dftfree, 2)
                    with act.Fori(0, B // 2) as pair:
                        for k in range(2):
                            bb = pair * 2 + k
                            for g in range(HP // G):
                                act.wait_ge(s_tr, bb * G + g + 2 + G)
                                act.wait_ge(s_dft, bb * G + g + 1)
                                nc.scalar.activation(yT[:, g % 2, :], ps_t[:, g % 2, :], ACT.Copy)\
                                    .then_inc(s_yT, 1)
                                if g % 2:
                                    act.wait_ge(s_dft, bb * G + g + 3)
                                    q0 = (g - 1) * G
                                    nc.scalar.activation(
                                        f_sb[:, :, q0:q0 + 2 * G, :, bb].rearrange("p m q r -> p q r m"),
                                        ps_f[:, g // 2].rearrange("p q (r m) -> p q r m", r=2), ACT.Copy)\
                                        .then_inc(s_dftfree, 1)

                    for m2 in range(M // 2):
                        k = (2 * m2 // MQ) % 2
                        act.wait_ge(s_leg, m2 + 1)
                        if 2 * m2 % MQ == 0 and 2 * m2 >= 2 * MQ:
                            act.wait_ge(s_cw[k], 32)
                        ml = 2 * m2 % MQ
                        nc.scalar.activation(c1[:, k, :, ml:ml + 2, :].rearrange("p ih m f -> p m ih f"),
                                             ps_l[:, m2 % 2].rearrange("p m (ih f) -> p m ih f", ih=HP), ACT.Copy)\
                            .then_inc(s_c1, 1)

        with ExitStack() as a:
            coefc = sb("coefc", [P, 2, M // MQ, LQ, MQ, RB], at=a)
            sblk = sb("sblk", [P, 2, LQ, M, 2 * RB], at=a)
            mo = sb("mo", [P, 2, 2, M, 16], at=a)
            ps_m = pb("ps_m", [P, 2, 2, 512], at=a)
            s_cc = [sem("coefficients_loaded_0"), sem("coefficients_loaded_1")]
            s_zero = sem("m_blocks_zeroed")
            s_sd = sem("m_lower_blocks")
            s_sa = sem("m_upper_blocks")
            s_mm = sem("m_mixed")
            s_ed = sem("m_first_orders_out")
            s_ea = sem("m_last_orders_out")
            s_mw = [sem("mixed_stored_0"), sem("mixed_stored_1")]

            def load_coef(eng, chunk, slot):
                for g in range(4):
                    half, part = g // 2, g % 2
                    base = coef[part].rearrange("q i l f -> i q (l f)")
                    off = (half * L2 + chunk * LQ) * MQ * RB
                    eng.dma_start(coefc[32 * g:32 * g + 32, slot].rearrange("i q l m f -> i q (l m f)"),
                                  base[:, :, bass.ds(off, LQ * MQ * RB)]).then_inc(s_cc[slot], 16)

            def store_mixed(eng, chunk, slot):
                eng.wait_ge(s_ed, chunk + 3)
                eng.wait_ge(s_ea, chunk + 3)
                eng.dma_start(mixed[:, bass.ds(chunk, 1)].rearrange("op k p f -> p (op k) f"),
                              mo[:, slot].rearrange("p op m o -> p op (m o)")).then_inc(s_mw[slot], 16)

            with nc.Block() as block:
                @block.sync
                def _(sp):
                    for k in range(2):
                        sp.sem_inc(s_mw[k], 1)
                    load_coef(sp, 0, 0)
                    load_coef(sp, 1, 1)
                    with sp.Fori(1, NCH // 2) as pair:
                        for k in range(2):
                            n = pair * 2 + k
                            sp.wait_ge(s_mm, n + 1)
                            load_w(sp, n, k)
                            sp.wait_ge(s_sd, n - 1)
                            sp.wait_ge(s_sa, n - 1)
                            load_coef(sp, n, k)
                            store_mixed(sp, n - 2, k)
                    for k in range(2):
                        store_mixed(sp, NCH - 2 + k, k)
                    for k in range(2):
                        sp.wait_ge(s_mw[k], 16 * NCH // 2 + 1)

                @block.gpsimd
                def _(pool):
                    nc.gpsimd.memset(sblk[:, 1], 0.0).then_inc(s_zero, 1)

                @block.vector
                def _(dve):
                    dve.sem_inc(s_ed, 2)
                    nc.vector.memset(sblk[:, 0], 0.0).then_inc(s_zero, 1)
                    dve.wait_ge(s_zero, 2)

                    with dve.Fori(0, NCH // 2) as pair:
                        for k in range(2):
                            n = pair * 2 + k
                            dve.wait_ge(s_cc[k], pair * 64 + 64)
                            dve.wait_ge(s_mm, n + 1)
                            for l in range(LQ):
                                ins = nc.vector.tensor_copy(
                                    sblk[0:64, k, l, :, 0:RB].rearrange("p (q m) f -> p q m f", q=M // MQ),
                                    coefc[0:64, k, :, l])
                            ins.then_inc(s_sd, 1)
                            dve.wait_ge(s_mm, n + 3)
                            dve.wait_ge(s_mw[k], pair * 16 + 1)
                            nc.vector.tensor_copy(
                                mo[:, k, :, 0:M // 2, :],
                                ps_m[:, k, 0, :].rearrange("p (m o op) -> p op m o", op=2, o=16))\
                                .then_inc(s_ed, 1)

                @block.scalar
                def _(act):
                    act.sem_inc(s_ea, 2)
                    act.wait_ge(s_zero, 2)
                    with act.Fori(0, NCH // 2) as pair:
                        for k in range(2):
                            n = pair * 2 + k
                            act.wait_ge(s_cc[k], pair * 64 + 64)
                            act.wait_ge(s_mm, n + 1)
                            for l in range(LQ):
                                ins = nc.scalar.activation(
                                    sblk[64:128, k, l, :, RB:2 * RB].rearrange("p (q m) f -> p q m f", q=M // MQ),
                                    coefc[64:128, k, :, l], ACT.Copy)
                            ins.then_inc(s_sa, 1)
                            act.wait_ge(s_mm, n + 3)
                            act.wait_ge(s_mw[k], pair * 16 + 1)
                            nc.scalar.activation(
                                mo[:, k, :, M // 2:M, :],
                                ps_m[:, k, 1, :].rearrange("p (m o op) -> p op m o", op=2, o=16), ACT.Copy)\
                                .then_inc(s_ea, 1)

                @block.tensor
                def _(pe):
                    pe.sem_inc(s_mm, 2)
                    with pe.Fori(0, NCH // 2) as pair:
                        for k in range(2):
                            n = pair * 2 + k
                            pe.wait_ge(s_w[k], pair * 64 + 64)
                            pe.wait_ge(s_sd, n + 1)
                            pe.wait_ge(s_sa, n + 1)
                            pe.wait_ge(s_ed, n + 1)
                            pe.wait_ge(s_ea, n + 1)
                            for l in range(LQ):
                                for m in range(M):
                                    half, col = m // (M // 2), (m % (M // 2)) * O
                                    ins = nc.tensor.matmul(ps_m[32 * l:32 * l + 32, k, half, col:col + O],
                                                           sblk[:, k, l, m, :], wc[:, k, :, l, m],
                                                           start=True, stop=True)
                            ins.then_inc(s_mm, 1)

    with ExitStack() as a:
        psyn = sb("psyn", [P, M, P], at=a)
        einv = sb("einv", [P, 2 * C], at=a)
        gin = sb("gin", [P, M // MQ, RB, MQ, 16], at=a)
        h_sb = sb("h_sb", [P, B, HP, 2, M], at=a)
        hc = sb("hc", [P, 2, HP, 2, M], at=a)
        hT = sb("hT", [P, 2, G * P], at=a)
        ps_g = pb("ps_g", [P, 2, 2, 256], at=a)
        ps_t = pb("ps_t2", [P, 2, G * P], at=a)
        ps_y = pb("ps_y", [P, 2, G, 2 * C], at=a)
        s_const = sem("c_constants")
        s_gin = [sem(f"mixed_loaded_{q}") for q in range(M // MQ)]
        s_leg = sem("c_legendre")
        s_h = [sem("c_orders_even"), sem("c_orders_odd")]
        s_hc = sem("c_batch_copied")
        s_tr = sem("c_transposed")
        s_hT = sem("c_orders_major")
        s_y = sem("c_grid")
        s_yfree = sem("c_grid_bank_free")

        def evacuate(copy, m2):
            return copy(h_sb[:, :, :, :, 2 * m2:2 * m2 + 2].rearrange("p b h r m -> p m r (b h)"),
                        ps_g[:, m2 % 2].rearrange("p m (r bh) -> p m r bh", r=2))

        with nc.Block() as block:
            @block.sync
            def _(sp):
                sp.dma_start(psyn[:, :, :], t["legendre_synthesis"].rearrange("p (m q) -> p m q", m=M)).then_inc(s_const, 16)
                sp.dma_start(einv[:, :], t["fourier_inverse"]).then_inc(s_const, 16)
                for q in range(M // MQ):
                    for op in range(2):
                        for half in range(2):
                            src = mixed[op].rearrange("k (l h r) (q f) -> h q (k l) r f", l=LQ, h=2, q=M // MQ)[half, q]
                            p0 = op * 64 + half * L2
                            sp.dma_start(gin[p0:p0 + L2, q].rearrange("p r m o -> p r (m o)"), src).then_inc(s_gin[q], 16)

            @block.tensor
            def _(pe):
                pe.sem_inc(s_tr, 3)
                pe.sem_inc(s_y, 2)
                pe.wait_ge(s_const, 32)
                for m in range(M):
                    if m % MQ == 0:
                        pe.wait_ge(s_gin[m // MQ], 16 * 4)
                    if m % 2 == 0 and m >= 4:
                        pe.wait_ge(s_h[(m // 2) % 2], m // 4)
                    ins = nc.tensor.matmul(ps_g[:, (m // 2) % 2, m % 2, :], psyn[:, m, :],
                                           gin[:, m // MQ, :, m % MQ, :], start=True, stop=True)
                    if m % 2:
                        ins.then_inc(s_leg, 1)

                with pe.Fori(0, B // 2) as pair:
                    for k in range(2):
                        b = pair * 2 + k

                        def transposes(g):
                            pe.wait_ge(s_hT, b * 2 + g + 1)
                            for q in range(G):
                                t0 = (g * G + q) * 2
                                ins = nc.tensor.transpose(ps_t[:, g % 2, q * P:(q + 1) * P],
                                                          hc[:, k, t0:t0 + 2].rearrange("p q r m -> p (q r m)"), ident[:, :])
                            ins.then_inc(s_tr, 1)

                        def grid(g):
                            pe.wait_ge(s_hT, b * 2 + g + 3)
                            pe.wait_ge(s_yfree, b * 2 + g + 1)
                            for q in range(G):
                                ins = nc.tensor.matmul(ps_y[:, g, q], hT[:, g, q * P:(q + 1) * P], einv[:, :],
                                                       start=True, stop=True)
                            ins.then_inc(s_y, 1)

                        pe.wait_ge(s_hc, b + 1)
                        transposes(0)
                        transposes(1)
                        grid(0)
                        grid(1)

            @block.scalar
            def _(act):
                act.sem_inc(s_hT, 2)
                for m2 in range(0, M // 2, 2):
                    act.wait_ge(s_leg, m2 + 1)
                    evacuate(lambda o, i: nc.scalar.activation(o, i, ACT.Copy), m2).then_inc(s_h[0], 1)
                with act.Fori(0, B // 2) as pair:
                    for k in range(2):
                        for g in range(2):
                            n = (pair * 2 + k) * 2 + g
                            act.wait_ge(s_tr, n + 4)
                            act.wait_ge(s_y, n + 1)
                            nc.scalar.activation(hT[:, g % 2, :], ps_t[:, g % 2, :], ACT.Copy)\
                                .then_inc(s_hT, 1)

            @block.gpsimd
            def _(pool):
                pool.wait_ge(s_h[0], M // 4)
                pool.wait_ge(s_h[1], M // 4)
                with pool.Fori(0, B // 2) as pair:
                    for k in range(2):
                        b = pair * 2 + k
                        pool.wait_ge(s_tr, b * 2 + 1)
                        nc.gpsimd.tensor_copy(hc[:, k], h_sb[:, b]).then_inc(s_hc, 1)

            @block.vector
            def _(dve):
                dve.sem_inc(s_yfree, 2)
                for m2 in range(1, M // 2, 2):
                    dve.wait_ge(s_leg, m2 + 1)
                    evacuate(nc.vector.tensor_copy, m2).then_inc(s_h[1], 1)
                with dve.Fori(0, B // 2) as pair:
                    for k in range(2):
                        for g in range(2):
                            n = (pair * 2 + k) * 2 + g
                            dve.wait_ge(s_y, n + 3)
                            for bank in range(2):
                                rows = x_sb[:, bass.ds(n * 2 * G + bank * G, G), :].rearrange("p q c -> p (q c)")
                                ins = nc.vector.tensor_tensor(
                                    rows, rows, ps_y[:, g, bank * 2:bank * 2 + 2].rearrange("p q c -> p (q c)"), ALU.add)
                            ins.then_inc(s_yfree, 1)


def split3(nc, chain, parts, x, rest):
    chain.link(nc.vector.tensor_copy(parts[0], x))
    chain.link(nc.vector.tensor_tensor(rest, x, parts[0], ALU.subtract))
    chain.link(nc.vector.tensor_copy(parts[1], rest))
    return nc.vector.tensor_tensor(parts[2], rest, parts[1], ALU.subtract)


def spiking_weights(nc, t, sb, pb, sem, ident, minus_half, keep, routing):
    wqkv = sb("wqkv", [P, 3 * C], at=keep)
    wo = sb("wo", [P, 3, C], BF16, at=keep)
    bias = sb("bias", [3, 4 * C], BF16, at=keep)
    ones = sb("ones", [3, P], BF16, at=keep)
    with ExitStack() as a:
        lw = sb("lw", [P, 4, C], at=a)
        par = sb("par", [P, 5, 4], at=a)
        col = sb("col", [P, 3, 4], at=a)
        bpart = sb("bpart", [P, 4, 3], at=a)
        bhalf = sb("bhalf", [P, 3, 4], BF16, at=a)
        rest = sb("rest", [P, C], at=a)
        rest4 = sb("rest4", [P, 4], at=a)
        ps_w = pb("ps_w", [P, 4 * C], at=a)
        ps_b = pb("ps_b", [3, 4 * C], at=a)
        s_load = sem("w_loaded")
        s_chain = sem("w_chain")
        s_var = sem("w_variance")
        s_rstd = sem("w_inverse_deviation")
        s_scaled = sem("w_scaled")
        s_t = sem("w_transposed")

        with nc.Block() as block:
            @block.sync
            def _(sp):
                sp.dma_start(lw[:, :, :], t["L1_conv_lin_w"].rearrange("i d c -> d i c")).then_inc(s_load, 16)
                for n, name in enumerate(("lin_b", "bn_g", "bn_b", "bn_m", "bn_v")):
                    with nc.allow_non_contiguous_dma(reason="512 parameters, once"):
                        sp.dma_start(par[:, n, :], t[f"L1_conv_{name}"].rearrange("i d -> d i")).then_inc(s_load, 16)
                for k in range(4):
                    sp.dma_start(routing.braw[k * E:(k + 1) * E, :], t["L1_ffn_b1"][:, k * P:(k + 1) * P]).then_inc(routing.s_braw, 16)
                sp.dma_start(routing.braw[4 * E:5 * E, :], t["L1_ffn_b2"]).then_inc(routing.s_braw, 16)

            @block.gpsimd
            def _(pool):
                pool.wait_ge(s_var, 1)
                nc.gpsimd.tensor_tensor(col[:, 0, :], col[:, 0, :], minus_half[:, 0:4], ALU.pow).then_inc(s_rstd, 1)

            @block.vector
            def _(dve):
                chain = Chain(dve, s_chain)
                dve.wait_ge(s_load, 96)
                nc.vector.memset(ones[:, :], 1.0)
                nc.vector.tensor_scalar(col[:, 0, :], par[:, 4, :], 1e-5, None, ALU.add).then_inc(s_var, 1)
                dve.wait_ge(s_rstd, 1)
                nc.vector.tensor_tensor(col[:, 1, :], par[:, 1, :], col[:, 0, :], ALU.mult)
                chain.link(nc.vector.tensor_tensor(col[:, 2, :], par[:, 0, :], par[:, 3, :], ALU.subtract))
                chain.link(nc.vector.tensor_tensor(col[:, 2, :], col[:, 2, :], col[:, 1, :], ALU.mult))
                chain.link(nc.vector.tensor_tensor(col[:, 2, :], col[:, 2, :], par[:, 2, :], ALU.add))
                chain.link(nc.vector.tensor_scalar(col[:, 2, :], col[:, 2, :], 0.5, None, ALU.mult))
                for i in range(4):
                    ins = nc.vector.tensor_scalar(lw[:, i, :], lw[:, i, :], col[:, 1, i:i + 1], 0.5, ALU.mult, ALU.mult)
                chain.link(ins)
                chain.link(split3(nc, chain, [bhalf[:, n, :] for n in range(3)], col[:, 2, :], rest4[:, :]))
                nc.vector.tensor_copy(bpart[:, :, :].rearrange("p i n -> p n i"), bhalf[:, :, :]).then_inc(s_scaled, 1)
                dve.wait_ge(routing.s_braw, 5 * 16)
                chain.link(split3(nc, chain, [routing.bpart[:, n, :] for n in range(3)], routing.braw[:, :], routing.brest[:, :]))
                dve.wait_ge(s_t, 1)
                nc.vector.tensor_copy(wqkv[:, :], ps_w[:, 0:3 * C])
                nc.vector.tensor_copy(bias[:, :], ps_b[:, :])
                split3(nc, chain, [wo[:, n, :] for n in range(3)], ps_w[:, 3 * C:4 * C], rest[:, :])

            @block.tensor
            def _(pe):
                pe.wait_ge(s_scaled, 1)
                for i in range(4):
                    nc.tensor.transpose(ps_w[:, i * C:(i + 1) * C], lw[:, i, :], ident[:, :])
                for i in range(4):
                    ins = nc.tensor.transpose(ps_b[:, i * C:(i + 1) * C], bpart[:, i, :], ident[:, :])
                ins.then_inc(s_t, 1)
    return wqkv, wo, bias, ones


def opcode_and_spikes(nc, t, sb, pb, sem, x_sb, ident, minus_half, weights, slots, routing):
    wqkv, wo, bias, ones = weights
    xv = x_sb[:, :, :].rearrange("p (b i j) c -> p b i j c", b=B, j=2)
    with ExitStack() as a:
        rank = sb("rank", [P, NT, 16], at=a)
        key = sb("key", [P, NT, 16], at=a)
        mask = sb("mask", [P, G * C], at=a)
        st = sb("e_st", [P, NT, 6], at=a)
        st2 = sb("e_st2", [P, NT, 6], at=a)
        tmp = sb("e_tmp", [P, 2, 4, NT], at=a)
        u = sb("u", [P, NT, C], at=a)
        win = sb("win", [P, 3, NT, 16], at=a)
        first = sb("first", [P, 3, NT], at=a)
        fl = sb("fl", [P, 4, NT], at=a)
        ints = sb("ints", [P, 10, NT], I32, at=a)
        flt = sb("flt", [P, 4, NT], at=a)
        eq = sb("eq", [P, 2, NT, 16], at=a)
        z = sb("z", [P, NT, C], at=a)
        zT = sb("zT", [P, NT, P], at=a)
        v1 = sb("v1", [P, 2, 2, 3 * C], at=a)
        r1 = sb("r1", [P, 2, 3 * C], at=a)
        spk = sb("spk", [P, B, 2, 3 * C], BF16, at=a)
        kvm = sb("kvm", [P, 2, 2, G * C], BF16, at=a)
        vo = sb("vo", [P, 2, 2 * P], at=a)
        ro = sb("ro", [P, 2 * P], at=a)
        so = sb("so", [P, 2, 2 * P], BF16, at=a)
        vy = sb("vy", [P, 2, C], at=a)
        ry = sb("ry", [P, 2, C], at=a)
        ps_q = pb("ps_q", [P, 2, 2, 512], at=a)
        ps_kv = pb("ps_kv", [P, 2, G * C], at=a)
        ps_o = pb("ps_o", [P, 512], at=a)
        ps_y = pb("ps_y2", [P, 512], at=a)

        zero = sb("zero", [P, C], at=a)
        wg = sb("wg", [P, E], at=a)
        bg = sb("bg", [P, E], at=a)
        num = sb("num", [P, NT, E], at=a)
        upto = sb("upto", [P, E, E], at=a)
        slot_no = sb("slot_no", [P, SLOT_TILES, E], at=a)
        first_slot = sb("first_slot", [P, NP2], at=a)
        before_f = sb("before_f", [P, P], at=a)
        before = sb("before", [P, P], BF16, at=a)
        every = sb("every", [P, P], BF16, at=a)
        r_st = sb("r_st", [P, NT, 6], at=a)
        r_tmp = sb("r_tmp", [P, 4, NT], at=a)
        r_y = routing.rows[:, NT * C:].rearrange("p (q c) -> p q c", c=C)
        lg = sb("lg", [P, NT, E], at=a)
        pick = sb("pick", [P, 2, NT, E], at=a)
        low = sb("low", [P, NT, E], at=a)
        chosen = sb("chosen", [P, NT + 1, E], BF16, at=a)
        lead = sb("lead", [P, NT], at=a)
        cnt = sb("cnt", [P, 2, E], I32, at=a)
        base = sb("base", [P, 3, E], at=a)
        prod = sb("prod", [P, E, E], at=a)
        place = sb("place", [P, NT, E], at=a)
        pp = sb("pp", [P, 2, NT, E], at=a)
        ppr = sb("ppr", [P, 2, NT], at=a)
        past = sb("past", [1, SLOT_TILES, E], at=a)
        pastr = sb("pastr", [1, SLOT_TILES], at=a)
        ps_log, ps_rank = ps_q[:, 0, 0, 0:NT * E], ps_q[:, 1, 0, 0:(NT + 1) * E]
        s_reset = sem("e_reset")
        s_rchain = sem("r_chain")
        s_rvar = sem("r_variance")
        s_rrstd = sem("r_inverse_deviation")
        s_rn = sem("r_scale_shift")
        s_ry = sem("r_normalised")
        s_rt = sem("r_transposed")
        s_rz = sem("r_channel_major")
        s_lg = sem("r_logits")
        s_ch = sem("r_chosen")
        s_rk = sem("r_ranked")
        s_placed = sem("r_placed")
        s_set = sem("r_constants_set")
        s_zero = sem("e_zero")
        s_clear = sem("slots_cleared")
        s_const = sem("e_constants")
        s_chain = sem("e_chain")
        s_schain = sem("e_statistics_chain")
        s_var = sem("e_variance")
        s_rstd = sem("e_inverse_deviation")
        s_u = sem("e_ffn_rows")
        s_var2 = sem("e_variance_2")
        s_rstd2 = sem("e_inverse_deviation_2")
        s_beat = sem("e_beat")
        s_z = sem("e_normalised")
        s_tr = sem("e_transposed")
        s_zT = sem("e_channel_major")
        s_qkv = sem("e_projected")
        s_v = sem("e_membranes")
        s_spk = sem("e_spikes")
        s_kv = sem("e_key_values")
        s_kvm = sem("e_key_values_masked")
        s_o = sem("e_attended")
        s_vo = sem("e_attended_membranes")
        s_so = sem("e_attended_spikes")
        s_y = sem("e_output_projected")
        s_vy = sem("e_output_membranes")

        FLAG_LINKS, SHIFT_LINKS, ADD_LINKS = 5, 8, 3
        FFN_LINKS = FLAG_LINKS + SHIFT_LINKS + ADD_LINKS
        PREP_LINKS = FFN_LINKS + LN_LINKS

        def statistics(dve, i):
            chain = Chain(dve, s_schain, i * LN_LINKS)
            layer_norm_stats(nc, chain, st, tmp[:, 0], lambda q: xv[:, q // 2, i, q % 2, :], NT, 1e-5, -1.0).then_inc(s_var, 1)

        def tile(i):
            return lambda q: xv[:, q // 2, i, q % 2, :]

        def rows_of(act, i, out, n):
            for q in range(NT):
                ins = nc.scalar.activation(out[:, q, :], tile(i)(q), ACT.Identity,
                                           bias=tmp[:, n, 1, q:q + 1], scale=tmp[:, n, 3, q:q + 1])
            return ins

        def ffn_rows(act, i):
            act.wait_ge(s_rstd, i * 2 + 2)
            rows_of(act, i, u, 0).then_inc(s_u, 1)

        def z_rows(act, i):
            act.wait_ge(s_rstd2, i * 2 + 2)
            rows_of(act, i, z, 1).then_inc(s_z, 1)

        def ffn_flags(dve, i):
            chain = Chain(dve, s_chain, i * PREP_LINKS)
            dve.wait_ge(s_u, i + 1)
            nc.vector.tensor_scalar(fl[:, 0, :], u[:, :, 0], 0.5, None, ALU.is_gt)
            for n, lo in enumerate((16, 20, 24)):
                ins = nc.vector.scalar_tensor_tensor(win[:, n], u[:, :, lo:lo + 16], 0.5, rank[:, :, :], ALU.is_gt, ALU.mult)
            chain.link(ins)
            nc.vector.tensor_reduce(first[:, :, :], win[:, :, :, :], AXX, ALU.max)
            nc.vector.scalar_tensor_tensor(fl[:, 1, :], u[:, :, 39], 0.5, fl[:, 0, :], ALU.is_gt, ALU.mult)
            chain.link(nc.vector.scalar_tensor_tensor(fl[:, 2, :], u[:, :, 39], 0.5, fl[:, 0, :], ALU.is_le, ALU.mult))
            chain.link(nc.vector.scalar_tensor_tensor(fl[:, 2, :], u[:, :, 40], 0.5, fl[:, 2, :], ALU.is_gt, ALU.mult))
            chain.link(nc.vector.tensor_scalar(ints[:, 0:3, :], first[:, :, :], -1.0, 16.0, ALU.mult, ALU.add))
            nc.vector.tensor_tensor(fl[:, 3, :], fl[:, 1, :], fl[:, 2, :], ALU.add)
            chain.link(nc.vector.tensor_scalar(ints[:, 0:3, :], ints[:, 0:3, :], 15, None, ALU.bitwise_and))
            assert chain.n == FLAG_LINKS

        def ffn_shift(dve, i):
            chain = Chain(dve, s_chain, i * PREP_LINKS + FLAG_LINKS)
            lo, hi, sa, val, shl, shr, res, rlo, rhi = (ints[:, n, :] for n in range(9))
            chain.link(nc.vector.scalar_tensor_tensor(val, hi, 4, lo, ALU.logical_shift_left, ALU.bitwise_or))
            nc.vector.tensor_tensor(shr, val, sa, ALU.logical_shift_right)
            chain.link(nc.vector.tensor_tensor(shl, val, sa, ALU.logical_shift_left))
            chain.link(nc.vector.tensor_scalar(shl, shl, 255, None, ALU.bitwise_and))
            nc.vector.tensor_tensor(flt[:, 0, :], shl, fl[:, 1, :], ALU.mult)
            chain.link(nc.vector.tensor_tensor(flt[:, 1, :], shr, fl[:, 2, :], ALU.mult))
            chain.link(nc.vector.tensor_tensor(res, flt[:, 0, :], flt[:, 1, :], ALU.add))
            nc.vector.tensor_scalar(rlo, res, 15, None, ALU.bitwise_and)
            chain.link(nc.vector.tensor_scalar(rhi, res, 4, None, ALU.logical_shift_right))
            nc.vector.scalar_tensor_tensor(flt[:, 2, :], fl[:, 3, :], -16.0, rlo, ALU.mult, ALU.add)
            chain.link(nc.vector.scalar_tensor_tensor(flt[:, 3, :], fl[:, 3, :], -16.0, rhi, ALU.mult, ALU.add))
            for n in range(2):
                ins = nc.vector.tensor_tensor(eq[:, n], key[:, :, :], flt[:, 2 + n, :].unsqueeze(2).broadcast_to([P, NT, 16]),
                                              ALU.is_equal)
            chain.link(ins)
            assert chain.n == SHIFT_LINKS

        def ffn_add(dve, i):
            chain = Chain(dve, s_chain, i * PREP_LINKS + FFN_LINKS - ADD_LINKS)
            for n, lo in enumerate((32, 36)):
                part = u[:, :, lo:lo + 16]
                chain.link(nc.vector.scalar_tensor_tensor(part, eq[:, n], 2.0, part, ALU.mult, ALU.add))
            rows = xv[:, :, i, :, :]
            chain.link(nc.vector.tensor_tensor(rows, rows, u[:, :, :].rearrange("p (b j) c -> p b j c", j=2), ALU.add))
            assert chain.n == ADD_LINKS

        def z_statistics(dve, i):
            chain = Chain(dve, s_chain, i * PREP_LINKS + FFN_LINKS)
            dve.sem_inc(s_beat, 1)
            layer_norm_stats(nc, chain, st2, tmp[:, 1], tile(i), NT, 1e-6, -1.0).then_inc(s_var2, 1)

        R_LINKS = LN_LINKS + 21

        def route_stats(dve, v):
            chain = Chain(dve, s_rchain, v * R_LINKS + 1)
            dve.wait_ge(s_reset, v * (3 * B) + 3 * B)
            layer_norm_stats(nc, chain, r_st, r_tmp, lambda q: xv[:, q // 2, v, q % 2, :], NT, 1e-5).then_inc(s_rvar, 1)

        def route_scale(dve, v):
            dve.wait_ge(s_rrstd, v + 1)
            at = bass.ds(v * NT, NT)
            nc.vector.tensor_copy(routing.scale[:, at], r_tmp[:, 3, :])
            nc.vector.scalar_tensor_tensor(routing.shift[:, at], r_tmp[:, 0, :], -1.0, r_tmp[:, 3, :], ALU.mult, ALU.mult)\
                .then_inc(s_rn, 1)

        def route_choose(dve, v):
            chain = Chain(dve, s_rchain, v * R_LINKS + 1 + LN_LINKS)
            dve.wait_ge(s_lg, v + 1)
            wide = lambda x: x.unsqueeze(2).broadcast_to([P, NT, E])
            chain.link(nc.vector.tensor_tensor(lg[:, :, :], ps_log.rearrange("p (q e) -> p q e", e=E),
                                               bg[:, :].unsqueeze(1).broadcast_to([P, NT, E]), ALU.add))

            def largest(n):
                val = routing.top[:, n, bass.ds(v * NT, NT)]
                chain.link(nc.vector.tensor_reduce(val, lg[:, :, :], AXX, ALU.max))
                chain.link(nc.vector.tensor_tensor(low[:, :, :], lg[:, :, :], wide(val), ALU.is_lt))
                chain.link(nc.vector.scalar_tensor_tensor(low[:, :, :], low[:, :, :], float(E), num[:, :, :], ALU.mult, ALU.add))
                chain.link(nc.vector.tensor_reduce(lead[:, :], low[:, :, :], AXX, ALU.min))
                chain.link(nc.vector.tensor_tensor(pick[:, n], num[:, :, :], wide(lead[:, :]), ALU.is_equal))

            largest(0)
            chain.link(nc.vector.scalar_tensor_tensor(lg[:, :, :], pick[:, 0], -3e38, lg[:, :, :], ALU.mult, ALU.add))
            largest(1)
            nc.vector.tensor_tensor(chosen[:, 0:NT, :], pick[:, 0], pick[:, 1], ALU.add).then_inc(s_ch, 1)
            assert chain.n == 12, chain.n

        def route_place(dve, v):
            chain = Chain(dve, s_rchain, v * R_LINKS + 1 + LN_LINKS + 12)
            dve.wait_ge(s_rk, v + 1)
            chain.link(nc.vector.tensor_scalar(cnt[:, 0], ps_rank[:, NT * E:], float(P - 1), None, ALU.add))
            chain.link(nc.vector.tensor_scalar(cnt[:, 1], cnt[:, 0], 7, None, ALU.logical_shift_right))
            chain.link(nc.vector.tensor_tensor(prod[:, :, :], upto[:, :, :], cnt[:, 1].unsqueeze(1).broadcast_to([P, E, E]), ALU.mult))
            chain.link(nc.vector.tensor_reduce(base[:, 0], prod[:, :, :], AXX, ALU.add))
            nc.vector.tensor_tensor(past[:, :, :], slot_no[0:1, :, :], base[0:1, 0].unsqueeze(1).broadcast_to([1, SLOT_TILES, E]), ALU.is_ge)
            chain.link(nc.vector.tensor_tensor(base[:, 1], base[:, 0], cnt[:, 1], ALU.subtract))
            nc.vector.tensor_reduce(pastr[:, :], past[:, :, :], AXX, ALU.add)
            chain.link(nc.vector.scalar_tensor_tensor(base[:, 2], base[:, 1], float(P), first_slot[:, bass.ds(v, 1)].broadcast_to([P, E]), ALU.mult, ALU.add))
            nc.vector.tensor_scalar(routing.offset[:, bass.ds(v * SLOT_TILES + LAG, SLOT_TILES)], pastr[:, :], float(E - 1), float(EW), ALU.min, ALU.mult)
            chain.link(nc.vector.tensor_tensor(place[:, :, :], ps_rank[:, 0:NT * E].rearrange("p (q e) -> p q e", e=E),
                                               base[:, 2].unsqueeze(1).broadcast_to([P, NT, E]), ALU.add))
            dve.sem_inc(s_placed, 1)
            for n in range(2):
                ins = nc.vector.tensor_tensor(pp[:, n], pick[:, n], place[:, :, :], ALU.mult)
            chain.link(ins)
            chain.link(nc.vector.tensor_reduce(ppr[:, :, :], pp[:, :, :, :], AXX, ALU.add))
            nc.vector.tensor_copy(routing.pos[:, :, bass.ds(v * NT, NT)], ppr[:, :, :])
            assert chain.n == 9, chain.n

        def route_turn(pe, v, i, g):
            if g == 0:
                pe.wait_ge(s_ry, v + 1)
                pe.wait_ge(s_v, i * B + B + 1)
            for q in range(G):
                ins = nc.tensor.transpose(ps_q[:, g // 2, g % 2, q * P:(q + 1) * P], r_y[:, g * G + q, :], ident[:, :])
            ins.then_inc(s_rt, 1)

        def route_logits(pe, v):
            pe.wait_ge(s_rz, v * 4 + 4)
            for q in range(NT):
                ins = nc.tensor.matmul(ps_log[:, q * E:(q + 1) * E], zT[:, q, :], wg[:, :], start=True, stop=True)
            ins.then_inc(s_lg, 1)

        def route_rank(pe, v):
            pe.wait_ge(s_ch, v + 1)
            nc.tensor.matmul(ps_rank, before[:, :], chosen[:, :, :].rearrange("p q e -> p (q e)"), start=True, stop=False)
            for d in range(1, NT + 1):
                ins = nc.tensor.matmul(ps_rank[:, d * E:], every[:, :],
                                       chosen[:, 0:NT + 1 - d, :].rearrange("p q e -> p (q e)"), start=False, stop=(d == NT))
            ins.then_inc(s_rk, 1)

        def route_rows(act, v):
            act.wait_ge(s_rn, v + 1)
            for q in range(NT):
                at = bass.ds(v * NT + q, 1)
                ins = nc.scalar.activation(r_y[:, q, :], xv[:, q // 2, v, q % 2, :], ACT.Identity,
                                           bias=routing.shift[:, at], scale=routing.scale[:, at])
            ins.then_inc(s_ry, 1)

        def route_major(act, v):
            for g in range(4):
                act.wait_ge(s_rt, v * 4 + g + 1)
                nc.scalar.activation(zT[:, g * G:(g + 1) * G, :].rearrange("p q k -> p (q k)"),
                                     ps_q[:, g // 2, g % 2, :], ACT.Copy).then_inc(s_rz, 1)


        def neurons(dve, i, ahead=None, statistics_of=None, route=None):
            resets = [i * (3 * B)]

            def reset(ins):
                resets.append(1)
                ins.then_inc(s_reset, 1)

            def resets_done(n):
                dve.wait_ge(s_reset, resets[0] + n)

            if route is not None:
                route_stats(dve, route)
            for b in range(B):
                if ahead is not None:
                    if b == 0:
                        ffn_flags(dve, ahead)
                    elif b == 1:
                        ffn_shift(dve, ahead)
                    elif b == 4:
                        ffn_add(dve, ahead)
                if route is not None and b == 0:
                    route_scale(dve, route)
                dve.wait_ge(s_qkv, i * B + b + 1 + 1)
                dve.wait_ge(s_spk, i * B + max(b - 1, 0) + 1)
                src = ps_q[:, b % 2, :, 0:3 * C]
                if b == 0:
                    nc.vector.tensor_copy(v1[:, 0], src).then_inc(s_v, 1)
                else:
                    resets_done(b)
                    nc.vector.scalar_tensor_tensor(v1[:, b % 2], r1[:, :, :], 0.5, src, ALU.mult, ALU.add).then_inc(s_v, 1)
                dve.wait_ge(s_v, i * B + b + 1 + 1)
                reset(nc.vector.scalar_tensor_tensor(r1[:, :, :], v1[:, b % 2], 1.0, v1[:, b % 2], ALU.is_lt, ALU.mult))

            def masked(bp):
                dve.wait_ge(s_kv, i * 4 + bp + 1 + 1)
                dve.wait_ge(s_o, i * B + max(2 * bp - 2, 0) + 1)
                for ip in range(2):
                    ins = nc.vector.tensor_tensor(kvm[:, bp % 2, ip], ps_kv[:, ip], mask[:, :], ALU.mult)
                ins.then_inc(s_kvm, 1)

            def attended(b):
                dve.wait_ge(s_o, i * B + b + 1 + 1)
                dve.wait_ge(s_so, i * B + max(b - 1, 0) + 1)
                if b == 0:
                    nc.vector.tensor_copy(vo[:, 0], ps_o[:, 0:2 * P]).then_inc(s_vo, 1)
                else:
                    resets_done(B + max(2 * b - 2, 1))
                    nc.vector.scalar_tensor_tensor(vo[:, b % 2], ro[:, :], 0.5, ps_o[:, 0:2 * P], ALU.mult, ALU.add)\
                        .then_inc(s_vo, 1)
                dve.wait_ge(s_vo, i * B + b + 1 + 1)
                reset(nc.vector.scalar_tensor_tensor(ro[:, :], vo[:, b % 2], 0.5, vo[:, b % 2], ALU.is_lt, ALU.mult))

            def output(b):
                dve.wait_ge(s_y, i * B + b + 1 + 1)
                src = ps_y[:, 0:2 * C].rearrange("p (j c) -> p j c", j=2)
                if b == 0:
                    nc.vector.tensor_copy(vy[:, :, :], src).then_inc(s_vy, 1)
                else:
                    resets_done(B + 2 * b + 1)
                    nc.vector.scalar_tensor_tensor(vy[:, :, :], ry[:, :, :], 0.5, src, ALU.mult, ALU.add).then_inc(s_vy, 1)
                dve.wait_ge(s_vy, i * B + b + 1 + 1)
                rows = xv[:, b, i, :, :]
                nc.vector.scalar_tensor_tensor(rows, vy[:, :, :], 1.0, rows, ALU.is_ge, ALU.add)
                reset(nc.vector.scalar_tensor_tensor(ry[:, :, :], vy[:, :, :], 1.0, vy[:, :, :], ALU.is_lt, ALU.mult))

            if ahead is not None:
                z_statistics(dve, ahead)
            masked(0)
            for b in range(B):
                if b % 2 == 0 and b // 2 + 1 < 4:
                    masked(b // 2 + 1)
                attended(b)
                if b:
                    output(b - 1)
                if statistics_of is not None and b == 2:
                    statistics(dve, statistics_of)
                if route is not None and b == 6:
                    route_choose(dve, route)
            output(B - 1)
            if route is not None:
                route_place(dve, route)
            assert len(resets) == 1 + 3 * B

        def project(pe, i):
            for b in range(B):
                if b < 2:
                    pe.wait_ge(s_zT, i * 4 + 2 * b + 2 + 1)
                else:
                    if b == 2:
                        pe.wait_ge(s_zT, i * 4 + 4 + 1)
                    pe.wait_ge(s_v, i * B + b - 1 + 1)
                for j in range(2):
                    q = 2 * b + j
                    dst = ps_q[:, b % 2, j]
                    nc.tensor.matmul(dst[:, 0:P], wqkv[:, 0:C], zT[:, q, :], start=True, stop=False)
                    nc.tensor.matmul(dst[:, 0:P], bias[:, 0:C], ones[:, :], start=False, stop=True)
                    nc.tensor.matmul(dst[:, P:3 * P], zT[:, q, :], wqkv[:, C:3 * C], start=True, stop=False)
                    ins = nc.tensor.matmul(dst[:, P:3 * P], ones[:, :], bias[:, C:3 * C], start=False, stop=True)
                ins.then_inc(s_qkv, 1)

        def attend(pe, i, beside=None):
            def key_values(bp):
                pe.wait_ge(s_spk, i * B + 2 * bp + 2 + 1)
                pe.wait_ge(s_kvm, i * 4 + bp + 1)
                for n in range(4):
                    b, j = 2 * bp + n // 2, n % 2
                    for ip in range(2):
                        rows = slice(64 * ip, 64 * ip + 64)
                        ins = nc.tensor.matmul(ps_kv[:, ip, n * C:(n + 1) * C], spk[rows, b, j, C:2 * C],
                                               spk[rows, b, j, 2 * C:3 * C], start=True, stop=True)
                ins.then_inc(s_kv, 1)

            def attended(b):
                pe.wait_ge(s_kvm, i * 4 + b // 2 + 1 + 1)
                pe.wait_ge(s_vo, i * B + b + 1)
                for j in range(2):
                    for ip in range(2):
                        n = (b % 2) * 2 + j
                        ins = nc.tensor.matmul(ps_o[:, j * P + ip * 64:j * P + ip * 64 + 64],
                                               kvm[:, (b // 2) % 2, ip, n * C:(n + 1) * C],
                                               spk[:, b, j, ip * 64:ip * 64 + 64], start=True, stop=True)
                ins.then_inc(s_o, 1)

            def output(b):
                pe.wait_ge(s_so, i * B + b + 1 + 1)
                pe.wait_ge(s_vy, i * B + b + 1)
                for j in range(2):
                    for n in range(3):
                        nc.tensor.matmul(ps_y[:, j * C:(j + 1) * C], so[:, b % 2, j * P:(j + 1) * P], wo[:, n, :],
                                         start=(n == 0), stop=False)
                    ins = nc.tensor.matmul(ps_y[:, j * C:(j + 1) * C], ones[:, :], bias[:, 3 * C:4 * C],
                                           start=False, stop=True)
                ins.then_inc(s_y, 1)

            key_values(0)
            for b in range(B):
                if b % 2 == 0 and b // 2 + 1 < 4:
                    key_values(b // 2 + 1)
                attended(b)
                if b:
                    output(b - 1)
                if beside is not None:
                    if b < 4:
                        route_turn(pe, beside, i, b)
                    elif b == 5:
                        route_logits(pe, beside)
                    elif b == 7:
                        route_rank(pe, beside)
            output(B - 1)

        def turn(pe, i):
            pe.wait_ge(s_z, i + 1 + 1)
            if not isinstance(i, int):
                pe.wait_ge(s_placed, i)
            pe.wait_ge(s_v, i * B + 1)
            for g in range(4):
                for q in range(G):
                    ins = nc.tensor.transpose(ps_q[:, g // 2, g % 2, q * P:(q + 1) * P], z[:, g * G + q, :], ident[:, :])
                ins.then_inc(s_tr, 1)

        def fire(pool, i, ahead=None):
            for b in range(B):
                pool.wait_ge(s_v, i * B + b + 1 + 1)
                if b == 0:
                    pool.wait_ge(s_o, i * B + 1)
                pool.sem_inc(s_beat, 1)
                nc.gpsimd.tensor_scalar(spk[:, b], v1[:, b % 2], 1.0, None, ALU.is_ge).then_inc(s_spk, 1)
            if ahead is not None:
                deviation_2(pool, ahead)
            for b in range(B):
                pool.wait_ge(s_vo, i * B + b + 1 + 1)
                pool.wait_ge(s_y, i * B + max(b - 1, 0) + 1)
                pool.sem_inc(s_beat, 1)
                nc.gpsimd.tensor_scalar(so[:, b % 2], vo[:, b % 2], 0.5, None, ALU.is_ge).then_inc(s_so, 1)

        def scale_shift(pool, n, s, i):
            inverse_deviation(nc, tmp[:, n], minus_half).then_inc(s, 1)
            pool.wait_ge(s, i * 2 + 1)
            nc.gpsimd.tensor_tensor(tmp[:, n, 1, :], tmp[:, n, 0, :], tmp[:, n, 3, :], ALU.mult).then_inc(s, 1)

        def deviation(pool, i):
            pool.wait_ge(s_var, i + 1)
            scale_shift(pool, 0, s_rstd, i)

        def deviation_2(pool, i):
            pool.wait_ge(s_var2, i + 1)
            scale_shift(pool, 1, s_rstd2, i)

        with nc.Block() as block:
            @block.sync
            def _(sp):
                sp.dma_start(rank[:, :, :], t["first_rank"].rearrange("p (q k) -> p q k", k=16)).then_inc(s_const, 16)
                sp.dma_start(key[:, :, :], t["nibble_key"].rearrange("p (q k) -> p q k", k=16)).then_inc(s_const, 16)
                sp.dma_start(mask[:, :], t["head_mask"]).then_inc(s_const, 16)
                sp.dma_start(wg[:, :], t["L1_ffn_Wg"]).then_inc(s_const, 16)
                sp.dma_start(bg[:, :], t["L1_ffn_bg"].rearrange("(a e) -> a e", a=1).broadcast_to([P, E])).then_inc(s_const, 16)
                sp.dma_start(num[:, :, :], t["expert_number"].rearrange("p (q e) -> p q e", e=E)).then_inc(s_const, 16)
                sp.dma_start(upto[:, :, :], t["expert_up_to"].rearrange("p (q e) -> p q e", e=E)).then_inc(s_const, 16)
                sp.dma_start(slot_no[:, :, :], t["slot_tile_number"].rearrange("p (q e) -> p q e", e=E)).then_inc(s_const, 16)
                sp.dma_start(first_slot[:, :], t["window_first_slot"]).then_inc(s_const, 16)
                sp.dma_start(before_f[:, :], t["token_before"]).then_inc(s_const, 16)
                sp.wait_ge(s_zero, 1)
                for w in range(NP2):
                    sp.dma_start(slots.rearrange("(w q p) c -> w p q c", w=NP2, p=P)[w],
                                 zero[:, :].unsqueeze(1).broadcast_to([P, SLOT_TILES, C])).then_inc(s_clear, 16)
                bias_rows = routing.bias[:, :].rearrange("p (e k f) -> p e k f", e=E, f=P)
                for n in range(3):
                    for k in range(5):
                        sp.dma_start(bias_rows[n:n + 1, :, k, :], routing.bpart[k * E:(k + 1) * E, n, :])\
                            .then_inc(routing.s_bias, 16)
                raw = routing.raw[:, :].rearrange("p (e f) -> p e f", e=E)
                sp.dma_start(raw[:, :, 0:2 * DFF], t["L1_ffn_W1"].rearrange("e c f -> c e f")).then_inc(routing.s_raw, 16)
                for k in range(2):
                    at = 2 * DFF + k * C
                    sp.dma_start(raw[:, :, at:at + C],
                                 t["L1_ffn_W2"][:, k * P:(k + 1) * P, :].rearrange("e f c -> f e c")).then_inc(routing.s_raw, 16)
                sp.wait_ge(s_clear, 16 * NP2)

            @block.vector
            def _(dve):
                for s in (s_z, s_v, s_kvm, s_vo, s_vy):
                    dve.sem_inc(s, 1)
                dve.sem_inc(s_rchain, 1)
                dve.sem_inc(s_placed, 1)
                nc.vector.memset(zero[:, :], 0.0).then_inc(s_zero, 1)
                nc.vector.memset(every[:, :], 1.0)
                nc.vector.memset(routing.offset[:, 0:LAG], 0)
                nc.vector.memset(chosen[:, :, :], 0.0)
                statistics(dve, 0)
                dve.wait_ge(s_const, 160)
                nc.vector.tensor_copy(before[:, :], before_f[:, :]).then_inc(s_set, 1)
                dve.wait_ge(s_set, 1)
                ffn_flags(dve, 0)
                statistics(dve, 1)
                ffn_shift(dve, 0)
                ffn_add(dve, 0)
                z_statistics(dve, 0)
                neurons(dve, 0, ahead=1, statistics_of=2)
                with dve.Fori(1, NP2 - 2) as i:
                    neurons(dve, i, ahead=i + 1, statistics_of=i + 2, route=i - 1)
                neurons(dve, NP2 - 2, ahead=NP2 - 1, route=NP2 - 3)
                neurons(dve, NP2 - 1, route=NP2 - 2)
                v = NP2 - 1
                route_stats(dve, v)
                route_scale(dve, v)
                route_choose(dve, v)
                route_place(dve, v)

            @block.gpsimd
            def _(pool):
                def route_deviation(v):
                    pool.wait_ge(s_rvar, v + 1)
                    inverse_deviation(nc, r_tmp, minus_half).then_inc(s_rrstd, 1)

                for s in (s_spk, s_so):
                    pool.sem_inc(s, 1)
                deviation(pool, 0)
                deviation(pool, 1)
                deviation_2(pool, 0)
                fire(pool, 0, ahead=1)
                deviation(pool, 2)
                with pool.Fori(1, NP2 - 2) as i:
                    route_deviation(i - 1)
                    fire(pool, i, ahead=i + 1)
                    deviation(pool, i + 2)
                route_deviation(NP2 - 3)
                fire(pool, NP2 - 2, ahead=NP2 - 1)
                route_deviation(NP2 - 2)
                fire(pool, NP2 - 1)
                route_deviation(NP2 - 1)
                pool.wait_ge(s_clear, 16 * NP2)
                routing.scatter(nc, pool, slots, 0, 0, 0)

            @block.scalar
            def _(act):
                act.sem_inc(s_zT, 1)

                def major(i):
                    for g in range(4):
                        act.wait_ge(s_tr, i * 4 + g + 1 + 1)
                        nc.scalar.activation(zT[:, g * G:(g + 1) * G, :].rearrange("p q k -> p (q k)"),
                                             ps_q[:, g // 2, g % 2, :], ACT.Copy).then_inc(s_zT, 1)

                ffn_rows(act, 0)
                z_rows(act, 0)
                major(0)
                ffn_rows(act, 1)
                z_rows(act, 1)
                ffn_rows(act, 2)
                with act.Fori(1, NP2 - 2) as i:
                    major(i)
                    route_rows(act, i - 1)
                    route_major(act, i - 1)
                    z_rows(act, i + 1)
                    ffn_rows(act, i + 2)
                for i in range(NP2 - 2, NP2):
                    major(i)
                    route_rows(act, i - 1)
                    route_major(act, i - 1)
                    if i == NP2 - 2:
                        z_rows(act, i + 1)
                        for quarter in range(4):
                            for q in range(G):
                                routing.normalise(nc, act, x_sb, 0, quarter, q)
                route_rows(act, NP2 - 1)
                route_major(act, NP2 - 1)

            @block.tensor
            def _(pe):
                for s in (s_tr, s_qkv, s_kv, s_o, s_y):
                    pe.sem_inc(s, 1)
                pe.wait_ge(s_set, 1)
                turn(pe, 0)
                project(pe, 0)
                attend(pe, 0)
                with pe.Fori(1, NP2) as i:
                    turn(pe, i)
                    project(pe, i)
                    attend(pe, i, beside=i - 1)
                for g in range(4):
                    route_turn(pe, NP2 - 1, NP2 - 1, g)
                route_logits(pe, NP2 - 1)
                route_rank(pe, NP2 - 1)


def experts(nc, t, sb, pb, sem, x_sb, ident, minus_half, slots, routing, out):
    out_view = out.rearrange("b (v j ip) w c -> v j (ip w) b c", ip=2, j=2)
    x_window = x_sb[:, :, :].rearrange("p (b v j) c -> p v j b c", b=B, j=2)
    slots_view = slots.rearrange("(g q p) c -> p g q c", q=G, p=P)
    with ExitStack() as a:
        wp = sb("wp", [P, 2, E * EW], F32R, at=a)
        wh, wl = wp[:, 0], wp[:, 1]
        bp = routing.bias
        ones = sb("m_ones", [P, P], BF16, at=a)
        scratch = routing.raw
        cut = 2 * NT * C
        results = scratch[:, 0:cut].rearrange("p (n f) -> p n f", n=2)
        rows_in, rows_out = (scratch[:, cut + n * 2 * G * C:cut + (n + 1) * 2 * G * C].rearrange("p (k q c) -> p k q c", k=2, c=C)
                             for n in range(2))
        sil = sb("sil", [P, 2, DFF], at=a)
        act_rows = sb("act_rows", [P, 2, DFF], at=a)
        uTh = sb("uTh", [P, 2, G * P], F32R, at=a)
        uTl = sb("uTl", [P, 2, G * P], F32R, at=a)
        aTh = sb("aTh", [P, 2, DFF], F32R, at=a)
        aTl = sb("aTl", [P, 2, DFF], F32R, at=a)
        wt = sb("wt", [P, 2, NTILES], at=a)
        top, offset = routing.top, routing.offset
        ps_u = pb("ps_u", [P, 2, G * P], at=a)
        ps_h = pb("ps_h", [P, 2, 2 * DFF], at=a)
        ps_a = pb("ps_a", [P, 2, 512], at=a)
        ps_y = pb("ps_y3", [P, 2, 2, 2, C], at=a)
        s_wh = sem("f_weights_upper")
        s_wl = sem("f_weights_rest")
        s_chain = sem("f_chain")
        s_raw, s_cp, s_scq = routing.s_raw, routing.s_cp, routing.s_scq
        s_dif = sem("f_difference")
        s_exp = sem("f_exponential")
        s_in = [sem("slot_rows_0"), sem("slot_rows_1")]
        s_turn = sem("slot_transposed")
        s_uh = sem("slot_upper")
        s_ul = sem("slot_rest")
        s_h = sem("slot_hidden")
        s_sil = sem("slot_silu")
        s_act = sem("slot_gated")
        s_at = sem("slot_gated_transposed")
        s_ah = sem("slot_gated_upper")
        s_al = sem("slot_gated_rest")
        s_ey = sem("slot_expert_out")
        s_yf = sem("slot_out_first_addend")
        s_yc = sem("slot_out_added")
        s_ys = [sem("slot_out_stored_0"), sem("slot_out_stored_1")]
        s_g = [sem("gathering_0"), sem("gathering_1")]
        s_one = sem("f_first_added")
        s_sum = sem("f_combined")
        s_out = sem("f_stored")

        STEPS = 2 * G
        TURNS = NP2 * SLOT_TILES // STEPS
        TW = SLOT_TILES // STEPS
        def need(eng, s, value):
            if not isinstance(value, int) or value > 0:
                eng.wait_ge(s, value)

        with nc.Block() as block:
            @block.sync
            def _(sp):
                def load_window(w):
                    sp.wait_ge(s_scq, (w + 1) * 4)

                    def load(n, j):
                        g = (w * TW + n) * 2 + j
                        need(sp, s_turn, g - 1)
                        src = slots_view[:, bass.ds(g, 1)] if not isinstance(g, int) else slots_view[:, g:g + 1]
                        sp.dma_start(rows_in[:, j:j + 1], src).then_inc(s_in[j], 16)

                    if w == 0:
                        load(0, 0)
                        load(0, 1)
                    with sp.Fori(1 if w == 0 else 0, TW) as n:
                        for j in range(2):
                            load(n, j)

                def store(w):
                    sp.wait_ge(s_sum, (w + 2) * NT)
                    for j in range(2):
                        sp.dma_start(out_view[w, j], x_window[:, w, j]).then_inc(s_out, 16)

                sp.wait_ge(s_wl, 1)
                for w in range(NP2):
                    if w >= 3:
                        store(w - 3)
                    load_window(w)
                for w in range(NP2 - 3, NP2):
                    store(w)
                sp.wait_ge(s_out, 2 * 16 * NP2)

            @block.gpsimd
            def _(pool):

                def gather(w, turn):
                    for j in range(2):
                        pool.wait_ge(s_ys[j], w * (TW * 16) + TW * 16)
                    routing.transfers(
                              nc, pool, w, turn, s_g,
                              lambda n, tile, at: nc.gpsimd.indirect_dma_start(
                                  results[:, n, tile * C:(tile + 1) * C], None,
                                  slots, bass.IndirectOffsetOnAxis(at, 0)),
                              lambda quarter: pool.wait_ge(s_sum, w * NT + quarter * 4 + 4),
                              lambda: None)

                routing.scatter(nc, pool, slots, 1, 1, 1)
                with pool.Fori(0, NP2 // 2 - 1) as m:
                    for k in range(2):
                        w = m * 2 + k
                        routing.scatter(nc, pool, slots, w + 2, k, w * 2 + 2)
                        gather(w, w * 2 + 3)
                for w in range(NP2 - 2, NP2):
                    gather(w, NP2 + w)

            @block.vector
            def _(dve):
                nc.vector.memset(ones[:, :], 1.0)
                dve.sem_inc(s_sum, NT)
                chain = Chain(dve, s_chain)
                dve.wait_ge(s_wh, 1)
                nc.vector.tensor_tensor(wl, scratch[:, :], wh.bitcast(F32), ALU.subtract).then_inc(s_wl, 1)
                nc.vector.tensor_tensor(wt[:, 0, :], top[:, 1, :], top[:, 0, :], ALU.subtract).then_inc(s_dif, 1)
                dve.wait_ge(s_exp, 1)
                chain.link(nc.vector.tensor_scalar(wt[:, 0, :], wt[:, 1, :], 1.0, None, ALU.add))
                chain.link(nc.vector.reciprocal(wt[:, 0, :], wt[:, 0, :]))
                chain.link(nc.vector.tensor_tensor(wt[:, 1, :], wt[:, 1, :], wt[:, 0, :], ALU.mult))

                def rest(g, j):
                    dve.wait_ge(s_uh, g + 1)
                    nc.vector.tensor_tensor(uTl[:, j], ps_u[:, j], uTh[:, j].bitcast(F32), ALU.subtract).then_inc(s_ul, 1)

                def gated(n, k):
                    dve.wait_ge(s_sil, n + 1)
                    need(dve, s_at, n - 1)
                    nc.vector.tensor_tensor(act_rows[:, k], ps_h[:, k, DFF:], sil[:, k], ALU.mult).then_inc(s_act, 1)

                def gated_rest(n, k):
                    dve.wait_ge(s_ah, n + 1)
                    nc.vector.tensor_tensor(aTl[:, k], ps_a[:, k, 0:DFF], aTh[:, k].bitcast(F32), ALU.subtract).then_inc(s_al, 1)

                def add_out(i, r):
                    pair, half, slot = i * 4 + r, r % 2, (r // 2) % 2
                    dve.wait_ge(s_yf, pair + 1)
                    dst = rows_out[:, slot, 2 * half:2 * half + 2, :]
                    nc.vector.tensor_tensor(dst, ps_y[:, half, :, 1, :], dst, ALU.add).then_inc(s_yc, 1)

                def turn(i, last=False, beside=lambda m: None):
                    head = isinstance(i, int) and i == 0
                    for m in range(STEPS):
                        n = i * STEPS + m
                        if m >= 2 or not head:
                            gated_rest(n - 2, m % 2)
                        gated(n, m % 2)
                        if m == 2:
                            rest(i * 2 + 1, 1)
                        if m == 6 and not last:
                            rest(i * 2 + 2, 0)
                        if m % 2 and (m >= 5 or not head):
                            add_out(i, (m - 5) // 2)
                        beside(m)

                def combine(w, h, k):
                    quarter = h * 2 + k

                    def part(m):
                        tile, n, q = quarter * 4 + m // 2, m % 2, m // 2
                        if m == 0:
                            dve.wait_ge(s_g[k], (w * 2 + h + 1) * QUARTER)
                        if n == 1:
                            dve.wait_ge(s_one, (w * 4 + quarter) * 4 + q + 1)
                        row = x_sb[:, bass.ds(quarter * 2 * HP + w * 2 + (q // 2) * HP + q % 2, 1), :].rearrange("p q c -> p (q c)")
                        ins = nc.vector.scalar_tensor_tensor(
                            row, results[:, n, bass.ds(tile * C, C)],
                            wt[:, n, bass.ds(w * NT + tile, 1)], row, ALU.mult, ALU.add)
                        ins.then_inc(s_sum if n else s_one, 1)
                    return part

                def window(w, start=2, last=False):
                    for n in range(TW):
                        if n >= 2:
                            beside = combine(w - 1, (n - 2) // 2, (n - 2) % 2)
                        elif n == 0 and start >= 2:
                            beside = combine(w - 2, 1, 1)
                        else:
                            beside = lambda m: None
                        turn(w * TW + n, last=last and n == TW - 1, beside=beside)

                rest(0, 0)
                turn(0)
                with dve.Fori(1, TW) as i:
                    turn(i)
                window(1, start=1)
                with dve.Fori(2, NP2 - 1) as w:
                    window(w)
                w = NP2 - 1
                window(w, last=True)
                for k in range(2):
                    gated_rest(NP2 * SLOT_TILES - 2 + k, k)
                for r in (-2, -1):
                    add_out(TURNS, r)
                for v, h, k in ((w - 1, 1, 1), (w, 0, 0), (w, 0, 1), (w, 1, 0), (w, 1, 1)):
                    part = combine(v, h, k)
                    for m in range(STEPS):
                        part(m)

            @block.scalar
            def _(act):
                def normalise(w, quarter, q):
                    if q == 0:
                        need(act, s_scq, w * 4 - 4 if not isinstance(w, int) or w >= 2 else 0)
                    routing.normalise(nc, act, x_sb, w, quarter, q)

                def normalise_window(w):
                    with act.Fori(0, 4) as quarter:
                        for q in range(G):
                            normalise(w, quarter, q)

                act.wait_ge(s_raw, 48)
                nc.scalar.activation(wh, scratch[:, :], ACT.Copy).then_inc(s_wh, 1)
                normalise_window(1)
                act.wait_ge(s_dif, 1)
                nc.scalar.activation(wt[:, 1, :], wt[:, 0, :], ACT.Exp).then_inc(s_exp, 1)
                normalise_window(2)

                def upper(g, j):
                    act.wait_ge(s_turn, g + 1)
                    need(act, s_h, g * G - G)
                    nc.scalar.activation(uTh[:, j], ps_u[:, j], ACT.Copy).then_inc(s_uh, 1)

                def silu(n, k):
                    act.wait_ge(s_h, n + 1)
                    need(act, s_act, n - 1)
                    nc.scalar.activation(sil[:, k], ps_h[:, k, 0:DFF], ACT.Silu).then_inc(s_sil, 1)

                def gated_upper(n, k):
                    act.wait_ge(s_at, n + 1)
                    need(act, s_ey, n - 1)
                    nc.scalar.activation(aTh[:, k], ps_a[:, k, 0:DFF], ACT.Copy).then_inc(s_ah, 1)

                def copy_out(i, r):
                    pair, half, slot = i * 4 + r, r % 2, (r // 2) % 2
                    act.wait_ge(s_ey, pair * 2 + 2)
                    if half == 0:
                        need(act, s_ys[slot], (i - slot) * 16)
                    nc.scalar.activation(rows_out[:, slot, 2 * half:2 * half + 2, :], ps_y[:, half, :, 0, :], ACT.Copy)\
                        .then_inc(s_yf, 1)

                def store(g, j):
                    act.wait_ge(s_yc, g * 2 + 2)
                    dst = slots_view[:, bass.ds(g, 1)] if not isinstance(g, int) else slots_view[:, g:g + 1]
                    act.dma_start(dst, rows_out[:, j:j + 1]).then_inc(s_ys[j], 16)

                def turn(i, last=False, beside=lambda m: None):
                    head = isinstance(i, int) and i == 0
                    for m in range(STEPS):
                        n = i * STEPS + m
                        if m >= 2 or not head:
                            gated_upper(n - 2, m % 2)
                        silu(n, m % 2)
                        if m == 2:
                            upper(i * 2 + 1, 1)
                        if m == 6 and not last:
                            upper(i * 2 + 2, 0)
                        if m % 2 and (m >= 5 or not head):
                            copy_out(i, (m - 5) // 2)
                        if m == 5 and not head:
                            store(i * 2 - 1, 1)
                        if m == 1 and not head:
                            store(i * 2 - 2, 0)
                        beside(m)

                upper(0, 0)
                turn(0)

                def quarters(w):
                    with act.Fori(0, 4) as quarter:
                        turn(w * TW + quarter + 1,
                             beside=lambda m: normalise(w + 3, quarter, m // 2) if m % 2 == 0 else None)

                quarters(0)
                with act.Fori(1, NP2 - 3) as w:
                    turn(w * TW)
                    quarters(w)
                with act.Fori((NP2 - 3) * TW, TURNS - 1) as i:
                    turn(i)
                turn(TURNS - 1, last=True)
                n = NP2 * SLOT_TILES
                store(n // G - 2, 0)
                for k in range(2):
                    gated_upper(n - 2 + k, k)
                for r in (-2, -1):
                    copy_out(TURNS, r)
                store(n // G - 1, 1)

            @block.tensor
            def _(pe):
                def transposes(g, j, i):
                    pe.wait_ge(s_in[j], i * 16 + 16)
                    need(pe, s_ul, g - 1)
                    for q in range(G):
                        ins = nc.tensor.transpose(ps_u[:, j, q * P:(q + 1) * P], rows_in[:, j, q, :], ident[:, :])
                    ins.then_inc(s_turn, 1)

                def load_offsets(i, count):
                    at = slice(0, count) if isinstance(i, int) and i == 0 else bass.ds(i * STEPS, count)
                    where = [pe.alloc_register(f"weights_at_{i if isinstance(i, int) else "turn"}_{k}") for k in range(count)]
                    pe.load(where, offset[0:1, at])
                    return [pe.snap(r, donate=True, min_val=0, max_val=(E - 1) * EW) for r in where]

                def hidden(i, m, o):
                    n, j, q, k = i * STEPS + m, m // G, m % G, m % 2
                    if q == 0:
                        pe.wait_ge(s_ul, i * 2 + j + 1)
                    dst = ps_h[:, k]
                    hi, lo = uTh[:, j, q * P:(q + 1) * P], uTl[:, j, q * P:(q + 1) * P]
                    at = bass.ds(o, 2 * DFF)
                    nc.tensor.matmul(dst, hi, wh[:, at], start=True, stop=False)
                    nc.tensor.matmul(dst, hi, wl[:, at], start=False, stop=False)
                    nc.tensor.matmul(dst, lo, wh[:, at], start=False, stop=False)
                    nc.tensor.matmul(dst, ones[0:3, :], bp[:, at], start=False, stop=True).then_inc(s_h, 1)

                def turn_gated(n, k):
                    for h in range(2):
                        ins = nc.tensor.transpose(ps_a[:, k, h * P:(h + 1) * P], act_rows[:, k, h * P:(h + 1) * P], ident[:, :])
                    ins.then_inc(s_at, 1)

                def expert_out(pair, m, o):
                    half, q, k = (m // 2) % 2, m % 2, m % 2
                    if q == 0:
                        need(pe, s_yc, pair - 1)
                    both, first = ps_y[:, half, q].rearrange("p a c -> p (a c)"), ps_y[:, half, q, 0]
                    for h in range(2):
                        hi, lo = aTh[:, k, h * P:(h + 1) * P], aTl[:, k, h * P:(h + 1) * P]
                        at = bass.ds(o + 2 * DFF + h * C, C)
                        nc.tensor.matmul(both, hi, wp[:, :, at], start=(h == 0), stop=False)
                        ins = nc.tensor.matmul(first, lo, wp[:, 0, at], start=False, stop=(h == 1))
                        if h == 0:
                            nc.tensor.matmul(first, ones[0:3, :], bp[:, bass.ds(o + 2 * DFF, C)], start=False, stop=False)
                    ins.then_inc(s_ey, 1)

                def turn(i, head=False, last=False):
                    at = load_offsets(i, LAG + STEPS)
                    for m in range(STEPS):
                        n = i * STEPS + m
                        if head and m == 2:
                            pe.wait_ge(s_act, 1)
                        elif m >= 3 or not head:
                            pe.wait_ge(s_al, n - 2)
                        if m >= 2 or not head:
                            turn_gated(n - 2, m % 2)
                        hidden(i, m, at[LAG + m])
                        if m == 1:
                            transposes(i * 2 + 1, 1, i)
                        if m == 5 and not last:
                            transposes(i * 2 + 2, 0, i + 1)
                        if m >= 3 or not head:
                            expert_out(i * 4 + (m - 3) // 2, (m - 3) % STEPS, at[m])

                pe.wait_ge(s_wl, 1)
                pe.wait_ge(routing.s_bias, 15 * 16)
                transposes(0, 0, 0)
                turn(0, head=True)
                with pe.Fori(1, TURNS - 1) as i:
                    turn(i)
                turn(TURNS - 1, last=True)
                at = load_offsets(TURNS, LAG)
                for m in range(3):
                    n = TURNS * STEPS + m
                    pe.wait_ge(s_al, n - 2)
                    if m < 2:
                        pe.wait_ge(s_act, n - 1)
                        turn_gated(n - 2, m % 2)
                    expert_out((n - 3) // 2, STEPS - 3 + m, at[m])


_CONSTANTS = spectral_tables()
_OUT = ((B, H, W, C), "float32")


def kernel(**inputs):
    import concourse.bacc as bacc
    from concourse.bass_utils import run_bass_kernel_spmd

    nc = bacc.Bacc("TRN2", target_bir_lowering=False, num_devices=1)
    arrays, tensors = {}, {}
    for name, a in {**inputs, **_CONSTANTS}.items():
        a = np.ascontiguousarray(a)
        arrays[f"in_{name}"] = a
        tensors[name] = nc.dram_tensor(f"in_{name}", a.shape, mybir.dt.from_np(a.dtype), kind="ExternalInput").ap()
    out = nc.dram_tensor("out_dram", _OUT[0], F32, kind="ExternalOutput").ap()
    build(nc, tensors, out)
    r = run_bass_kernel_spmd(nc, [arrays], core_ids=[0])
    return r.results[0]["out_dram"]
```
